# Optimizing a Trainium2 kernel written in Bass

```python
import numpy as np
import jax
import jax.numpy as jnp

def _softmax(x, axis=-1):
    return jax.nn.softmax(x, axis=axis)

def _gelu(x):
    return jax.nn.gelu(x, approximate=True)

def _silu(x):
    return jax.nn.silu(x)

def _sigmoid(x):
    return jax.nn.sigmoid(x)

def _layernorm(x, axis=-1, eps=1e-05):
    m = jnp.mean(x, axis=axis, keepdims=True)
    v = jnp.var(x, axis=axis, keepdims=True)
    return (x - m) / jnp.sqrt(v + eps)

def _scatter_add(tgt, idx, src, axis=0):
    return tgt.at[idx].add(src)

def _segment_sum(src, seg, n):
    return jax.ops.segment_sum(src, seg, n)
kernel_name = 'mk_conv_attn_hybrid_d2_conv_nhwc768_r2_c5be90'

def setup_inputs(seed: int=0):
    np.random.seed(seed)
    _w = jnp.asarray

    def _rec_inputs():
        import jax
        import jax.numpy as jnp
        _gk = jax.random.key(seed)
        x = -0.0004039 + 1 * jax.random.normal(jax.random.fold_in(_gk, 1), (4, 32, 32, 384), jnp.float32)
        return x
    x = _rec_inputs()

    def _L0_conv_setup():
        import jax, jax.numpy as jnp
        import numpy as np
        B_, H_, W_, DM = (4, 32, 32, 384)
        DI = int(0.5 * DM)
        N = 16
        R = -(-DM // 16)
        K = 4

        def selective_scan(xs, dts, As, Bs, Cs, Dsk):
            u = jnp.moveaxis(xs, -1, 0)
            d = jnp.moveaxis(dts, -1, 0)
            Bt = jnp.moveaxis(Bs, -1, 0)
            Ct = jnp.moveaxis(Cs, -1, 0)

            def step(h, inp):
                u_t, d_t, B_t, C_t = inp
                dA = jnp.exp(d_t[..., None] * As)
                h = h * dA + (d_t * u_t)[..., None] * B_t[:, :, None, :]
                y = jnp.einsum('bkcn,bkn->bkc', h, C_t)
                return (h, y)
            h0 = jnp.zeros(u.shape[1:] + (As.shape[-1],), u.dtype)
            _, ys = jax.lax.scan(step, h0, (u, d, Bt, Ct))
            ys = jnp.moveaxis(ys, 0, -1)
            return ys + Dsk[None, :, :, None] * xs
        key = jax.random.key(seed)
        ks = jax.random.split(key, 8)
        s = lambda i, shape, sc=0.02: jax.random.normal(ks[i], shape, jnp.float32) * sc
        return dict(x=jax.random.normal(ks[0], (B_, H_, W_, DM), jnp.float32), in_proj_w=s(1, (2 * DI, DM)), conv_w=s(2, (DI, 1, 3, 3)), conv_b=jnp.zeros((DI,), jnp.float32), x_proj_w=s(3, (K, R + 2 * N, DI)), dt_projs_w=s(4, (K, DI, R)), dt_projs_b=s(5, (K, DI)), A_logs=jnp.log(jnp.tile(jnp.arange(1, N + 1, dtype=jnp.float32)[None, :], (K * DI, 1))), Ds=jnp.ones((K * DI,), jnp.float32), out_norm_g=jnp.ones((DI,), jnp.float32), out_norm_b=jnp.zeros((DI,), jnp.float32), out_proj_w=s(6, (DM, DI)))
    _L0_conv_all = _L0_conv_setup()
    _L0_conv_in = {k: v for k, v in _L0_conv_all.items() if k in ('in_proj_w', 'conv_w', 'conv_b', 'x_proj_w', 'dt_projs_w', 'dt_projs_b', 'A_logs', 'Ds', 'out_norm_g', 'out_norm_b', 'out_proj_w')}
    del _L0_conv_all

    def _L1_attn_setup():
        import jax, jax.numpy as jnp
        import numpy as np
        NUM_HEADS = 12
        key = jax.random.key(seed)
        k1, k2, k3 = jax.random.split(key, 3)
        B, N, C = (2, 2048, 384)
        x = jax.random.normal(k1, (B, N, C), dtype=jnp.float32)
        w_qkv = jax.random.normal(k2, (C, 3 * C), dtype=jnp.float32) * 0.02
        b_qkv = jnp.zeros((3 * C,), dtype=jnp.float32)
        w_proj = jax.random.normal(k3, (C, C), dtype=jnp.float32) * 0.02
        b_proj = jnp.zeros((C,), dtype=jnp.float32)
        return {'x': x, 'w_qkv': w_qkv, 'b_qkv': b_qkv, 'w_proj': w_proj, 'b_proj': b_proj}
    _L1_attn_all = _L1_attn_setup()
    _L1_attn_in = {k: v for k, v in _L1_attn_all.items() if k in ('w_qkv', 'b_qkv', 'w_proj', 'b_proj')}
    del _L1_attn_all

    def _L1_ffn_setup():
        import jax, jax.numpy as jnp
        import numpy as np
        import math
        SQRT_2_OVER_PI = math.sqrt(2.0 / math.pi)

        def gelu(x):
            return x * 0.5 * (1.0 + jnp.tanh(SQRT_2_OVER_PI * (x + 0.044715 * x * x * x)))
        key = jax.random.key(seed)
        ks = jax.random.split(key, 6)
        B, S, D, M, E = (8, 256, 384, 1536, 8)
        return {'x': jax.random.normal(ks[0], (B, S, D), dtype=jnp.float32), 'router_w': jax.random.normal(ks[1], (D, E), dtype=jnp.float32) * (1.0 / np.sqrt(D)), 'w1': jax.random.normal(ks[2], (E, D, M), dtype=jnp.float32) * (1.0 / np.sqrt(D)), 'b1': jax.random.normal(ks[3], (E, M), dtype=jnp.float32) * 1e-06, 'w2': jax.random.normal(ks[4], (E, M, D), dtype=jnp.float32) * (1.0 / np.sqrt(M)), 'b2': jax.random.normal(ks[5], (E, D), dtype=jnp.float32) * 1e-06}
    _L1_ffn_all = _L1_ffn_setup()
    _L1_ffn_in = {k: v for k, v in _L1_ffn_all.items() if k in ('router_w', 'w1', 'b1', 'w2', 'b2')}
    del _L1_ffn_all
    return {'x': x, 'L0_conv_in_proj_w': _L0_conv_in['in_proj_w'], 'L0_conv_conv_w': _L0_conv_in['conv_w'], 'L0_conv_conv_b': _L0_conv_in['conv_b'], 'L0_conv_x_proj_w': _L0_conv_in['x_proj_w'], 'L0_conv_dt_projs_w': _L0_conv_in['dt_projs_w'], 'L0_conv_dt_projs_b': _L0_conv_in['dt_projs_b'], 'L0_conv_A_logs': _L0_conv_in['A_logs'], 'L0_conv_Ds': _L0_conv_in['Ds'], 'L0_conv_out_norm_g': _L0_conv_in['out_norm_g'], 'L0_conv_out_norm_b': _L0_conv_in['out_norm_b'], 'L0_conv_out_proj_w': _L0_conv_in['out_proj_w'], 'L1_attn_w_qkv': _L1_attn_in['w_qkv'], 'L1_attn_b_qkv': _L1_attn_in['b_qkv'], 'L1_attn_w_proj': _L1_attn_in['w_proj'], 'L1_attn_b_proj': _L1_attn_in['b_proj'], 'L1_ffn_router_w': _L1_ffn_in['router_w'], 'L1_ffn_w1': _L1_ffn_in['w1'], 'L1_ffn_b1': _L1_ffn_in['b1'], 'L1_ffn_w2': _L1_ffn_in['w2'], 'L1_ffn_b2': _L1_ffn_in['b2']}

def reference(x, L0_conv_in_proj_w, L0_conv_conv_w, L0_conv_conv_b, L0_conv_x_proj_w, L0_conv_dt_projs_w, L0_conv_dt_projs_b, L0_conv_A_logs, L0_conv_Ds, L0_conv_out_norm_g, L0_conv_out_norm_b, L0_conv_out_proj_w, L1_attn_w_qkv, L1_attn_b_qkv, L1_attn_w_proj, L1_attn_b_proj, L1_ffn_router_w, L1_ffn_w1, L1_ffn_b1, L1_ffn_w2, L1_ffn_b2):
    import jax
    import jax.numpy as jnp

    def _L0_conv_ref(x, in_proj_w, conv_w, conv_b, x_proj_w, dt_projs_w, dt_projs_b, A_logs, Ds, out_norm_g, out_norm_b, out_proj_w):
        import jax, jax.numpy as jnp
        import numpy as np
        B_, H_, W_, DM = (4, 32, 32, 384)
        DI = int(0.5 * DM)
        N = 16
        R = -(-DM // 16)
        K = 4

        def selective_scan(xs, dts, As, Bs, Cs, Dsk):
            u = jnp.moveaxis(xs, -1, 0)
            d = jnp.moveaxis(dts, -1, 0)
            Bt = jnp.moveaxis(Bs, -1, 0)
            Ct = jnp.moveaxis(Cs, -1, 0)

            def step(h, inp):
                u_t, d_t, B_t, C_t = inp
                dA = jnp.exp(d_t[..., None] * As)
                h = h * dA + (d_t * u_t)[..., None] * B_t[:, :, None, :]
                y = jnp.einsum('bkcn,bkn->bkc', h, C_t)
                return (h, y)
            h0 = jnp.zeros(u.shape[1:] + (As.shape[-1],), u.dtype)
            _, ys = jax.lax.scan(step, h0, (u, d, Bt, Ct))
            ys = jnp.moveaxis(ys, 0, -1)
            return ys + Dsk[None, :, :, None] * xs
        B, H, W, _ = x.shape
        L = H * W
        xz = x @ in_proj_w.T
        xh, z = jnp.split(xz, 2, axis=-1)
        xc = jnp.transpose(xh, (0, 3, 1, 2))
        xc = jax.lax.conv_general_dilated(xc, conv_w, (1, 1), 'SAME', feature_group_count=DI)
        xc = jax.nn.silu(xc + conv_b[None, :, None, None])
        x_flat = xc.reshape(B, DI, L)
        x_t = jnp.transpose(xc, (0, 1, 3, 2)).reshape(B, DI, L)
        x_hwwh = jnp.stack([x_flat, x_t], 1)
        xs = jnp.concatenate([x_hwwh, jnp.flip(x_hwwh, -1)], 1)
        x_dbl = jnp.einsum('bkdl,kcd->bkcl', xs, x_proj_w)
        dts, Bs, Cs = jnp.split(x_dbl, [R, R + N], axis=2)
        dts = jnp.einsum('bkrl,kdr->bkdl', dts, dt_projs_w)
        dts = jax.nn.softplus(dts + dt_projs_b[None, :, :, None])
        As = -jnp.exp(A_logs).reshape(K, DI, N)
        out_y = selective_scan(xs, dts, As, Bs, Cs, Ds.reshape(K, DI))
        inv_y = jnp.flip(out_y[:, 2:4], -1)
        wh_y = jnp.transpose(out_y[:, 1].reshape(B, DI, W, H), (0, 1, 3, 2)).reshape(B, DI, L)
        invwh_y = jnp.transpose(inv_y[:, 1].reshape(B, DI, W, H), (0, 1, 3, 2)).reshape(B, DI, L)
        y = out_y[:, 0] + inv_y[:, 0] + wh_y + invwh_y
        y = jnp.transpose(y, (0, 2, 1)).reshape(B, H, W, DI)
        mu = y.mean(-1, keepdims=True)
        var = y.var(-1, keepdims=True)
        y = (y - mu) / jnp.sqrt(var + 1e-05) * out_norm_g + out_norm_b
        y = y * jax.nn.silu(z)
        return y @ out_proj_w.T

    def _L1_attn_ref(x, w_qkv, b_qkv, w_proj, b_proj):
        import jax, jax.numpy as jnp
        import numpy as np
        NUM_HEADS = 12
        B, N, C = x.shape
        H = NUM_HEADS
        D = C // H
        qkv = (x @ w_qkv + b_qkv).reshape(B, N, 3, H, D).transpose(2, 0, 3, 1, 4)
        q, k, v = (qkv[0], qkv[1], qkv[2])
        attn = jnp.einsum('bhnd,bhmd->bhnm', q, k) / jnp.sqrt(jnp.float32(D))
        out = jnp.einsum('bhnm,bhmd->bhnd', attn, v)
        out = out.transpose(0, 2, 1, 3).reshape(B, N, C)
        return out @ w_proj + b_proj

    def _L1_ffn_ref(x, router_w, w1, b1, w2, b2):
        import jax, jax.numpy as jnp
        import numpy as np
        import math
        SQRT_2_OVER_PI = math.sqrt(2.0 / math.pi)

        def gelu(x):
            return x * 0.5 * (1.0 + jnp.tanh(SQRT_2_OVER_PI * (x + 0.044715 * x * x * x)))
        B, S, D = x.shape
        E = router_w.shape[1]
        T = B * S
        C = T // E
        xf = x.reshape(T, D)
        router_logits = xf @ router_w
        router_probs = jax.nn.softmax(router_logits, axis=-1)
        expert_gate = jnp.max(router_probs, axis=-1)
        expert_index = jnp.argmax(router_probs, axis=-1)
        expert_mask = jax.nn.one_hot(expert_index, E, dtype=xf.dtype)
        position_in_expert = (jnp.cumsum(expert_mask, axis=0) * expert_mask).astype(jnp.int32)
        expert_mask = expert_mask * (position_in_expert < C).astype(xf.dtype)
        expert_mask_flat = jnp.sum(expert_mask, axis=-1)
        expert_gate = expert_gate * expert_mask_flat
        combine = (expert_gate * expert_mask_flat)[:, None, None] * jax.nn.one_hot(expert_index, E, dtype=xf.dtype)[:, :, None] * jax.nn.one_hot(position_in_expert, C, dtype=xf.dtype)
        dispatch = (combine != 0).astype(xf.dtype)
        expert_inputs = jnp.einsum('td,tec->ecd', xf, dispatch)
        h = gelu(jnp.einsum('ecd,edm->ecm', expert_inputs, w1) + b1[:, None, :])
        expert_outputs = gelu(jnp.einsum('ecm,emd->ecd', h, w2) + b2[:, None, :])
        out = jnp.einsum('ecd,tec->td', expert_outputs, combine)
        return out.reshape(B, S, D)

    def _gn(v, G=32, eps=1e-05):
        B_, H_, W_, C_ = v.shape
        g = v.reshape(B_, H_, W_, G, C_ // G)
        m = jnp.mean(g, axis=(1, 2, 4), keepdims=True)
        s = jnp.var(g, axis=(1, 2, 4), keepdims=True)
        return ((g - m) / jnp.sqrt(s + eps)).reshape(v.shape)

    def _ln_c(v, eps=1e-06):
        m = jnp.mean(v, axis=-1, keepdims=True)
        s = jnp.var(v, axis=-1, keepdims=True)
        return (v - m) / jnp.sqrt(s + eps)

    def _ln_t(v, eps=1e-05):
        m = jnp.mean(v, axis=-1, keepdims=True)
        s = jnp.var(v, axis=-1, keepdims=True)
        return (v - m) / jnp.sqrt(s + eps)

    def _to_tokens(v):
        B_, H_, W_, C_ = v.shape
        return v.reshape(B_, H_ * W_, C_)

    def _from_tokens(t, like):
        return t.reshape(like.shape)
    x = x + _L0_conv_ref(_gn(x), L0_conv_in_proj_w, L0_conv_conv_w, L0_conv_conv_b, L0_conv_x_proj_w, L0_conv_dt_projs_w, L0_conv_dt_projs_b, L0_conv_A_logs, L0_conv_Ds, L0_conv_out_norm_g, L0_conv_out_norm_b, L0_conv_out_proj_w)
    t = _to_tokens(x)
    t = t + _L1_attn_ref(_ln_t(t), L1_attn_w_qkv, L1_attn_b_qkv, L1_attn_w_proj, L1_attn_b_proj)
    t = t + _L1_ffn_ref(_ln_t(t), L1_ffn_router_w, L1_ffn_w1, L1_ffn_b1, L1_ffn_w2, L1_ffn_b2)
    x = _from_tokens(t, x)
    return x

_drawn_inputs = setup_inputs


def setup_inputs(seed=0):
    import zlib

    import numpy as np

    out = dict(_drawn_inputs(seed))
    spreads = {'L0_conv_conv_b': (0.0, 0.1),
     'L0_conv_Ds': (1.0, 0.6),
     'L0_conv_out_norm_g': (1.0, 0.6),
     'L0_conv_out_norm_b': (0.0, 0.724),
     'L1_attn_b_qkv': (0.0, 0.1),
     'L1_attn_b_proj': (0.0, 0.1)}
    factors = {'L0_conv_conv_w': 3.257,
     'L0_conv_x_proj_w': 64.0,
     'L0_conv_dt_projs_w': 64.0,
     'L0_conv_dt_projs_b': 195.129,
     'L0_conv_A_logs': 64.0,
     'L1_ffn_b1': 200.0,
     'L1_ffn_b2': 200.0}
    for name, (base, spread) in spreads.items():
        noise = np.random.default_rng([zlib.crc32(name.encode()), seed]).standard_normal(out[name].shape)
        drawn = base * np.exp(spread * noise) if base else spread * noise
        out[name] = jnp.asarray(drawn.astype(out[name].dtype))
    for name, factor in factors.items():
        out[name] = (out[name] * factor).astype(out[name].dtype)
    return out
```

```python
from contextlib import ExitStack

import concourse.bass as bass
from concourse import mybir

ALU = mybir.AluOpType
ACT = mybir.ActivationFunctionType
AX = mybir.AxisListType
F32 = mybir.dt.float32
BF16 = mybir.dt.bfloat16
U32 = mybir.dt.uint32

B, HW, C, DI, N, R, K = 4, 32, 384, 192, 16, 24, 4
S = HW * HW
T = B * S
P = 128
CT = C // P
H2 = P // 2
J = DI // H2
NP = B // 2
NQ = NP * 2 * J
OJ = 2 * J
PART = 3
BR = 2 * PART * N
DR = 2 * R
XR = 2 * BR + DR
UN = 2 * N
HALF = S // 2
POOL_AT = (5, 7, 9, 11)
ACT_AT = (3, 4, 5, 6, 7)
RING = 4
LAG = 3
PADW = HW + 2
NT = T // P
TB = S // P
NH = 12
HD = C // NH
E, M = 8, 1536
MT = M // P
CAP = T // E
CPT = CAP // P
GRP = 32
A_LOG_MAX = 84.0
DROPPED = 100000.0


class Count:

    def __init__(self, eng, sem):
        self.eng, self.sem, self.base, self.n, self.loop, self.per = eng, sem, 0, 0, None, 0

    def enter(self, i, per):
        self.base, self.n, self.loop, self.per = self.base + self.n, 0, i, per

    def leave(self, trips):
        assert self.n == self.per, (self.n, self.per)
        self.base, self.n, self.loop = self.base + self.per * trips, 0, None

    def step(self, ins):
        ins.then_inc(self.sem, 1)
        self.n += 1
        v = self.base + self.n
        return v if self.loop is None else self.loop * self.per + v

    def link(self, ins):
        self.eng.wait_ge(self.sem, self.step(ins))


class Region:

    def __init__(self, arena, start, end):
        self.arena, self.at, self.end = arena, start, end

    def take(self, *dims, dtype=F32, rows=P):
        n = 1
        for d in dims:
            n *= d
        cols = n // 2 if dtype == BF16 else n
        assert self.at + cols <= self.end, (self.at, cols, self.end)
        v = self.arena[0:rows, self.at:self.at + cols]
        self.at += cols
        if dtype != F32:
            v = v.bitcast(dtype)
        if len(dims) > 1:
            names = [f"d{i}" for i in range(len(dims))]
            v = v.rearrange(f"p ({' '.join(names)}) -> p {' '.join(names)}", **dict(zip(names[1:], dims[1:])))
        return v


def hybrid_block_kernel(nc, a, out):
    with ExitStack() as ctx:
        def sem(name):
            return ctx.enter_context(nc.semaphore(name))

        z_dram = nc.dram_tensor("z_scratch", (NP, P, J, S), F32, kind="Internal").ap()
        slot_in = nc.dram_tensor("slot_in", (E * CAP, C), F32, kind="Internal").ap()
        slot_out = nc.dram_tensor("slot_out", (E * CAP, C), F32, kind="Internal").ap()

        COLS = 53100
        arena = ctx.enter_context(nc.sbuf_tensor("arena", [P, COLS], F32))
        ALWAYS = 3500
        XY = ALWAYS + NQ * S
        BCD = XY + 16 * S
        always = Region(arena, 0, ALWAYS)
        ident, ones = always.take(P), always.take(P)
        one_col, neg_col, eps_col = always.take(1), always.take(1), always.take(1)
        a_neg = always.take(OJ, 2, N)
        dt_bias = always.take(OJ, 2, 1)
        d_sum = always.take(OJ, 1)
        d_two = always.take(2, OJ)
        mask1, mask2 = always.take(1), always.take(1)
        conv_b, norm_g, norm_b = always.take(J), always.take(J), always.take(J)
        b1_col, bq_col = always.take(E, MT), always.take(CT)
        sel_lhs = always.take(N, P, dtype=BF16)
        dt_w = always.take(OJ, 2, P)
        xy = Region(arena, ALWAYS, XY).take(NQ, S)

        rb = Region(arena, XY, BCD)
        bc = rb.take(2 * NP, 2, 2, S, dtype=BF16)
        dts = rb.take(2 * NP, 2, S)

        ra = Region(arena, XY, BCD)
        xt = ra.take(2, CT, S)
        w_in, conv_w = ra.take(CT, 2, J, P), ra.take(J, 9)
        gn_sel, gn_back = ra.take(CT, GRP), ra.take(CT, P)
        bst, mv, chan = ra.take(2, CT, 2, 6), ra.take(2, CT, 2), ra.take(2, CT, 2)
        gst, gaff, caff = ra.take(2, 4), ra.take(2, 2), ra.take(2, CT, 2)
        rw = Region(arena, BCD, COLS - CPT * C)
        z_sb, xpad, conv_diag = rw.take(J, S), rw.take(J, PADW, PADW), rw.take(J, 9, P)
        xproj_w = rw.take(K, J, XR)
        split_hi, split_mid = rw.take(2, S, dtype=BF16), rw.take(2, S, dtype=BF16)
        split_rest = rw.take(2, S)
        zeros = Region(arena, COLS - CPT * C, COLS).take(CPT * C)

        rs = Region(arena, BCD, COLS - CPT * C)
        t_abs, t_w = rs.take(S), rs.take(S)
        dlt, dux, decay = rs.take(2, S), rs.take(2, S), rs.take(RING, S)
        hst, c_sb = rs.take(RING, S), rs.take(RING, S)
        wdt_cur, d_diag = rs.take(2, P), rs.take(P)

        tok = Region(arena, XY, BCD).take(NT, C)
        R4 = XY + NT * C
        r4 = Region(arena, R4, COLS - CPT * C)
        w_out, mean_w = r4.take(J, C), r4.take(P)
        z4, yt, ysq, yg, rst4 = r4.take(J, HALF), r4.take(J, HALF), r4.take(J, HALF), r4.take(J, HALF), r4.take(HALF)

        x2 = Region(arena, ALWAYS, XY).take(NT, C)
        r5 = Region(arena, R4 + CT * M, COLS)
        w_kv, w_qT, w_p = r5.take(CT, 2 * C), r5.take(CT, C), r5.take(CT, C)
        bkv, head_mask, rt_w = r5.take(2, C), r5.take(C), r5.take(CT, E)
        xn5, xnT, kv, x2T = r5.take(2, C), r5.take(CT, S), r5.take(2, 2, C), r5.take(2, CT, P)
        x2_cur = r5.take(2, C)
        bd, m_sb, w_eff = r5.take(CT, P), r5.take(CT, C), r5.take(CT, C)
        brow, bproj = r5.take(C), r5.take(C)
        bst5, mv5, rstd5 = r5.take(2, 6), r5.take(2, 2), r5.take(2, 1)
        logit, hot, cpos, tot, run, rank8 = (r5.take(NT, E) for _ in range(6))
        tri = r5.take(P)
        mx, esum, best, pos, keep = (r5.take(NT) for _ in range(5))
        rg = Region(arena, ALWAYS - 200, ALWAYS)
        assert always.at <= ALWAYS - 200
        gate, slot_s, slot_g = rg.take(NT), rg.take(NT, dtype=U32), rg.take(NT, dtype=U32)

        w1 = [Region(arena, R4, R4 + CT * M).take(CT, M), None]
        r6y = Region(arena, ALWAYS, XY)
        w1[1] = r6y.take(CT, M)
        w2 = [None, r6y.take(MT, C)]
        b2_bc = r6y.take(E, C)
        r6 = Region(arena, R4 + CT * M, COLS)
        w2[0] = r6.take(MT, C)
        xe, xeT, h_sb = r6.take(CPT, C), r6.take(CT, CAP), r6.take(MT, CAP)
        y_pre, yo = r6.take(2, C), r6.take(CPT, C)
        got = Region(arena, ALWAYS, XY).take(NT, C)

        ps = ctx.enter_context(nc.psum_tensor("ps", [P, 8, 512], F32))

        def pair_of_banks(b):
            return ps[:, b:b + 2, :].rearrange("p b c -> p (b c)")

        SLOT3 = [pair_of_banks(b) for b in (0, 2, 4)]
        B_PS = [pair_of_banks(0), pair_of_banks(2)]
        C_PS, Y_PS = pair_of_banks(4), pair_of_banks(6)

        ld_c, ld_x, z_st = sem("ld_consts"), [sem("ld_x0"), sem("ld_x1")], [sem("z_stored0"), sem("z_stored1")]
        pool_set, dve_c, act_c = sem("pool_set"), sem("dve_chain"), sem("act_chain")
        a_cut, a_exp, setup = sem("a_clamped"), sem("a_exp"), sem("dve_setup")
        chan_ok, grp_ok, gaff_ok, caff_ok, xn_ok = (sem(n) for n in ("channel_stats", "group_sums", "group_affine", "channel_affine", "xn_ready"))
        ip_ok, ev_free, xh_ok, xT_ok = sem("slot_filled"), sem("slot_free"), sem("xh_padded"), sem("x_by_columns")
        xp_ok, hi_ok, mid_ok, split_ok, dts_free = (sem(n) for n in ("xproj_filled", "split_hi", "split_mid", "split_steps", "dt_rows_copied"))
        wdt_ok, dt_ok, dtev_ok, lost_ok, ln_ok = (sem(n) for n in ("dt_weights", "dt_filled", "dt_evacuated", "lost_part", "ln_ready"))
        d_ok, du_ok, pd_ok = sem("delta_ready"), sem("delta_x_ready"), sem("pool_delta")
        b_ok, c_ok, c_free, dec_ok, dd_ok = (sem(n) for n in ("b_spread", "c_spread", "c_copied", "decay_ready", "d_diag_ready"))
        p1_ok, sc_ok, p2_ok, ya_ok, yev_ok = (sem(n) for n in ("input_ready", "scanned", "readout_ready", "y_added", "y_evacuated"))
        ld4, ld_t, ld_z, yt_ok, mean_ok, yc_ok, sq_ok, var_ok, yn_ok, af_ok, yg_ok, op_ok, ta_ok = (sem(n) for n in (
            "ld_w4", "ld_tokens", "ld_z", "yt_ready", "mean_filled", "centred", "squared", "var_filled", "normed",
            "affine_done", "gated", "outproj_filled", "tokens_added"))
        ld5, xn5_ok, tp_ok, tpc_ok, kv_ok, kvc_ok, vk_ok, bd_ok, m_ok, mc_ok, we_ok, wec_ok, bro_ok = (sem(n) for n in (
            "ld_w5", "tokens_normed", "turned", "turned_copied", "kv_filled", "kv_copied", "vk_added", "vk_masked",
            "m_filled", "m_copied", "weff_filled", "weff_copied", "bias_row"))
        at_ok, ta2_ok, x2_ok, t2_ok, t2c_ok, lg_ok, lgc_ok = (sem(n) for n in (
            "attn_filled", "attn_added", "x2_ready", "x2_turned", "x2_turned_copied", "logits_filled", "logits_copied"))
        x2s_ok = sem("x2_stored")
        passed = sem("passed")
        gvar_ok, gstd_ok, std_ok = sem("group_var"), sem("group_std"), sem("std_ready")
        tvar_ok, tstd_ok = sem("token_var"), sem("token_std")
        shift_ok, rexp_ok, hot_ok, cum_ok, idx_ok = (sem(n) for n in ("logits_shifted", "router_exp", "one_hot", "cumsum_filled", "slots_ready"))
        zero_st, scat, ld_w, ld_xe, ld_b2 = sem("zeros_stored"), sem("scattered"), [sem("ld_set0"), sem("ld_set1")], sem("ld_slots"), sem("ld_b2")
        xt_ok, xtc_ok, h_ok, hg_ok, o_ok, ob_ok, og_ok, yo_st = (sem(n) for n in (
            "slots_turned", "slots_turned_copied", "h_filled", "h_gelu", "o_filled", "o_biased", "o_gelu", "slots_stored"))
        gath, fin_ok, out_st = [sem(f"gathered{g}") for g in range(NT // 4)], sem("final_ready"), sem("out_stored")

        CONSTS = [
            (ident, "ident"), (ones, "ones"), (a_neg, "a_logs"), (dt_bias, "dt_bias"), (d_two, "ds"),
            (mask1, "mask1"), (mask2, "mask2"), (conv_b, "conv_b"), (norm_g, "norm_g"), (norm_b, "norm_b"),
            (b1_col, "b1"), (bq_col, "bq"), (sel_lhs, "sel"), (dt_w[0:DR], "dt_w"), (w_in, "w_in"),
            (conv_w, "conv_w"), (gn_sel, "gn_sel"), (gn_back[0:GRP], "gn_back"), (xproj_w, "xproj_w"),
        ]
        LD_C = 16 * len(CONSTS)
        block = ctx.enter_context(nc.Block())

        def settled(eng):
            eng.sem_inc(passed, 1)

        @block.sync
        def _(sp):
            for s in (*z_st, yo_st):
                sp.sem_inc(s, 1)
            for dst, name in CONSTS:
                sp.dma_start(dst, a[name]).then_inc(ld_c, 16)
            sp.wait_ge(pool_set, 5)
            for e in range(E):
                sp.dma_start(slot_in[e * CAP:(e + 1) * CAP].rearrange("(p i) c -> p (i c)", i=CPT), zeros).then_inc(zero_st, 16)
            with nc.sync.Fori(0, NP) as p:
                for r in range(2):
                    sp.wait_ge(ip_ok, 1 + p * 9)
                    sp.dma_start(xt[:, r], a["xT"][p * 2 + r]).then_inc(ld_x[r], 16)
                for r in range(2):
                    sp.wait_ge(ev_free, 3 + p * 9 + (3 * r + 3))
                    lo = H2 * (1 - r)
                    sp.dma_start(z_dram[p, H2 * r:H2 * r + H2], z_sb[lo:lo + H2]).then_inc(z_st[r], 16)
            sp.wait_ge(yev_ok, NQ)
            sp.wait_ge(du_ok, 2 * NQ)
            for r in range(2):
                sp.wait_ge(z_st[r], 1 + 16 * NP)
            sp.dma_start(w_out, a["w_out"]).then_inc(ld4, 16)
            sp.dma_start(mean_w, a["mean_w"]).then_inc(ld4, 16)
            sp.dma_start(tok, a["x_tok"]).then_inc(ld_t, 16)
            with nc.sync.Fori(0, 2 * NP) as c:
                sp.wait_ge(yg_ok, 1 + c * J)
                sp.dma_start(z4, z_dram[c // 2, :, :, bass.ts(c % 2, HALF)]).then_inc(ld_z, 16)
            sp.wait_ge(ta_ok, 4 + NT)
            sp.wait_ge(zero_st, 16 * E)
            for dst, name in ((w_kv, "w_kv"), (w_qT, "w_qT"), (w_p, "w_p"), (bkv, "b_kv"), (head_mask, "head_mask"),
                              (rt_w, "router_w"), (bproj[0:1], "b_proj"), (rank8, "rank"), (tri, "tri")):
                sp.dma_start(dst, a[name]).then_inc(ld5, 16)
            w1_v = a["w1"].rearrange("e (t p) m -> e p t m", p=P)
            w2_v = a["w2"].rearrange("e (t p) c -> e p t c", p=P)
            sp.dma_start(w1[0], w1_v[0]).then_inc(ld_w[0], 16)
            sp.wait_ge(idx_ok, 1)
            sp.dma_start(w2[0], w2_v[0]).then_inc(ld_w[0], 16)
            sp.wait_ge(scat, 16 * NT)
            slot_in_v = slot_in.rearrange("(e i p) c -> e p i c", i=CPT, p=P)
            slot_out_v = slot_out.rearrange("(e i p) c -> e p i c", i=CPT, p=P)
            sp.dma_start(xe, slot_in_v[0]).then_inc(ld_xe, 16)
            sp.dma_start(b2_bc, a["b2"].rearrange("e c -> (e c)").partition_broadcast(P)).then_inc(ld_b2, 16)
            sp.dma_start(w1[1], w1_v[1]).then_inc(ld_w[1], 16)
            sp.dma_start(w2[1], w2_v[1]).then_inc(ld_w[1], 16)

            def slots_in(e):
                sp.wait_ge(xt_ok, e * CT)
                sp.dma_start(xe, slot_in_v[e]).then_inc(ld_xe, 16)

            def slots_out(e):
                sp.wait_ge(og_ok, 1 + e * CPT + CPT)
                sp.dma_start(slot_out_v[e], yo).then_inc(yo_st, 16)

            with nc.sync.Fori(0, E // 2 - 1) as g:
                for s in range(2):
                    slots_in(g * 2 + (s + 1))
                    slots_out(g * 2 + s)
                    sp.dma_start(w1[s], w1_v[g * 2 + (s + 2)]).then_inc(ld_w[s], 16)
                    sp.dma_start(w2[s], w2_v[g * 2 + (s + 2)]).then_inc(ld_w[s], 16)
            slots_in(E - 1)
            slots_out(E - 2)
            slots_out(E - 1)
            out_v = out.rearrange("(i p) c -> p i c", p=P)
            for g in range(NT // 4):
                sp.wait_ge(fin_ok, 4 * g + 4)
                sp.dma_start(out_v[:, 4 * g:4 * g + 4], tok[:, 4 * g:4 * g + 4]).then_inc(out_st, 16)
            sp.wait_ge(out_st, 16 * (NT // 4))

        @block.gpsimd
        def _(pool):
            pool.memset(xpad, 0.0).then_inc(pool_set, 1)
            pool.memset(one_col, 1.0).then_inc(pool_set, 1)
            pool.memset(neg_col, -1.0).then_inc(pool_set, 1)
            pool.memset(eps_col, 1e-5).then_inc(pool_set, 1)
            pool.memset(zeros, 0.0).then_inc(pool_set, 1)
            pool.sem_inc(p2_ok, RING)
            pool.sem_inc(x2s_ok, 2)

            with nc.gpsimd.Fori(0, NP) as p:
                for j in range(J):
                    pool.wait_ge(ev_free, 3 + p * 9 + (6 + j + 1))
                    nc.gpsimd.tensor_copy(xy[:, p * OJ + (J + j), :].rearrange("p (w h) -> p w h", h=HW),
                                          xy[:, p * OJ + j, :].rearrange("p (h w) -> p w h", w=HW)).then_inc(xT_ok, 1)

            def delta(q, dr, step):
                jq = q * 2 + dr
                if step == 0:
                    pool.wait_ge(lost_ok, jq + 1)
                    nc.gpsimd.tensor_tensor(dux[:, dr], dux[:, dr], t_abs, ALU.subtract).then_inc(pd_ok, 1)
                elif step == 1:
                    pool.wait_ge(ln_ok, jq + 1)
                    nc.gpsimd.tensor_tensor(dlt[:, dr], dlt[:, dr], t_w, ALU.add).then_inc(pd_ok, 1)
                elif step == 2:
                    pool.wait_ge(pd_ok, jq * 2 + 2)
                    nc.gpsimd.tensor_tensor(dlt[:, dr], dlt[:, dr], dux[:, dr], ALU.add).then_inc(d_ok, 1)
                else:
                    pool.wait_ge(d_ok, jq + 1)
                    nc.gpsimd.tensor_tensor(dux[:, dr], dlt[:, dr], xy[:, q, :], ALU.mult).then_inc(du_ok, 1)

            def read_outs(q, last):
                for u in range(UN):
                    dr, n = divmod(u, N)
                    U = q * UN + u
                    pool.wait_ge(sc_ok, U + 3)
                    pool.wait_ge(c_free, U + 2)
                    nc.gpsimd.tensor_tensor(hst[:, u % RING], hst[:, u % RING], c_sb[:, u % RING], ALU.mult).then_inc(p2_ok, 1)
                    if n in POOL_AT and not (last and dr):
                        delta(q + dr, 1 - dr, POOL_AT.index(n))

            pool.wait_ge(xT_ok, NP * J)
            for s in range(4):
                delta(0, 0, s)
            with nc.gpsimd.Fori(0, NQ - 1) as q:
                read_outs(q, False)
            read_outs(NQ - 1, True)

            with nc.gpsimd.Fori(0, B) as b:
                for i in range(TB):
                    pool.wait_ge(x2_ok, b * TB + (i + 1))
                    nc.gpsimd.tensor_copy(x2[:, b * TB + i, :], x2_cur[:, i % 2]).then_inc(x2s_ok, 1)

            pool.wait_ge(idx_ok, 1)
            pool.wait_ge(zero_st, 16 * E)
            pool.wait_ge(x2s_ok, 2 + NT)
            for i in range(NT):
                pool.indirect_dma_start(out=slot_in, out_offset=bass.IndirectOffsetOnAxis(ap=slot_s[:, i:i + 1], axis=0),
                                        in_=x2[:, i, :], in_offset=None, bounds_check=E * CAP - 1,
                                        oob_is_err=False).then_inc(scat, 16)
            pool.wait_ge(yo_st, 1 + 16 * E)
            pool.wait_ge(o_ok, E * CPT + 2)
            pool.wait_ge(ob_ok, 1 + E * CPT)
            for i in range(NT):
                pool.indirect_dma_start(out=got[:, i, :], out_offset=None, in_=slot_out,
                                        in_offset=bass.IndirectOffsetOnAxis(ap=slot_g[:, i:i + 1], axis=0),
                                        bounds_check=E * CAP - 1, oob_is_err=False).then_inc(gath[i // 4], 16)

        @block.scalar
        def _(act):
            chain = Count(act, act_c)
            act.sem_inc(ev_free, 3)
            act.sem_inc(dts_free, 1)
            act.sem_inc(c_free, 1)
            act.sem_inc(tpc_ok, 2)
            for s in (t2c_ok, lgc_ok, og_ok):
                act.sem_inc(s, 1)
            act.wait_ge(ld_c, LD_C)
            act.wait_ge(a_cut, 1)
            nc.scalar.activation(a_neg, a_neg, ACT.Exp).then_inc(a_exp, 1)
            act.wait_ge(pool_set, 5)

            with nc.scalar.Fori(0, NP) as p:
                for r in range(2):
                    act.wait_ge(gvar_ok, p * 2 + (r + 1))
                    nc.scalar.activation(gaff[0:GRP, r, 0:1], gst[0:GRP, r, 3:4], ACT.Sqrt, bias=eps_col[0:GRP]).then_inc(gstd_ok, 1)
                    act.wait_ge(z_st[r], 1 + p * 16)
                    for j in range(J):
                        n = 3 * r + j
                        lo, zlo = H2 * r, H2 * (1 - r)
                        act.wait_ge(ip_ok, 1 + p * 9 + (n + 1))
                        nc.scalar.activation(xpad[lo:lo + H2, j, 1:1 + HW, 1:1 + HW],
                                             SLOT3[n % 3][lo:lo + H2].rearrange("p (h w) -> p h w", w=HW),
                                             ACT.Copy).then_inc(xh_ok, 1)
                        nc.scalar.activation(z_sb[zlo:zlo + H2, j], SLOT3[n % 3][zlo:zlo + H2], ACT.Silu).then_inc(ev_free, 1)
                for j in range(J):
                    act.wait_ge(ip_ok, 1 + p * 9 + (7 + j))
                    settled(act)
                    nc.scalar.activation(xy[:, p * OJ + j, :], SLOT3[j], ACT.Silu, bias=conv_b[:, j:j + 1]).then_inc(ev_free, 1)

            with nc.scalar.Fori(0, NP) as p:
                for k in range(K):
                    o, dr = k % 2, k // 2
                    for m in range(2):
                        act.wait_ge(xp_ok, p * (3 * K) + (3 * k + m + 1))
                        nc.scalar.activation(split_hi[0:BR, m], SLOT3[m][0:BR], ACT.Copy).then_inc(hi_ok, 1)
                    act.wait_ge(xp_ok, p * (3 * K) + (3 * k + 3))
                    settled(act)
                    nc.scalar.activation(dts[0:DR, p * 2 + o, dr, :], SLOT3[2][0:DR], ACT.Copy).then_inc(dts_free, 1)
                    for m in range(2):
                        act.wait_ge(split_ok, p * (4 * K) + (4 + 4 * k + m + 1))
                        nc.scalar.activation(split_mid[0:BR, m], split_rest[0:BR, m], ACT.Copy).then_inc(mid_ok, 1)

            def delta_weights(q, dr):
                nc.scalar.activation(wdt_cur[0:DR, dr], dt_w[0:DR, q % OJ, dr, :], ACT.Copy).then_inc(wdt_ok, 1)

            u_made = [None]

            def delta_parts(q, dr, step):
                jq = q * 2 + dr
                bias = dt_bias[:, q % OJ, dr, :]
                if step == 0:
                    act.wait_ge(dt_ok, jq + 1)
                    if not (isinstance(jq, int) and jq == 0):
                        act.wait_ge(d_ok, jq)
                    settled(act)
                    chain.link(nc.scalar.activation(t_abs, C_PS, ACT.Abs, bias=bias))
                    settled(act)
                    nc.scalar.activation(dlt[:, dr], C_PS, ACT.Relu, bias=bias).then_inc(dtev_ok, 1)
                elif step == 1:
                    u_made[0] = chain.step(nc.scalar.activation(dux[:, dr], t_abs, ACT.Exp, scale=-1.0))
                elif step == 2:
                    act.wait_ge(act_c, u_made[0])
                    u_made[0] = chain.step(nc.scalar.activation(t_w, dux[:, dr], ACT.Identity, bias=one_col))
                elif step == 3:
                    act.wait_ge(act_c, u_made[0])
                    nc.scalar.activation(t_abs, t_w, ACT.Identity, bias=neg_col).then_inc(lost_ok, 1)
                else:
                    act.wait_ge(lost_ok, jq + 1)
                    nc.scalar.activation(t_w, t_w, ACT.Ln).then_inc(ln_ok, 1)

            def units(q, first, last):
                for u in range(UN):
                    dr, n = divmod(u, N)
                    U = q * UN + u
                    if n == 0:
                        act.wait_ge(d_ok, q * 2 + (dr + 1))
                    if not (first and u < RING):
                        act.wait_ge(sc_ok, U + (3 - RING))
                        settled(act)
                    nc.scalar.activation(decay[:, u % RING], dlt[:, dr], ACT.Exp,
                                         scale=a_neg[:, q % OJ, dr, n:n + 1]).then_inc(dec_ok, 1)
                    if u == LAG and not first:
                        evacuate_y(q - 1)
                    act.wait_ge(c_ok, U + 1)
                    act.wait_ge(p2_ok, U + 1)
                    nc.scalar.activation(c_sb[:, u % RING], C_PS, ACT.Copy).then_inc(c_free, 1)
                    if not (last and dr):
                        nq, nd = q + dr, 1 - dr
                        if n == 1:
                            delta_weights(nq, nd)
                        if n in ACT_AT:
                            delta_parts(nq, nd, ACT_AT.index(n))

            def evacuate_y(q):
                act.wait_ge(ya_ok, q * UN + (UN + RING))
                act.wait_ge(du_ok, q * 2 + 2)
                settled(act)
                nc.scalar.activation(xy[:, q, :], Y_PS, ACT.Copy).then_inc(yev_ok, 1)

            act.wait_ge(split_ok, 4 + 4 * K * NP)
            act.wait_ge(xp_ok, 3 * K * NP)
            for r in range(2):
                act.wait_ge(z_st[r], 1 + 16 * NP)
            act.wait_ge(setup, 2)
            delta_weights(0, 0)
            for s in range(5):
                delta_parts(0, 0, s)
            units(0, True, False)
            PER = 6
            with nc.scalar.Fori(1, NQ - 1) as q:
                chain.enter(q - 1, PER)
                units(q, False, False)
            chain.leave(NQ - 2)
            units(NQ - 1, False, True)
            evacuate_y(NQ - 1)

            with nc.scalar.Fori(0, 2 * NP) as c:
                for j in range(J):
                    act.wait_ge(yc_ok, c * J + (j + 1))
                    act.wait_ge(var_ok, 1 + c)
                    nc.scalar.activation(ysq[:, j], yt[:, j], ACT.Square).then_inc(sq_ok, 1)
                act.wait_ge(var_ok, 1 + c + 1)
                nc.scalar.activation(rst4, ps[:, 1, :], ACT.Sqrt, bias=eps_col).then_inc(std_ok, 1)
                for j in range(J):
                    act.wait_ge(yn_ok, c * J + (j + 1))
                    nc.scalar.activation(yt[:, j], yt[:, j], ACT.Identity, bias=norm_b[:, j:j + 1],
                                         scale=norm_g[:, j:j + 1]).then_inc(af_ok, 1)

            def token_std(b, k):
                act.wait_ge(tvar_ok, b * (2 * TB) + (k + 1))
                nc.scalar.activation(rstd5[:, k % 2], mv5[:, k % 2, 1:2], ACT.Sqrt, bias=eps_col).then_inc(tstd_ok, 1)

            with nc.scalar.Fori(0, B) as b:
                token_std(b, 0)
                for i in range(TB):
                    if i < TB - 1:
                        token_std(b, i + 1)
                    act.wait_ge(tp_ok, b * TB + (2 + i + 1))
                    act.wait_ge(at_ok, 1 + b * TB)
                    nc.scalar.activation(xnT[:, :, i * P:(i + 1) * P],
                                         ps[:, i % 2, 0:C].rearrange("p (t c) -> p t c", t=CT), ACT.Copy).then_inc(tpc_ok, 1)
                act.wait_ge(m_ok, b + 1)
                nc.scalar.activation(m_sb, ps[:, 2:5, 0:C], ACT.Copy).then_inc(mc_ok, 1)
                act.wait_ge(we_ok, b + 1)
                for cb, bank in enumerate((5, 7, 2)):
                    ins = nc.scalar.activation(w_eff[:, cb], ps[:, bank, 0:C], ACT.Copy)
                ins.then_inc(wec_ok, 1)
                token_std(b, TB)
                for i in range(TB):
                    if i < TB - 1:
                        token_std(b, TB + i + 1)
                    act.wait_ge(t2_ok, b * TB + (i + 3))
                    act.wait_ge(lg_ok, b * TB + (i + 1))
                    nc.scalar.activation(x2T[:, i % 2], ps[:, 2 + i % 2, 0:C].rearrange("p (t c) -> p t c", t=CT),
                                         ACT.Copy).then_inc(t2c_ok, 1)
                act.wait_ge(lg_ok, b * TB + (2 + TB))
                settled(act)
                nc.scalar.activation(logit[:, bass.ts(b, TB), :], ps[:, 4, 0:TB * E].rearrange("p (i e) -> p i e", e=E),
                                     ACT.Copy).then_inc(lgc_ok, 1)
            act.wait_ge(shift_ok, 1)
            nc.scalar.activation(logit, logit, ACT.Exp).then_inc(rexp_ok, 1)

            act.wait_ge(idx_ok, 1)
            with nc.scalar.Fori(0, E) as e:
                for t in range(CT):
                    act.wait_ge(xt_ok, e * CT + (t + 1))
                    nc.scalar.activation(xeT[:, t], ps[:, t, :], ACT.Copy).then_inc(xtc_ok, 1)
                for m in range(MT):
                    act.wait_ge(h_ok, e * MT + (m + 1))
                    if m == 0:
                        act.wait_ge(o_ok, e * CPT + 2)
                    settled(act)
                    nc.scalar.activation(h_sb[:, m], ps[:, 3 + m % 3, :], ACT.Gelu_apprx_tanh,
                                         bias=b1_col[:, e, m:m + 1]).then_inc(hg_ok, 1)
                act.wait_ge(yo_st, 1 + e * 16)
                for i in range(CPT):
                    act.wait_ge(ob_ok, 1 + e * CPT + (i + 1))
                    nc.scalar.activation(yo[:, i], y_pre[:, i % 2], ACT.Gelu_apprx_tanh).then_inc(og_ok, 1)

        @block.tensor
        def _(pe):
            pe.sem_inc(ya_ok, RING)
            for s in (tp_ok, vk_ok, t2_ok, lg_ok, o_ok):
                pe.sem_inc(s, 2)
            for s in (ip_ok, var_ok, at_ok, op_ok):
                pe.sem_inc(s, 1)
            pe.wait_ge(ld_c, LD_C)
            pe.wait_ge(setup, 1)

            with nc.tensor.Fori(0, NP) as p:
                for r in range(2):
                    pe.wait_ge(chan_ok, p * 2 + (r + 1))
                    for t in range(CT):
                        mm = pe.matmul(ps[0:GRP, 6, 0:2], gn_sel[:, t], chan[:, r, t], start=(t == 0), stop=(t == CT - 1))
                    mm.then_inc(grp_ok, 1)
                    pe.wait_ge(gaff_ok, p * 2 + (r + 1))
                    for t in range(CT):
                        mm = pe.matmul(ps[:, 7, 2 * t:2 * t + 2], gn_back[0:GRP, t], gaff[0:GRP, r], start=True, stop=True)
                    mm.then_inc(caff_ok, 1)
                    pe.wait_ge(xn_ok, p * 2 + (r + 1))
                    for j in range(J):
                        n = 3 * r + j
                        pe.wait_ge(ev_free, p * 9 + (n + 1))
                        for h in range(2):
                            for t in range(CT):
                                mm = pe.matmul(SLOT3[n % 3][:, h * 512:(h + 1) * 512], w_in[:, t, r, j],
                                               xt[:, r, t, h * 512:(h + 1) * 512], start=(t == 0), stop=(t == CT - 1))
                        mm.then_inc(ip_ok, 1)
                for j in range(J):
                    pe.wait_ge(ev_free, p * 9 + (7 + j))
                    pe.wait_ge(xh_ok, p * 6 + (3 + j + 1))
                    for h in range(2):
                        for tap in range(9):
                            dy, dx = divmod(tap, 3)
                            y0 = dy + h * (HW // 2)
                            mm = pe.matmul(SLOT3[j][:, h * 512:(h + 1) * 512].rearrange("p (h w) -> p h w", w=HW),
                                           conv_diag[:, j, tap], xpad[:, j, y0:y0 + HW // 2, dx:dx + HW],
                                           start=(tap == 0), stop=(tap == 8))
                    mm.then_inc(ip_ok, 1)

            pe.wait_ge(ev_free, 3 + 9 * NP)
            pe.wait_ge(xT_ok, J * NP)
            with nc.tensor.Fori(0, NP) as p:
                for k in range(K):
                    o = k % 2
                    for m, (r0, rows) in enumerate(((0, BR), (BR, BR), (2 * BR, DR))):
                        if m < 2:
                            pe.wait_ge(split_ok, p * (4 * K) + (4 * k + m + 1))
                        else:
                            pe.wait_ge(dts_free, p * K + (k + 1))
                            settled(pe)
                        for h in range(2):
                            for j in range(J):
                                mm = pe.matmul(SLOT3[m][0:rows, h * 512:(h + 1) * 512], xproj_w[:, k, j, r0:r0 + rows],
                                               xy[:, p * OJ + (o * J + j), h * 512:(h + 1) * 512],
                                               start=(j == 0), stop=(j == J - 1))
                        mm.then_inc(xp_ok, 1)

            def spread(q, u, m, dst):
                dr, n = divmod(u, N)
                for h in range(2):
                    mm = pe.matmul(dst[:, h * 512:(h + 1) * 512], sel_lhs[0:BR, n],
                                   bc[0:BR, q // J, dr, m, h * 512:(h + 1) * 512], start=True, stop=True)
                return mm

            def delta_product(q, dr):
                pe.wait_ge(wdt_ok, q * 2 + (dr + 1))
                for h in range(2):
                    mm = pe.matmul(C_PS[:, h * 512:(h + 1) * 512], wdt_cur[0:DR, dr],
                                   dts[0:DR, q // J, dr, h * 512:(h + 1) * 512], start=True, stop=True)
                mm.then_inc(dt_ok, 1)

            def add_y(q, u):
                if u == 0:
                    pe.wait_ge(dd_ok, q + 1)
                    if not (isinstance(q, int) and q == 0):
                        pe.wait_ge(yev_ok, q)
                    for h in range(2):
                        pe.matmul(Y_PS[:, h * 512:(h + 1) * 512], d_diag, xy[:, q, h * 512:(h + 1) * 512], start=True, stop=False)
                pe.wait_ge(p2_ok, q * UN + (u + 1 + RING))
                for h in range(2):
                    mm = pe.matmul(Y_PS[:, h * 512:(h + 1) * 512], ident, hst[:, u % RING, h * 512:(h + 1) * 512],
                                   start=False, stop=(u == UN - 1))
                mm.then_inc(ya_ok, 1)

            def tile_steps(q, first, last):
                for u in range(UN):
                    dr, n = divmod(u, N)
                    U = q * UN + u
                    pe.wait_ge(sc_ok, U + 1)
                    spread(q, u, 0, B_PS[u % 2]).then_inc(b_ok, 1)
                    pe.wait_ge(c_free, U + 1)
                    if n == 4 and not (last and dr):
                        pe.wait_ge(dtev_ok, q * 2 + (dr + 2))
                    spread(q, u, 1, C_PS).then_inc(c_ok, 1)
                    if n == 3 and not (last and dr):
                        pe.wait_ge(c_free, U + 2)
                        delta_product(q + dr, 1 - dr)
                    if u >= LAG:
                        add_y(q, u - LAG)
                    elif not first:
                        add_y(q - 1, UN - LAG + u)

            pe.wait_ge(split_ok, 4 + 4 * K * NP)
            pe.wait_ge(dts_free, 1 + K * NP)
            delta_product(0, 0)
            pe.wait_ge(dtev_ok, 1)
            tile_steps(0, True, False)
            with nc.tensor.Fori(1, NQ - 1) as q:
                tile_steps(q, False, False)
            tile_steps(NQ - 1, False, True)
            for u in range(UN - LAG, UN):
                add_y(NQ - 1, u)

            pe.wait_ge(ld4, 32)
            with nc.tensor.Fori(0, 2 * NP) as c:
                pe.wait_ge(yt_ok, c * J + J)
                for j in range(J):
                    mm = pe.matmul(ps[:, 0, :], mean_w, yt[:, j], start=(j == 0), stop=(j == J - 1))
                mm.then_inc(mean_ok, 1)
                pe.wait_ge(sq_ok, c * J + J)
                for j in range(J):
                    mm = pe.matmul(ps[:, 1, :], mean_w, ysq[:, j], start=(j == 0), stop=(j == J - 1))
                mm.then_inc(var_ok, 1)
                pe.wait_ge(yg_ok, 1 + c * J + J)
                for r in range(2):
                    lo = H2 * r
                    for i in range(4):
                        pe.wait_ge(ta_ok, c * 8 + (4 * r + i + 1))
                        for j in range(J):
                            mm = pe.matmul(ps[:, 2 + i, 0:C], yg[lo:lo + H2, j, i * P:(i + 1) * P], w_out[lo:lo + H2, j],
                                           start=(j == 0), stop=(j == J - 1))
                        mm.then_inc(op_ok, 1)

            pe.wait_ge(ld5, 16 * 9)
            pe.wait_ge(ta_ok, 4 + NT)
            with nc.tensor.Fori(0, B) as b:
                pe.wait_ge(ta2_ok, 1 + b * TB)
                pe.wait_ge(t2c_ok, 1 + b * TB)
                pe.wait_ge(lgc_ok, 1 + b)
                for s in range(TB + 2):
                    if s < TB:
                        i = s
                        pe.wait_ge(xn5_ok, b * TB + (i + 1))
                        pe.wait_ge(tpc_ok, b * TB + (i + 1))
                        for t in range(CT):
                            mm = pe.transpose(ps[:, i % 2, t * P:(t + 1) * P], xn5[:, i % 2, t * P:(t + 1) * P], ident)
                        mm.then_inc(tp_ok, 1)
                    if 1 <= s <= TB:
                        i = s - 1
                        pe.wait_ge(tpc_ok, b * TB + (2 + i + 1))
                        pe.wait_ge(kvc_ok, b * TB + (i + 1))
                        for w in range(2):
                            for t in range(CT):
                                mm = pe.matmul(ps[:, 2 + 2 * (i % 2) + w, 0:C], xnT[:, t, i * P:(i + 1) * P],
                                               w_kv[:, t, w * C:(w + 1) * C], start=(t == 0), stop=(t == CT - 1))
                        mm.then_inc(kv_ok, 1)
                    if s >= 2:
                        i = s - 2
                        pe.wait_ge(kvc_ok, b * TB + (2 + i + 1))
                        if i == 0:
                            pe.wait_ge(bd_ok, 1 + b)
                        for t in range(CT):
                            mm = pe.matmul(ps[:, 6, t * P:(t + 1) * P], kv[:, i % 2, 1, t * P:(t + 1) * P],
                                           kv[:, i % 2, 0, t * P:(t + 1) * P], start=(i == 0 and t == 0),
                                           stop=(i == TB - 1), skip_group_check=True)
                        mm.then_inc(vk_ok, 1)
                pe.wait_ge(bd_ok, 1 + b + 1)
                for t in range(CT):
                    mm = pe.matmul(ps[:, 2 + t, 0:C], bd[:, t], w_p[:, t], start=True, stop=True)
                mm.then_inc(m_ok, 1)
                pe.wait_ge(mc_ok, b + 1)
                for cb, bank in enumerate((5, 7, 2)):
                    for t in range(CT):
                        pe.matmul(ps[:, bank, 0:C], w_qT[:, t, cb * P:(cb + 1) * P], m_sb[:, t], start=(t == 0), stop=(t == CT - 1))
                for t in range(CT):
                    mm = pe.matmul(ps[0:1, 3, 0:C], bq_col[:, t:t + 1], m_sb[:, t], start=(t == 0), stop=(t == CT - 1))
                mm.then_inc(we_ok, 1)
                pe.wait_ge(wec_ok, b + 1)
                pe.wait_ge(bro_ok, b + 1)
                for s in range(TB + 2):
                    if s < TB:
                        i = s
                        if i >= 2:
                            pe.wait_ge(ta2_ok, 1 + b * TB + (i - 1))
                        for t in range(CT):
                            pe.matmul(ps[:, i % 2, 0:C], xnT[:, t, i * P:(i + 1) * P], w_eff[:, t], start=(t == 0), stop=False)
                        pe.matmul(ps[:, i % 2, 0:C], ones[0:1], brow[0:1], start=False, stop=True).then_inc(at_ok, 1)
                    if 1 <= s <= TB:
                        i = s - 1
                        pe.wait_ge(x2_ok, b * TB + (i + 1))
                        if i >= 2:
                            pe.wait_ge(t2c_ok, 1 + b * TB + (i - 1))
                        for t in range(CT):
                            mm = pe.transpose(ps[:, 2 + i % 2, t * P:(t + 1) * P], x2_cur[:, i % 2, t * P:(t + 1) * P], ident)
                        mm.then_inc(t2_ok, 1)
                    if s >= 2:
                        i = s - 2
                        pe.wait_ge(t2c_ok, 1 + b * TB + (i + 1))
                        for t in range(CT):
                            mm = pe.matmul(ps[:, 4, i * E:(i + 1) * E], x2T[:, i % 2, t], rt_w[:, t], start=(t == 0), stop=(t == CT - 1))
                        mm.then_inc(lg_ok, 1)
            pe.wait_ge(hot_ok, 1)
            pe.matmul(ps[:, 0, 0:NT * E], tri, hot.rearrange("p i e -> p (i e)"), start=True, stop=True)
            pe.matmul(ps[:, 1, 0:NT * E], ones, hot.rearrange("p i e -> p (i e)"), start=True, stop=True).then_inc(cum_ok, 1)

            pe.wait_ge(idx_ok, 1)
            with nc.tensor.Fori(0, E // 2) as g:
                for s in range(2):
                    e = g * 2 + s
                    pe.wait_ge(ld_xe, e * 16 + 16)
                    for t in range(CT):
                        for i in range(CPT):
                            mm = pe.transpose(ps[:, t, i * P:(i + 1) * P], xe[:, i, t * P:(t + 1) * P], ident)
                        mm.then_inc(xt_ok, 1)
                    pe.wait_ge(ld_w[s], g * 32 + 32)
                    pe.wait_ge(xtc_ok, e * CT + CT)
                    for m in range(MT):
                        if m >= 3:
                            pe.wait_ge(hg_ok, e * MT + (m - 2))
                        for t in range(CT):
                            mm = pe.matmul(ps[:, 3 + m % 3, :], w1[s][:, t, m * P:(m + 1) * P], xeT[:, t],
                                           start=(t == 0), stop=(t == CT - 1))
                        mm.then_inc(h_ok, 1)
                    for i in range(CPT):
                        if i == 0:
                            pe.wait_ge(hg_ok, e * MT + MT)
                        if i >= 2:
                            pe.wait_ge(ob_ok, 1 + e * CPT + (i - 1))
                        else:
                            pe.wait_ge(ob_ok, 1 + e * CPT)
                        for m in range(MT):
                            mm = pe.matmul(ps[:, 6 + i % 2, 0:C], h_sb[:, m, i * P:(i + 1) * P], w2[s][:, m],
                                           start=(m == 0), stop=(m == MT - 1))
                        mm.then_inc(o_ok, 1)

        @block.vector
        def _(dve):
            chain = Count(dve, dve_c)
            dve.sem_inc(split_ok, 4)
            dve.sem_inc(sc_ok, 2)
            dve.sem_inc(ta_ok, 4)
            dve.sem_inc(kvc_ok, 2)
            for s in (yg_ok, ta2_ok, bd_ok, ob_ok):
                dve.sem_inc(s, 1)
            dve.wait_ge(ld_c, LD_C)
            nc.vector.tensor_scalar(a_neg, a_neg, A_LOG_MAX, None, ALU.min).then_inc(a_cut, 1)
            for j in range(J):
                for tap in range(9):
                    nc.vector.tensor_scalar(conv_diag[:, j, tap], ident, conv_w[:, j, tap:tap + 1], None, ALU.mult)
            nc.vector.tensor_tensor(d_sum.rearrange("p q one -> p (q one)"), d_two[:, 0], d_two[:, 1], ALU.add).then_inc(setup, 1)
            dve.wait_ge(a_exp, 1)
            nc.vector.tensor_scalar(a_neg, a_neg, -1.0, None, ALU.mult).then_inc(setup, 1)

            with nc.vector.Fori(0, NP) as p:
                chain.enter(p, 2 * 8)
                for r in range(2):
                    dve.wait_ge(ld_x[r], p * 16 + 16)
                    for t in range(CT):
                        for h in range(2):
                            ins = nc.vector.bn_stats(bst[:, r, t, h], xt[:, r, t, h * 512:(h + 1) * 512])
                    chain.link(ins)
                    settled(dve)
                    for t in range(CT):
                        ins = nc.vector.bn_aggr(mv[:, r, t], bst[:, r, t].rearrange("p h s -> p (h s)"))
                    chain.link(ins)
                    chain.link(nc.vector.tensor_tensor(chan[:, r, :, 1], mv[:, r, :, 0], mv[:, r, :, 0], ALU.mult))
                    chain.link(nc.vector.tensor_tensor(chan[:, r, :, 1], chan[:, r, :, 1], mv[:, r, :, 1], ALU.add))
                    nc.vector.tensor_copy(chan[:, r, :, 0], mv[:, r, :, 0]).then_inc(chan_ok, 1)
                    dve.wait_ge(grp_ok, p * 2 + (r + 1))
                    g = gst[0:GRP, r]
                    chain.link(nc.vector.tensor_copy(g[:, 0:2], ps[0:GRP, 6, 0:2]))
                    chain.link(nc.vector.tensor_tensor(g[:, 2:3], g[:, 0:1], g[:, 0:1], ALU.mult))
                    nc.vector.tensor_tensor(g[:, 3:4], g[:, 1:2], g[:, 2:3], ALU.subtract).then_inc(gvar_ok, 1)
                    dve.wait_ge(gstd_ok, p * 2 + (r + 1))
                    chain.link(nc.vector.reciprocal(gaff[0:GRP, r, 0:1], gaff[0:GRP, r, 0:1]))
                    nc.vector.scalar_tensor_tensor(out=gaff[0:GRP, r, 1:2], in0=g[:, 0:1], scalar=-1.0,
                                                   in1=gaff[0:GRP, r, 0:1], op0=ALU.mult, op1=ALU.mult).then_inc(gaff_ok, 1)
                    dve.wait_ge(caff_ok, p * 2 + (r + 1))
                    chain.link(nc.vector.tensor_copy(caff[:, r], ps[:, 7, 0:2 * CT].rearrange("p (t s) -> p t s", s=2)))
                    for t in range(CT):
                        ins = nc.vector.tensor_scalar(xt[:, r, t], xt[:, r, t], caff[:, r, t, 0:1], caff[:, r, t, 1:2], ALU.mult, ALU.add)
                    ins.then_inc(xn_ok, 1)
            chain.leave(NP)

            with nc.vector.Fori(0, NP) as p:
                for k in range(K):
                    o, dr = k % 2, k // 2
                    for m in range(2):
                        dve.wait_ge(split_ok, p * (4 * K) + (4 * k + m + 3))
                        dve.wait_ge(hi_ok, p * (2 * K) + (2 * k + m + 1))
                        nc.vector.scalar_tensor_tensor(out=split_rest[0:BR, m], in0=split_hi[0:BR, m], scalar=mask1[0:BR],
                                                       in1=SLOT3[m][0:BR], op0=ALU.mult, op1=ALU.add).then_inc(split_ok, 1)
                    for m in range(2):
                        dve.wait_ge(mid_ok, p * (2 * K) + (2 * k + m + 1))
                        nc.vector.scalar_tensor_tensor(out=bc[0:BR, p * 2 + o, dr, m, :], in0=split_mid[0:BR, m],
                                                       scalar=mask2[0:BR], in1=split_rest[0:BR, m],
                                                       op0=ALU.mult, op1=ALU.add).then_inc(split_ok, 1)

            def scans(q):
                for u in range(UN):
                    dr, n = divmod(u, N)
                    U = q * UN + u
                    if n == 0:
                        dve.wait_ge(du_ok, q * 2 + (dr + 1))
                    dve.wait_ge(b_ok, U + 1)
                    nc.vector.tensor_tensor(B_PS[u % 2], B_PS[u % 2], dux[:, dr], ALU.mult).then_inc(p1_ok, 1)
                    if u == 1:
                        nc.vector.tensor_scalar(d_diag, ident, d_sum[:, q % OJ, :], None, ALU.mult).then_inc(dd_ok, 1)
                    dve.wait_ge(p1_ok, U + 1)
                    dve.wait_ge(dec_ok, U + 1)
                    dve.wait_ge(ya_ok, U + 1)
                    h, f, x = hst[:, u % RING], decay[:, u % RING], B_PS[u % 2]
                    if dr:
                        h, f, x = h[:, ::-1], f[:, ::-1], x[:, ::-1]
                    nc.vector.tensor_tensor_scan(h, f, x, 0.0, ALU.mult, ALU.add).then_inc(sc_ok, 1)

            with nc.vector.Fori(0, NQ) as q:
                scans(q)

            dve.wait_ge(yev_ok, NQ)
            dve.wait_ge(ld_t, 16)
            with nc.vector.Fori(0, 2 * NP) as c:
                chain.enter(c, 1)
                p, h = c // 2, c % 2
                for j in range(J):
                    nc.vector.tensor_tensor(yt[:, j].rearrange("p (h w) -> p h w", w=HW),
                                            xy[:, p * OJ + j, :].rearrange("p (h w) -> p h w", w=HW)[:, bass.ts(h, HW // 2), :],
                                            xy[:, p * OJ + (J + j), :].rearrange("p (w h) -> p h w", h=HW)[:, bass.ts(h, HW // 2), :],
                                            ALU.add).then_inc(yt_ok, 1)
                dve.wait_ge(mean_ok, c + 1)
                for j in range(J):
                    nc.vector.tensor_tensor(yt[:, j], yt[:, j], ps[:, 0, :], ALU.subtract).then_inc(yc_ok, 1)
                dve.wait_ge(std_ok, c + 1)
                chain.link(nc.vector.reciprocal(rst4, rst4))
                for j in range(J):
                    nc.vector.tensor_tensor(yt[:, j], yt[:, j], rst4, ALU.mult).then_inc(yn_ok, 1)
                dve.wait_ge(ld_z, c * 16 + 16)
                dve.wait_ge(op_ok, 1 + c * 8)
                for j in range(J):
                    dve.wait_ge(af_ok, c * J + (j + 1))
                    nc.vector.tensor_tensor(yg[:, j], yt[:, j], z4[:, j], ALU.mult).then_inc(yg_ok, 1)
                for r in range(2):
                    for i in range(4):
                        dve.wait_ge(op_ok, 1 + c * 8 + (4 * r + i + 1))
                        row = tok[:, p * (2 * TB) + h * 4 + (r * TB + i), :]
                        nc.vector.tensor_tensor(row, row, ps[:, 2 + i, 0:C], ALU.add).then_inc(ta_ok, 1)
            chain.leave(2 * NP)

            def layer_norm(dst, src, b, k, done):
                s = k % 2
                settled(dve)
                chain.link(nc.vector.bn_stats(bst5[:, s], src))
                settled(dve)
                nc.vector.bn_aggr(mv5[:, s], bst5[:, s]).then_inc(tvar_ok, 1)
                dve.wait_ge(tstd_ok, b * (2 * TB) + (k + 1))
                chain.link(nc.vector.reciprocal(rstd5[:, s], rstd5[:, s]))
                nc.vector.tensor_scalar(dst, src, mv5[:, s, 0:1], rstd5[:, s], ALU.subtract, ALU.mult).then_inc(done, 1)

            dve.wait_ge(ta_ok, 4 + NT)
            dve.wait_ge(ld5, 16 * 9)
            with nc.vector.Fori(0, B) as b:
                chain.enter(b, 2 * 2 * TB)
                for i in range(TB + 1):
                    if i < TB:
                        dve.wait_ge(tp_ok, b * TB + (i + 1))
                        layer_norm(xn5[:, i % 2], tok[:, b * TB + i, :], b, i, xn5_ok)
                    if i >= 1:
                        k = i - 1
                        dve.wait_ge(kv_ok, b * TB + (k + 1))
                        dve.wait_ge(vk_ok, b * TB + (k + 1))
                        s = 2 + 2 * (k % 2)
                        nc.vector.tensor_tensor(kv[:, k % 2], ps[:, s:s + 2, 0:C], bkv, ALU.add).then_inc(kvc_ok, 1)
                dve.wait_ge(vk_ok, b * TB + (2 + TB))
                nc.vector.tensor_tensor(bd.rearrange("p t c -> p (t c)"), ps[:, 6, 0:C], head_mask, ALU.mult).then_inc(bd_ok, 1)
                dve.wait_ge(we_ok, b + 1)
                nc.vector.tensor_tensor(brow[0:1], ps[0:1, 3, 0:C], bproj[0:1], ALU.add).then_inc(bro_ok, 1)
                for i in range(TB):
                    dve.wait_ge(at_ok, 1 + b * TB + (i + 1))
                    row = tok[:, b * TB + i, :]
                    nc.vector.tensor_tensor(row, row, ps[:, i % 2, 0:C], ALU.add).then_inc(ta2_ok, 1)
                    dve.wait_ge(ta2_ok, 1 + b * TB + (i + 1))
                    dve.wait_ge(t2_ok, b * TB + (i + 1))
                    dve.wait_ge(x2s_ok, b * TB + (i + 1))
                    layer_norm(x2_cur[:, i % 2], row, b, TB + i, x2_ok)
            chain.leave(B)

            dve.wait_ge(lgc_ok, 1 + B)
            chain.link(nc.vector.tensor_reduce(mx, logit, AX.X, ALU.max))
            v = chain.step(nc.vector.tensor_tensor(logit, logit, mx.unsqueeze(2).to_broadcast([P, NT, E]), ALU.subtract))
            dve.wait_ge(dve_c, v)
            nc.vector.scalar_tensor_tensor(out=hot, in0=logit, scalar=0.0, in1=rank8, op0=ALU.is_ge, op1=ALU.mult).then_inc(shift_ok, 1)
            dve.wait_ge(shift_ok, 1)
            chain.link(nc.vector.tensor_reduce(best, hot, AX.X, ALU.max))
            nc.vector.tensor_tensor(hot, rank8, best.unsqueeze(2).to_broadcast([P, NT, E]), ALU.is_equal).then_inc(hot_ok, 1)
            dve.wait_ge(rexp_ok, 1)
            chain.link(nc.vector.tensor_reduce(esum, logit, AX.X, ALU.add))
            chain.link(nc.vector.reciprocal(gate, esum))
            dve.wait_ge(cum_ok, 1)
            chain.link(nc.vector.tensor_copy(tot.rearrange("p i e -> p (i e)"), ps[:, 1, 0:NT * E]))
            for e in range(E):
                ins = nc.vector.tensor_tensor_scan(run[:, :, e], ones[:, 0:NT], tot[:, :, e], 0.0, ALU.mult, ALU.add)
            chain.link(ins)
            chain.link(nc.vector.tensor_tensor(run, run, tot, ALU.subtract))
            chain.link(nc.vector.tensor_tensor(cpos, run, ps[:, 0, 0:NT * E].rearrange("p (i e) -> p i e", e=E), ALU.add))
            chain.link(nc.vector.tensor_tensor(cpos, cpos, hot, ALU.mult))
            chain.link(nc.vector.tensor_reduce(pos, cpos, AX.X, ALU.add))
            chain.link(nc.vector.tensor_scalar(keep, pos, float(CAP) - 0.5, None, ALU.is_lt))
            chain.link(nc.vector.scalar_tensor_tensor(out=pos, in0=best, scalar=-float(CAP), in1=pos, op0=ALU.mult, op1=ALU.add))
            chain.link(nc.vector.tensor_scalar(pos, pos, float(E * CAP), None, ALU.add))
            chain.link(nc.vector.tensor_tensor(slot_g, pos, keep, ALU.mult))
            chain.link(nc.vector.tensor_tensor(gate, gate, keep, ALU.mult))
            chain.link(nc.vector.tensor_scalar(keep, keep, -DROPPED, DROPPED, ALU.mult, ALU.add))
            nc.vector.tensor_tensor(slot_s, pos, keep, ALU.add).then_inc(idx_ok, 1)

            dve.wait_ge(ld_b2, 16)
            with nc.vector.Fori(0, E) as e:
                for i in range(CPT):
                    dve.wait_ge(o_ok, e * CPT + (i + 3))
                    if i >= 2:
                        dve.wait_ge(og_ok, 1 + e * CPT + (i - 1))
                    else:
                        dve.wait_ge(og_ok, 1 + e * CPT)
                    nc.vector.tensor_tensor(y_pre[:, i % 2], ps[:, 6 + i % 2, 0:C], b2_bc[:, e, :], ALU.add).then_inc(ob_ok, 1)

            for i in range(NT):
                if i % 4 == 0:
                    dve.wait_ge(gath[i // 4], 64)
                nc.vector.scalar_tensor_tensor(out=tok[:, i], in0=got[:, i], scalar=gate[:, i:i + 1], in1=tok[:, i],
                                               op0=ALU.mult, op1=ALU.add).then_inc(fin_ok, 1)


def _layouts(i):
    import numpy as np
    f = np.float32
    twice = lambda v: np.concatenate([v, v], 0)
    thirds = lambda v: twice(np.moveaxis(v.reshape((J, H2) + v.shape[1:]), 1, 0))
    order = [[o + 2 * d for d in range(2)] for o in range(2)]
    x = i["x"].reshape(B, S, C)
    d = {}
    d["xT"] = x.transpose(0, 2, 1).reshape(B, CT, P, S).transpose(0, 2, 1, 3)
    d["x_tok"] = x.reshape(NT, P, C).transpose(1, 0, 2)
    w = i["L0_conv_in_proj_w"].T.reshape(CT, P, 2, J, H2)
    d["w_in"] = np.stack([np.concatenate([w[:, :, 0], w[:, :, 1]], -1), np.concatenate([w[:, :, 1], w[:, :, 0]], -1)], 2).transpose(1, 0, 2, 3, 4)
    d["conv_w"] = thirds(i["L0_conv_conv_w"].reshape(DI, 9))
    for name, key in (("conv_b", "L0_conv_conv_b"), ("norm_g", "L0_conv_out_norm_g"), ("norm_b", "L0_conv_out_norm_b")):
        d[name] = thirds(i[key])
    xp = i["L0_conv_x_proj_w"]
    big = np.zeros((2, H2, K, J, XR), f)
    for im in range(2):
        for part in range(PART):
            for m in range(2):
                rows = xp[:, R + m * N:R + (m + 1) * N].reshape(K, N, J, H2).transpose(3, 0, 2, 1)
                at = m * BR + im * PART * N + part * N
                big[im, :, :, :, at:at + N] = rows
        at = 2 * BR + im * R
        big[im, :, :, :, at:at + R] = xp[:, 0:R].reshape(K, R, J, H2).transpose(3, 0, 2, 1)
    d["xproj_w"] = big.reshape(P, K, J, XR)
    dw = i["L0_conv_dt_projs_w"].reshape(K, J, H2, R)[order]
    big = np.zeros((2, R, 2, J, 2, 2, H2), f)
    for im in range(2):
        big[im, :, :, :, :, im, :] = dw.transpose(4, 0, 2, 1, 3)
    d["dt_w"] = big.reshape(DR, OJ, 2, P)
    d["dt_bias"] = twice(i["L0_conv_dt_projs_b"].reshape(K, J, H2)[order].transpose(3, 0, 2, 1).reshape(H2, OJ, 2, 1))
    d["a_logs"] = twice(i["L0_conv_A_logs"].reshape(K, J, H2, N)[order].transpose(3, 0, 2, 1, 4).reshape(H2, OJ, 2, N))
    d["ds"] = twice(i["L0_conv_Ds"].reshape(K, J, H2)[order].transpose(3, 1, 0, 2).reshape(H2, 2, OJ))
    d["w_out"] = thirds(i["L0_conv_out_proj_w"].T)
    wq = i["L1_attn_w_qkv"]
    rows = lambda v: v.reshape((CT, P) + v.shape[1:]).swapaxes(0, 1)
    d["w_kv"], d["w_qT"], d["w_p"] = rows(wq[:, C:]), rows(wq[:, :C].T), rows(i["L1_attn_w_proj"])
    bqkv = i["L1_attn_b_qkv"]
    d["bq"] = bqkv[:C].reshape(CT, P).T
    d["b_kv"] = np.broadcast_to(bqkv[C:].reshape(1, 2, C), (P, 2, C))
    d["b_proj"] = i["L1_attn_b_proj"].reshape(1, C)
    d["router_w"] = rows(i["L1_ffn_router_w"])
    d["w1"], d["w2"], d["b2"] = i["L1_ffn_w1"], i["L1_ffn_w2"], i["L1_ffn_b2"]
    d["b1"] = i["L1_ffn_b1"].reshape(E, MT, P).transpose(2, 0, 1)
    d["ident"], d["ones"] = np.eye(P, dtype=f), np.ones((P, P), f)
    row = np.arange(BR)
    part = (row // N) % PART
    d["mask1"], d["mask2"] = -(part >= 1).astype(f)[:, None], -(part == 2).astype(f)[:, None]
    d["mask1"], d["mask2"] = (np.concatenate([m, np.zeros((P - BR, 1), f)]) for m in (d["mask1"], d["mask2"]))
    d["sel"] = ((row[:, None, None] % N == np.arange(N)[None, :, None])
                & (row[:, None, None] // (PART * N) == np.arange(P)[None, None, :] // H2)).astype(f)
    d["sel"] = np.concatenate([d["sel"], np.zeros((P - BR, N, P), f)])
    ch = np.arange(C)
    g = (ch[:, None] // (C // GRP) == np.arange(GRP)[None]).astype(f)
    d["gn_sel"] = rows(g / f(C // GRP))
    d["gn_back"] = g.T.reshape(GRP, CT, P)
    pp = np.arange(P)
    d["mean_w"] = (pp[:, None] // H2 == pp[None] // H2).astype(f) / f(DI)
    d["head_mask"] = np.tile((pp[:, None] // HD == pp[None] // HD).astype(f) / np.sqrt(f(HD)), (1, CT))
    d["rank"] = np.broadcast_to((E - np.arange(E)).astype(f), (P, NT, E))
    d["tri"] = np.triu(np.ones((P, P), f))
    return d


def kernel(**inputs):
    import numpy as np
    import concourse.bacc as _bacc
    from concourse import mybir as _mybir
    from concourse.bass_utils import run_bass_kernel_spmd as _run

    nc = _bacc.Bacc("TRN2", target_bir_lowering=False, num_devices=1)
    arrays, aps = {}, {}
    for name, v in _layouts({k: np.asarray(v) for k, v in inputs.items()}).items():
        dt = BF16 if name == "sel" else F32
        v = np.ascontiguousarray(v).astype(_mybir.dt.np(BF16)) if name == "sel" else np.ascontiguousarray(v)
        arrays[f"in_{name}"] = v
        aps[name] = nc.dram_tensor(f"in_{name}", v.shape, dt, kind="ExternalInput").ap()
    out = nc.dram_tensor("out_0", (T, C), F32, kind="ExternalOutput").ap()
    hybrid_block_kernel(nc, aps, out)
    r = _run(nc, [arrays], core_ids=[0])
    return r.results[0]["out_0"].reshape(B, HW, HW, C)
```

```python
from contextlib import ExitStack

import concourse.bass as bass
from concourse import mybir

ALU = mybir.AluOpType
ACT = mybir.ActivationFunctionType
AX = mybir.AxisListType
F32 = mybir.dt.float32
BF16 = mybir.dt.bfloat16
U32 = mybir.dt.uint32

B, HW, C, DI, N, R, K = 4, 32, 384, 192, 16, 24, 4
S = HW * HW
T = B * S
P = 128
CT = C // P
H2 = P // 2
J = DI // H2
NP = B // 2
NQ = NP * 2 * J
OJ = 2 * J
PART = 3
BR = 2 * PART * N
DR = 2 * R
XR = 2 * BR + DR
UN = 2 * N
HALF = S // 2
DELTA_AT = (9, 10, 12, 13)
POOL_AT = 13
DT_AT = 4
ACT_AT = (5, 6, 8, 11)
RING = 4
LAG = 3
PADW = HW + 2
NT = T // P
TB = S // P
NH = 12
HD = C // NH
E, M = 8, 1536
MT = M // P
CAP = T // E
CPT = CAP // P
GRP = 32
A_LOG_MAX = 84.0
DROPPED = 100000.0


class Count:

    def __init__(self, eng, sem):
        self.eng, self.sem, self.base, self.n, self.loop, self.per = eng, sem, 0, 0, None, 0

    def enter(self, i, per):
        self.base, self.n, self.loop, self.per = self.base + self.n, 0, i, per

    def leave(self, trips):
        assert self.n == self.per, (self.n, self.per)
        self.base, self.n, self.loop = self.base + self.per * trips, 0, None

    def step(self, ins):
        ins.then_inc(self.sem, 1)
        self.n += 1
        v = self.base + self.n
        return v if self.loop is None else self.loop * self.per + v

    def link(self, ins):
        self.eng.wait_ge(self.sem, self.step(ins))


class Region:

    def __init__(self, arena, start, end):
        self.arena, self.at, self.end = arena, start, end

    def take(self, *dims, dtype=F32, rows=P):
        n = 1
        for d in dims:
            n *= d
        cols = n // 2 if dtype == BF16 else n
        assert self.at + cols <= self.end, (self.at, cols, self.end)
        v = self.arena[0:rows, self.at:self.at + cols]
        self.at += cols
        if dtype != F32:
            v = v.bitcast(dtype)
        if len(dims) > 1:
            names = [f"d{i}" for i in range(len(dims))]
            v = v.rearrange(f"p ({' '.join(names)}) -> p {' '.join(names)}", **dict(zip(names[1:], dims[1:])))
        return v


def hybrid_block_kernel(nc, a, out):
    with ExitStack() as ctx:
        def sem(name):
            return ctx.enter_context(nc.semaphore(name))

        z_dram = nc.dram_tensor("z_scratch", (NP, P, J, S), F32, kind="Internal").ap()
        slot_in = nc.dram_tensor("slot_in", (E * CAP, C), F32, kind="Internal").ap()
        slot_out = nc.dram_tensor("slot_out", (E * CAP, C), F32, kind="Internal").ap()

        COLS = 53200
        arena = ctx.enter_context(nc.sbuf_tensor("arena", [P, COLS], F32))
        ALWAYS = 3700
        XY = ALWAYS + NQ * S
        BCD = XY + 16 * S
        always = Region(arena, 0, ALWAYS)
        ident, ones = always.take(P), always.take(P)
        eps_col = always.take(1)
        a_neg = always.take(OJ, 2, N)
        dt_bias = always.take(OJ, 2, 1)
        d_sum = always.take(OJ, 1)
        d_two = always.take(2, OJ)
        mask1, mask2 = always.take(1), always.take(1)
        conv_b, norm_g, norm_b = always.take(J), always.take(J), always.take(J)
        b1_col, bq_col = always.take(E, MT), always.take(CT)
        sel_lhs = always.take(N, P, dtype=BF16)
        dt_w = always.take(OJ, 2, P)
        xy = Region(arena, ALWAYS, XY).take(NQ, S)

        rb = Region(arena, XY, BCD)
        bc = rb.take(2 * NP, 2, 2, S, dtype=BF16)
        dts = rb.take(2 * NP, 2, S)

        ra = Region(arena, XY, BCD)
        xt = ra.take(2, CT, S)
        w_in, conv_w = ra.take(CT, 2, J, P), ra.take(J, 9)
        gn_sel, gn_back = ra.take(CT, GRP), ra.take(CT, P)
        bst, mv, chan = ra.take(2, CT, 2, 6), ra.take(2, CT, 2), ra.take(2, CT, 2)
        gst, gaff, caff = ra.take(2, 4), ra.take(2, 2), ra.take(2, CT, 2)
        rw = Region(arena, BCD, COLS - CPT * C)
        z_sb, xpad, conv_diag = rw.take(J, S), rw.take(J, PADW, PADW), rw.take(J, 9, P)
        xproj_w = rw.take(K, J, XR)
        split_hi, split_mid = rw.take(2, S, dtype=BF16), rw.take(2, S, dtype=BF16)
        split_rest = rw.take(2, S)
        zeros = Region(arena, COLS - CPT * C, COLS).take(CPT * C)

        rs = Region(arena, BCD, COLS - CPT * C)
        t_abs, t_w = rs.take(S), rs.take(S)
        dlt, dux, decay = rs.take(2, S), rs.take(2, S), rs.take(RING, S)
        hst, c_sb = rs.take(RING, S), rs.take(RING, S)
        wdt_cur, d_diag = rs.take(2, P), rs.take(P)

        tok = Region(arena, XY, BCD).take(NT, C)
        R4 = XY + NT * C
        r4 = Region(arena, R4, COLS - CPT * C)
        w_out, mean_w = r4.take(J, C), r4.take(P)
        z4, yt, ysq, yg, rst4 = r4.take(J, HALF), r4.take(J, HALF), r4.take(J, HALF), r4.take(J, HALF), r4.take(HALF)

        x2 = Region(arena, ALWAYS, XY).take(NT, C)
        r5 = Region(arena, R4 + CT * M, COLS)
        w_kv, w_qT, w_p = r5.take(CT, 2 * C), r5.take(CT, C), r5.take(CT, C)
        bkv, head_mask, rt_w = r5.take(2, C), r5.take(C), r5.take(CT, E)
        xn5, xnT, kv, x2T = r5.take(2, C), r5.take(CT, S), r5.take(2, 2, C), r5.take(2, CT, P)
        x2_cur = r5.take(TB, C)
        bd, m_sb, w_eff = r5.take(CT, P), r5.take(CT, C), r5.take(CT, C)
        brow, bproj = r5.take(C), r5.take(C)
        bst5, mv5, rstd5 = r5.take(TB, 6), r5.take(TB, 2), r5.take(TB, 1)
        logit, hot, cpos, tot, run, rank8 = (r5.take(NT, E) for _ in range(6))
        tri = r5.take(P)
        pos, keep = r5.take(NT), r5.take(NT)
        rg = always
        mx, esum, best = (rg.take(NT) for _ in range(3))
        gate, slot_s, slot_g = rg.take(NT), rg.take(NT, dtype=U32), rg.take(NT, dtype=U32)
        tstat, trstd, tbst, tmv = rg.take(NT, 2), rg.take(NT, 1), rg.take(4, 6), rg.take(4, 2)

        w1 = [Region(arena, R4, R4 + CT * M).take(CT, M), None]
        r6y = Region(arena, ALWAYS, XY)
        w1[1] = r6y.take(CT, M)
        w2 = [None, r6y.take(MT, C)]
        b2_bc = r6y.take(E, C)
        r6 = Region(arena, R4 + CT * M, COLS)
        w2[0] = r6.take(MT, C)
        xe, xeT, h_sb = r6.take(CPT, C), r6.take(CT, CAP), r6.take(MT, CAP)
        y_pre, yo = r6.take(2, C), r6.take(CPT, C)
        got = Region(arena, ALWAYS, XY).take(NT, C)

        ps = ctx.enter_context(nc.psum_tensor("ps", [P, 8, 512], F32))

        def pair_of_banks(b):
            return ps[:, b:b + 2, :].rearrange("p b c -> p (b c)")

        SLOT3 = [pair_of_banks(b) for b in (0, 2, 4)]
        B_PS = [pair_of_banks(0), pair_of_banks(2)]
        C_PS, Y_PS = pair_of_banks(4), pair_of_banks(6)

        ld_c, ld_x, z_st = sem("ld_consts"), [sem("ld_x0"), sem("ld_x1")], [sem("z_stored0"), sem("z_stored1")]
        pool_set, dve_c, act_c = sem("pool_set"), sem("dve_chain"), sem("act_chain")
        a_cut, a_exp, setup = sem("a_clamped"), sem("a_exp"), sem("dve_setup")
        chan_ok, grp_ok, gaff_ok, caff_ok, xn_ok = (sem(n) for n in ("channel_stats", "group_sums", "group_affine", "channel_affine", "xn_ready"))
        ip_ok, ev_free, xh_ok, xT_ok = sem("slot_filled"), sem("slot_free"), sem("xh_padded"), sem("x_by_columns")
        xp_ok, hi_ok, mid_ok, split_ok, dts_free = (sem(n) for n in ("xproj_filled", "split_hi", "split_mid", "split_steps", "dt_rows_copied"))
        wdt_ok, dt_ok, dtev_ok, lost_ok, ln_ok = (sem(n) for n in ("dt_weights", "dt_filled", "dt_evacuated", "lost_part", "ln_ready"))
        d_ok, du_ok, pd_ok = sem("delta_ready"), sem("delta_x_ready"), sem("delta_uncorrected")
        u_ok, w_ok = sem("u_ready"), sem("w_ready")
        b_ok, c_ok, c_free, dec_ok, dd_ok = (sem(n) for n in ("b_spread", "c_spread", "c_copied", "decay_ready", "d_diag_ready"))
        p1_ok, sc_ok, p2_ok, ya_ok, yev_ok = (sem(n) for n in ("input_ready", "scanned", "readout_ready", "y_added", "y_evacuated"))
        ld4, ld_t, ld_z, yt_ok, mean_ok, yc_ok, sq_ok, var_ok, yn_ok, af_ok, yg_ok, op_ok, ta_ok = (sem(n) for n in (
            "ld_w4", "ld_tokens", "ld_z", "yt_ready", "mean_filled", "centred", "squared", "var_filled", "normed",
            "affine_done", "gated", "outproj_filled", "tokens_added"))
        ld5, xn5_ok, tp_ok, tpc_ok, kv_ok, kvc_ok, vk_ok, bd_ok, m_ok, mc_ok, we_ok, wec_ok, bro_ok = (sem(n) for n in (
            "ld_w5", "tokens_normed", "turned", "turned_copied", "kv_filled", "kv_copied", "vk_added", "vk_masked",
            "m_filled", "m_copied", "weff_filled", "weff_copied", "bias_row"))
        at_ok, ta2_ok, x2_ok, t2_ok, t2c_ok, lg_ok, lgc_ok = (sem(n) for n in (
            "attn_filled", "attn_added", "x2_ready", "x2_turned", "x2_turned_copied", "logits_filled", "logits_copied"))
        x2s_ok = sem("x2_stored")
        passed = sem("passed")
        gvar_ok, gstd_ok, std_ok = sem("group_var"), sem("group_std"), sem("std_ready")
        tvar_ok, tstd_ok = sem("token_var"), sem("token_std")
        shift_ok, rexp_ok, hot_ok, cum_ok, idx_ok = (sem(n) for n in ("logits_shifted", "router_exp", "one_hot", "cumsum_filled", "slots_ready"))
        zero_st, scat, ld_w, ld_xe, ld_b2 = sem("zeros_stored"), sem("scattered"), [sem("ld_set0"), sem("ld_set1")], sem("ld_slots"), sem("ld_b2")
        xt_ok, xtc_ok, h_ok, hg_ok, o_ok, ob_ok, og_ok, yo_st = (sem(n) for n in (
            "slots_turned", "slots_turned_copied", "h_filled", "h_gelu", "o_filled", "o_biased", "o_gelu", "slots_stored"))
        gath, fin_ok, out_st = [sem(f"gathered{g}") for g in range(NT // 4)], sem("final_ready"), sem("out_stored")

        CONSTS = [
            (ident, "ident"), (ones, "ones"), (a_neg, "a_logs"), (dt_bias, "dt_bias"), (d_two, "ds"),
            (mask1, "mask1"), (mask2, "mask2"), (conv_b, "conv_b"), (norm_g, "norm_g"), (norm_b, "norm_b"),
            (b1_col, "b1"), (bq_col, "bq"), (sel_lhs, "sel"), (dt_w[0:DR], "dt_w"), (w_in, "w_in"),
            (conv_w, "conv_w"), (gn_sel, "gn_sel"), (gn_back[0:GRP], "gn_back"), (xproj_w, "xproj_w"),
        ]
        LD_C = 16 * len(CONSTS)
        block = ctx.enter_context(nc.Block())

        def settled(eng):
            eng.sem_inc(passed, 1)

        @block.sync
        def _(sp):
            for s in (*z_st, yo_st):
                sp.sem_inc(s, 1)
            for dst, name in CONSTS:
                sp.dma_start(dst, a[name]).then_inc(ld_c, 16)
            sp.wait_ge(pool_set, 3)
            for e in range(E):
                sp.dma_start(slot_in[e * CAP:(e + 1) * CAP].rearrange("(p i) c -> p (i c)", i=CPT), zeros).then_inc(zero_st, 16)
            with nc.sync.Fori(0, NP) as p:
                for r in range(2):
                    sp.wait_ge(ip_ok, 1 + p * 9)
                    sp.dma_start(xt[:, r], a["xT"][p * 2 + r]).then_inc(ld_x[r], 16)
                for r in range(2):
                    sp.wait_ge(ev_free, 3 + p * 9 + (3 * r + 3))
                    lo = H2 * (1 - r)
                    sp.dma_start(z_dram[p, H2 * r:H2 * r + H2], z_sb[lo:lo + H2]).then_inc(z_st[r], 16)
            sp.wait_ge(yev_ok, NQ)
            sp.wait_ge(du_ok, 2 * NQ)
            for r in range(2):
                sp.wait_ge(z_st[r], 1 + 16 * NP)
            sp.dma_start(w_out, a["w_out"]).then_inc(ld4, 16)
            sp.dma_start(mean_w, a["mean_w"]).then_inc(ld4, 16)
            sp.dma_start(tok, a["x_tok"]).then_inc(ld_t, 16)
            with nc.sync.Fori(0, 2 * NP) as c:
                sp.wait_ge(yg_ok, 1 + c * J)
                sp.dma_start(z4, z_dram[c // 2, :, :, bass.ts(c % 2, HALF)]).then_inc(ld_z, 16)
            sp.wait_ge(ta_ok, 4 + NT)
            sp.wait_ge(zero_st, 16 * E)
            for dst, name in ((w_kv, "w_kv"), (w_qT, "w_qT"), (w_p, "w_p"), (bkv, "b_kv"), (head_mask, "head_mask"),
                              (rt_w, "router_w"), (bproj[0:1], "b_proj"), (rank8, "rank"), (tri, "tri")):
                sp.dma_start(dst, a[name]).then_inc(ld5, 16)
            w1_v = a["w1"].rearrange("e (t p) m -> e p t m", p=P)
            w2_v = a["w2"].rearrange("e (t p) c -> e p t c", p=P)
            sp.dma_start(w1[0], w1_v[0]).then_inc(ld_w[0], 16)
            sp.wait_ge(idx_ok, 1)
            sp.dma_start(w2[0], w2_v[0]).then_inc(ld_w[0], 16)
            sp.wait_ge(scat, 16 * NT)
            slot_in_v = slot_in.rearrange("(e i p) c -> e p i c", i=CPT, p=P)
            slot_out_v = slot_out.rearrange("(e i p) c -> e p i c", i=CPT, p=P)
            sp.dma_start(xe, slot_in_v[0]).then_inc(ld_xe, 16)
            sp.dma_start(b2_bc, a["b2"].rearrange("e c -> (e c)").partition_broadcast(P)).then_inc(ld_b2, 16)
            sp.dma_start(w1[1], w1_v[1]).then_inc(ld_w[1], 16)
            sp.dma_start(w2[1], w2_v[1]).then_inc(ld_w[1], 16)

            def slots_in(e):
                sp.wait_ge(xt_ok, e * CT)
                sp.dma_start(xe, slot_in_v[e]).then_inc(ld_xe, 16)

            def slots_out(e):
                sp.wait_ge(og_ok, 1 + e * CPT + CPT)
                sp.dma_start(slot_out_v[e], yo).then_inc(yo_st, 16)

            with nc.sync.Fori(0, E // 2 - 1) as g:
                for s in range(2):
                    slots_in(g * 2 + (s + 1))
                    slots_out(g * 2 + s)
                    sp.dma_start(w1[s], w1_v[g * 2 + (s + 2)]).then_inc(ld_w[s], 16)
                    sp.dma_start(w2[s], w2_v[g * 2 + (s + 2)]).then_inc(ld_w[s], 16)
            slots_in(E - 1)
            slots_out(E - 2)
            slots_out(E - 1)
            out_v = out.rearrange("(i p) c -> p i c", p=P)
            for g in range(NT // 4):
                sp.wait_ge(fin_ok, 4 * g + 4)
                sp.dma_start(out_v[:, 4 * g:4 * g + 4], tok[:, 4 * g:4 * g + 4]).then_inc(out_st, 16)
            sp.wait_ge(out_st, 16 * (NT // 4))

        @block.gpsimd
        def _(pool):
            pool.memset(xpad, 0.0).then_inc(pool_set, 1)
            pool.memset(eps_col, 1e-5).then_inc(pool_set, 1)
            pool.memset(zeros, 0.0).then_inc(pool_set, 1)
            pool.sem_inc(p2_ok, RING)
            pool.sem_inc(x2s_ok, 2)

            with nc.gpsimd.Fori(0, NP) as p:
                for j in range(J):
                    pool.wait_ge(ev_free, 3 + p * 9 + (6 + j + 1))
                    nc.gpsimd.tensor_copy(xy[:, p * OJ + (J + j), :].rearrange("p (w h) -> p w h", h=HW),
                                          xy[:, p * OJ + j, :].rearrange("p (h w) -> p w h", w=HW)).then_inc(xT_ok, 1)

            def delta_x(q, dr):
                pool.wait_ge(d_ok, q * 2 + (dr + 1))
                nc.gpsimd.tensor_tensor(dux[:, dr], dlt[:, dr], xy[:, q, :], ALU.mult).then_inc(du_ok, 1)

            def read_outs(q, last):
                for u in range(UN):
                    dr, n = divmod(u, N)
                    U = q * UN + u
                    pool.wait_ge(sc_ok, U + 3)
                    pool.wait_ge(c_free, U + 2)
                    nc.gpsimd.tensor_tensor(hst[:, u % RING], hst[:, u % RING], c_sb[:, u % RING], ALU.mult).then_inc(p2_ok, 1)
                    if n == POOL_AT and not (last and dr):
                        delta_x(q + dr, 1 - dr)

            pool.wait_ge(xT_ok, NP * J)
            delta_x(0, 0)
            with nc.gpsimd.Fori(0, NQ - 1) as q:
                read_outs(q, False)
            read_outs(NQ - 1, True)

            with nc.gpsimd.Fori(0, B) as b:
                for i in range(TB):
                    pool.wait_ge(x2_ok, b * TB + (i + 1))
                    nc.gpsimd.tensor_copy(x2[:, b * TB + i, :], x2_cur[:, i]).then_inc(x2s_ok, 1)

            pool.wait_ge(idx_ok, 1)
            pool.wait_ge(zero_st, 16 * E)
            pool.wait_ge(x2s_ok, 2 + NT)
            for i in range(NT):
                pool.indirect_dma_start(out=slot_in, out_offset=bass.IndirectOffsetOnAxis(ap=slot_s[:, i:i + 1], axis=0),
                                        in_=x2[:, i, :], in_offset=None, bounds_check=E * CAP - 1,
                                        oob_is_err=False).then_inc(scat, 16)
            pool.wait_ge(yo_st, 1 + 16 * E)
            pool.wait_ge(o_ok, E * CPT + 2)
            pool.wait_ge(ob_ok, 1 + E * CPT)
            for i in range(NT):
                pool.indirect_dma_start(out=got[:, i, :], out_offset=None, in_=slot_out,
                                        in_offset=bass.IndirectOffsetOnAxis(ap=slot_g[:, i:i + 1], axis=0),
                                        bounds_check=E * CAP - 1, oob_is_err=False).then_inc(gath[i // 4], 16)

        @block.scalar
        def _(act):
            chain = Count(act, act_c)
            act.sem_inc(ev_free, 3)
            act.sem_inc(dts_free, 1)
            act.sem_inc(c_free, 1)
            act.sem_inc(tpc_ok, 2)
            for s in (t2c_ok, lgc_ok, og_ok):
                act.sem_inc(s, 1)
            act.wait_ge(ld_c, LD_C)
            act.wait_ge(a_cut, 1)
            nc.scalar.activation(a_neg, a_neg, ACT.Exp).then_inc(a_exp, 1)
            act.wait_ge(pool_set, 3)

            with nc.scalar.Fori(0, NP) as p:
                for r in range(2):
                    act.wait_ge(gvar_ok, p * 2 + (r + 1))
                    nc.scalar.activation(gaff[0:GRP, r, 0:1], gst[0:GRP, r, 3:4], ACT.Sqrt, bias=eps_col[0:GRP]).then_inc(gstd_ok, 1)
                    act.wait_ge(z_st[r], 1 + p * 16)
                    for j in range(J):
                        n = 3 * r + j
                        lo, zlo = H2 * r, H2 * (1 - r)
                        act.wait_ge(ip_ok, 1 + p * 9 + (n + 1))
                        nc.scalar.activation(xpad[lo:lo + H2, j, 1:1 + HW, 1:1 + HW],
                                             SLOT3[n % 3][lo:lo + H2].rearrange("p (h w) -> p h w", w=HW),
                                             ACT.Copy).then_inc(xh_ok, 1)
                        nc.scalar.activation(z_sb[zlo:zlo + H2, j], SLOT3[n % 3][zlo:zlo + H2], ACT.Silu).then_inc(ev_free, 1)
                for j in range(J):
                    act.wait_ge(ip_ok, 1 + p * 9 + (7 + j))
                    settled(act)
                    nc.scalar.activation(xy[:, p * OJ + j, :], SLOT3[j], ACT.Silu, bias=conv_b[:, j:j + 1]).then_inc(ev_free, 1)

            with nc.scalar.Fori(0, NP) as p:
                for k in range(K):
                    o, dr = k % 2, k // 2
                    for m in range(2):
                        act.wait_ge(xp_ok, p * (3 * K) + (3 * k + m + 1))
                        nc.scalar.activation(split_hi[0:BR, m], SLOT3[m][0:BR], ACT.Copy).then_inc(hi_ok, 1)
                    act.wait_ge(xp_ok, p * (3 * K) + (3 * k + 3))
                    settled(act)
                    nc.scalar.activation(dts[0:DR, p * 2 + o, dr, :], SLOT3[2][0:DR], ACT.Copy).then_inc(dts_free, 1)
                    for m in range(2):
                        act.wait_ge(split_ok, p * (4 * K) + (4 + 4 * k + m + 1))
                        nc.scalar.activation(split_mid[0:BR, m], split_rest[0:BR, m], ACT.Copy).then_inc(mid_ok, 1)

            def delta_weights(q, dr):
                nc.scalar.activation(wdt_cur[0:DR, dr], dt_w[0:DR, q % OJ, dr, :], ACT.Copy).then_inc(wdt_ok, 1)

            u_made = [None]

            def delta_parts(q, dr, step):
                jq = q * 2 + dr
                bias = dt_bias[:, q % OJ, dr, :]
                if step == 0:
                    act.wait_ge(dt_ok, jq + 1)
                    if not (isinstance(jq, int) and jq == 0):
                        act.wait_ge(d_ok, jq)
                    settled(act)
                    nc.scalar.activation(dlt[:, dr], C_PS, ACT.Identity, bias=bias).then_inc(dtev_ok, 1)
                elif step == 1:
                    act.wait_ge(dtev_ok, jq + 1)
                    u_made[0] = chain.step(nc.scalar.activation(t_abs, dlt[:, dr], ACT.Abs))
                elif step == 2:
                    act.wait_ge(act_c, u_made[0])
                    nc.scalar.activation(dux[:, dr], t_abs, ACT.Exp, scale=-1.0).then_inc(u_ok, 1)
                else:
                    act.wait_ge(lost_ok, jq + 1)
                    nc.scalar.activation(t_w, t_w, ACT.Ln).then_inc(ln_ok, 1)

            def units(q, first, last):
                for u in range(UN):
                    dr, n = divmod(u, N)
                    U = q * UN + u
                    if n == 0:
                        act.wait_ge(d_ok, q * 2 + (dr + 1))
                    if not (first and u < RING):
                        act.wait_ge(sc_ok, U + (3 - RING))
                        settled(act)
                    nc.scalar.activation(decay[:, u % RING], dlt[:, dr], ACT.Exp,
                                         scale=a_neg[:, q % OJ, dr, n:n + 1]).then_inc(dec_ok, 1)
                    if u == LAG and not first:
                        evacuate_y(q - 1)
                    if n == ACT_AT[0] and not (last and dr):
                        delta_parts(q + dr, 1 - dr, 0)
                    act.wait_ge(c_ok, U + 1)
                    act.wait_ge(p2_ok, U + 1)
                    nc.scalar.activation(c_sb[:, u % RING], C_PS, ACT.Copy).then_inc(c_free, 1)
                    if not (last and dr):
                        nq, nd = q + dr, 1 - dr
                        if n == 1:
                            delta_weights(nq, nd)
                        if n in ACT_AT[1:]:
                            delta_parts(nq, nd, ACT_AT.index(n))

            def evacuate_y(q):
                act.wait_ge(ya_ok, q * UN + (UN + RING))
                act.wait_ge(du_ok, q * 2 + 2)
                settled(act)
                nc.scalar.activation(xy[:, q, :], Y_PS, ACT.Copy).then_inc(yev_ok, 1)

            act.wait_ge(split_ok, 4 + 4 * K * NP)
            act.wait_ge(xp_ok, 3 * K * NP)
            for r in range(2):
                act.wait_ge(z_st[r], 1 + 16 * NP)
            act.wait_ge(setup, 2)
            delta_weights(0, 0)
            for s in range(len(ACT_AT)):
                delta_parts(0, 0, s)
            units(0, True, False)
            PER = 2
            with nc.scalar.Fori(1, NQ - 1) as q:
                chain.enter(q - 1, PER)
                units(q, False, False)
            chain.leave(NQ - 2)
            units(NQ - 1, False, True)
            evacuate_y(NQ - 1)

            with nc.scalar.Fori(0, 2 * NP) as c:
                for j in range(J):
                    act.wait_ge(yc_ok, c * J + (j + 1))
                    act.wait_ge(var_ok, 1 + c)
                    nc.scalar.activation(ysq[:, j], yt[:, j], ACT.Square).then_inc(sq_ok, 1)
                act.wait_ge(var_ok, 1 + c + 1)
                nc.scalar.activation(rst4, ps[:, 1, :], ACT.Sqrt, bias=eps_col).then_inc(std_ok, 1)
                for j in range(J):
                    act.wait_ge(yn_ok, c * J + (j + 1))
                    nc.scalar.activation(yt[:, j], yt[:, j], ACT.Identity, bias=norm_b[:, j:j + 1],
                                         scale=norm_g[:, j:j + 1]).then_inc(af_ok, 1)

            act.wait_ge(tvar_ok, 1)
            nc.scalar.activation(trstd.rearrange("p i s -> p (i s)"), tstat[:, :, 1], ACT.Sqrt, bias=eps_col).then_inc(tstd_ok, 1)

            def turned(b, i):
                act.wait_ge(tp_ok, b * TB + (2 + i + 1))
                act.wait_ge(at_ok, 1 + b * TB)
                nc.scalar.activation(xnT[:, :, i * P:(i + 1) * P],
                                     ps[:, i % 2, 0:C].rearrange("p (t c) -> p t c", t=CT), ACT.Copy).then_inc(tpc_ok, 1)

            def x2_turned(b, i):
                act.wait_ge(t2_ok, b * TB + (i + 2))
                act.wait_ge(lg_ok, b * TB + (i + 1))
                nc.scalar.activation(x2T[:, i % 2], ps[:, 7, 0:C].rearrange("p (t c) -> p t c", t=CT),
                                     ACT.Copy).then_inc(t2c_ok, 1)

            def logits_out(b):
                act.wait_ge(lg_ok, b * TB + (2 + TB))
                settled(act)
                nc.scalar.activation(logit[:, bass.ts(b, TB), :], ps[:, 7, C:C + TB * E].rearrange("p (i e) -> p i e", e=E),
                                     ACT.Copy).then_inc(lgc_ok, 1)

            def image(b, first):
                for s in range(TB + 1):
                    if s < TB:
                        turned(b, s)
                    if s >= 1 and not first:
                        x2_turned(b - 1, s - 1)
                if not first:
                    logits_out(b - 1)
                act.wait_ge(m_ok, b + 1)
                nc.scalar.activation(m_sb, ps[:, 2:5, 0:C], ACT.Copy).then_inc(mc_ok, 1)
                act.wait_ge(we_ok, b + 1)
                for cb, bank in enumerate((5, 0, 1)):
                    ins = nc.scalar.activation(w_eff[:, cb], ps[:, bank, 0:C], ACT.Copy)
                ins.then_inc(wec_ok, 1)
                for g in range(2):
                    act.wait_ge(tvar_ok, b * 2 + (g + 2))
                    nc.scalar.activation(rstd5[:, 4 * g:4 * g + 4, 0], mv5[:, 4 * g:4 * g + 4, 1], ACT.Sqrt,
                                         bias=eps_col).then_inc(tstd_ok, 1)

            image(0, True)
            with nc.scalar.Fori(1, B) as b:
                image(b, False)
            for i in range(TB):
                x2_turned(B - 1, i)
            logits_out(B - 1)
            act.wait_ge(shift_ok, 1)
            nc.scalar.activation(logit, logit, ACT.Exp).then_inc(rexp_ok, 1)

            act.wait_ge(idx_ok, 1)
            with nc.scalar.Fori(0, E) as e:
                for t in range(CT):
                    act.wait_ge(xt_ok, e * CT + (t + 1))
                    nc.scalar.activation(xeT[:, t], ps[:, t, :], ACT.Copy).then_inc(xtc_ok, 1)
                for m in range(MT):
                    act.wait_ge(h_ok, e * MT + (m + 1))
                    if m == 0:
                        act.wait_ge(o_ok, e * CPT + 2)
                    settled(act)
                    nc.scalar.activation(h_sb[:, m], ps[:, 3 + m % 3, :], ACT.Gelu_apprx_tanh,
                                         bias=b1_col[:, e, m:m + 1]).then_inc(hg_ok, 1)
                act.wait_ge(yo_st, 1 + e * 16)
                for i in range(CPT):
                    act.wait_ge(ob_ok, 1 + e * CPT + (i + 1))
                    nc.scalar.activation(yo[:, i], y_pre[:, i % 2], ACT.Gelu_apprx_tanh).then_inc(og_ok, 1)

        @block.tensor
        def _(pe):
            pe.sem_inc(ya_ok, RING)
            for s in (tp_ok, vk_ok, lg_ok, o_ok):
                pe.sem_inc(s, 2)
            pe.sem_inc(t2_ok, 1)
            for s in (ip_ok, var_ok, at_ok, op_ok):
                pe.sem_inc(s, 1)
            pe.wait_ge(ld_c, LD_C)
            pe.wait_ge(setup, 1)

            with nc.tensor.Fori(0, NP) as p:
                for r in range(2):
                    pe.wait_ge(chan_ok, p * 2 + (r + 1))
                    for t in range(CT):
                        mm = pe.matmul(ps[0:GRP, 6, 0:2], gn_sel[:, t], chan[:, r, t], start=(t == 0), stop=(t == CT - 1))
                    mm.then_inc(grp_ok, 1)
                    pe.wait_ge(gaff_ok, p * 2 + (r + 1))
                    for t in range(CT):
                        mm = pe.matmul(ps[:, 7, 2 * t:2 * t + 2], gn_back[0:GRP, t], gaff[0:GRP, r], start=True, stop=True)
                    mm.then_inc(caff_ok, 1)
                    pe.wait_ge(xn_ok, p * 2 + (r + 1))
                    for j in range(J):
                        n = 3 * r + j
                        pe.wait_ge(ev_free, p * 9 + (n + 1))
                        for h in range(2):
                            for t in range(CT):
                                mm = pe.matmul(SLOT3[n % 3][:, h * 512:(h + 1) * 512], w_in[:, t, r, j],
                                               xt[:, r, t, h * 512:(h + 1) * 512], start=(t == 0), stop=(t == CT - 1))
                        mm.then_inc(ip_ok, 1)
                for j in range(J):
                    pe.wait_ge(ev_free, p * 9 + (7 + j))
                    pe.wait_ge(xh_ok, p * 6 + (3 + j + 1))
                    for h in range(2):
                        for tap in range(9):
                            dy, dx = divmod(tap, 3)
                            y0 = dy + h * (HW // 2)
                            mm = pe.matmul(SLOT3[j][:, h * 512:(h + 1) * 512].rearrange("p (h w) -> p h w", w=HW),
                                           conv_diag[:, j, tap], xpad[:, j, y0:y0 + HW // 2, dx:dx + HW],
                                           start=(tap == 0), stop=(tap == 8))
                    mm.then_inc(ip_ok, 1)

            pe.wait_ge(ev_free, 3 + 9 * NP)
            pe.wait_ge(xT_ok, J * NP)
            with nc.tensor.Fori(0, NP) as p:
                for k in range(K):
                    o = k % 2
                    for m, (r0, rows) in enumerate(((0, BR), (BR, BR), (2 * BR, DR))):
                        if m < 2:
                            pe.wait_ge(split_ok, p * (4 * K) + (4 * k + m + 1))
                        else:
                            pe.wait_ge(dts_free, p * K + (k + 1))
                            settled(pe)
                        for h in range(2):
                            for j in range(J):
                                mm = pe.matmul(SLOT3[m][0:rows, h * 512:(h + 1) * 512], xproj_w[:, k, j, r0:r0 + rows],
                                               xy[:, p * OJ + (o * J + j), h * 512:(h + 1) * 512],
                                               start=(j == 0), stop=(j == J - 1))
                        mm.then_inc(xp_ok, 1)

            def spread(q, u, m, dst):
                dr, n = divmod(u, N)
                for h in range(2):
                    mm = pe.matmul(dst[:, h * 512:(h + 1) * 512], sel_lhs[0:BR, n],
                                   bc[0:BR, q // J, dr, m, h * 512:(h + 1) * 512], start=True, stop=True)
                return mm

            def delta_product(q, dr):
                pe.wait_ge(wdt_ok, q * 2 + (dr + 1))
                for h in range(2):
                    mm = pe.matmul(C_PS[:, h * 512:(h + 1) * 512], wdt_cur[0:DR, dr],
                                   dts[0:DR, q // J, dr, h * 512:(h + 1) * 512], start=True, stop=True)
                mm.then_inc(dt_ok, 1)

            def add_y(q, u):
                if u == 0:
                    pe.wait_ge(dd_ok, q + 1)
                    if not (isinstance(q, int) and q == 0):
                        pe.wait_ge(yev_ok, q)
                    for h in range(2):
                        pe.matmul(Y_PS[:, h * 512:(h + 1) * 512], d_diag, xy[:, q, h * 512:(h + 1) * 512], start=True, stop=False)
                pe.wait_ge(p2_ok, q * UN + (u + 1 + RING))
                for h in range(2):
                    mm = pe.matmul(Y_PS[:, h * 512:(h + 1) * 512], ident, hst[:, u % RING, h * 512:(h + 1) * 512],
                                   start=False, stop=(u == UN - 1))
                mm.then_inc(ya_ok, 1)

            def add_trailing_y(q, u, first):
                if u >= LAG:
                    add_y(q, u - LAG)
                elif not first:
                    add_y(q - 1, UN - LAG + u)

            def tile_steps(q, first, last):
                for u in range(UN):
                    dr, n = divmod(u, N)
                    U = q * UN + u
                    pe.wait_ge(sc_ok, U + 1)
                    spread(q, u, 0, B_PS[u % 2]).then_inc(b_ok, 1)
                    after_dt = n == DT_AT + 1 and not (last and dr)
                    if after_dt:
                        add_trailing_y(q, u, first)
                        pe.wait_ge(dtev_ok, q * 2 + (dr + 2))
                    pe.wait_ge(c_free, U + 1)
                    spread(q, u, 1, C_PS).then_inc(c_ok, 1)
                    if not after_dt:
                        add_trailing_y(q, u, first)
                    if n == DT_AT and not (last and dr):
                        pe.wait_ge(c_free, U + 2)
                        delta_product(q + dr, 1 - dr)

            pe.wait_ge(split_ok, 4 + 4 * K * NP)
            pe.wait_ge(dts_free, 1 + K * NP)
            delta_product(0, 0)
            pe.wait_ge(dtev_ok, 1)
            tile_steps(0, True, False)
            with nc.tensor.Fori(1, NQ - 1) as q:
                tile_steps(q, False, False)
            tile_steps(NQ - 1, False, True)
            for u in range(UN - LAG, UN):
                add_y(NQ - 1, u)

            pe.wait_ge(ld4, 32)
            def mean_sums(c):
                pe.wait_ge(yt_ok, c * J + J)
                for j in range(J):
                    mm = pe.matmul(ps[:, 0, :], mean_w, yt[:, j], start=(j == 0), stop=(j == J - 1))
                mm.then_inc(mean_ok, 1)

            def square_sums(c):
                pe.wait_ge(sq_ok, c * J + J)
                for j in range(J):
                    mm = pe.matmul(ps[:, 1, :], mean_w, ysq[:, j], start=(j == 0), stop=(j == J - 1))
                mm.then_inc(var_ok, 1)

            def out_proj(c, r, tiles):
                lo = H2 * r
                pe.wait_ge(yg_ok, 1 + c * J + J)
                for i in tiles:
                    pe.wait_ge(ta_ok, c * 8 + (4 * r + i + 1))
                    for j in range(J):
                        mm = pe.matmul(ps[:, 2 + i, 0:C], yg[lo:lo + H2, j, i * P:(i + 1) * P], w_out[lo:lo + H2, j],
                                       start=(j == 0), stop=(j == J - 1))
                    mm.then_inc(op_ok, 1)

            def gated_steps(c, last):
                out_proj(c, 0, range(4))
                if not last:
                    mean_sums(c + 1)
                out_proj(c, 1, range(2))
                if not last:
                    square_sums(c + 1)
                out_proj(c, 1, range(2, 4))

            mean_sums(0)
            square_sums(0)
            with nc.tensor.Fori(0, 2 * NP - 1) as c:
                gated_steps(c, False)
            gated_steps(2 * NP - 1, True)

            pe.wait_ge(ld5, 16 * 9)
            pe.wait_ge(ta_ok, 4 + NT)

            def turn(b, i):
                pe.wait_ge(xn5_ok, b * TB + (i + 1))
                pe.wait_ge(tpc_ok, b * TB + (i + 1))
                for t in range(CT):
                    mm = pe.transpose(ps[:, i % 2, t * P:(t + 1) * P], xn5[:, i % 2, t * P:(t + 1) * P], ident)
                mm.then_inc(tp_ok, 1)

            def keys_values(b, i):
                pe.wait_ge(tpc_ok, b * TB + (2 + i + 1))
                pe.wait_ge(kvc_ok, b * TB + (i + 1))
                for w in range(2):
                    for t in range(CT):
                        mm = pe.matmul(ps[:, 2 + 2 * (i % 2) + w, 0:C], xnT[:, t, i * P:(i + 1) * P],
                                       w_kv[:, t, w * C:(w + 1) * C], start=(t == 0), stop=(t == CT - 1))
                mm.then_inc(kv_ok, 1)

            def values_by_keys(b, i):
                pe.wait_ge(kvc_ok, b * TB + (2 + i + 1))
                if i == 0:
                    pe.wait_ge(bd_ok, 1 + b)
                for t in range(CT):
                    mm = pe.matmul(ps[:, 6, t * P:(t + 1) * P], kv[:, i % 2, 1, t * P:(t + 1) * P],
                                   kv[:, i % 2, 0, t * P:(t + 1) * P], start=(i == 0 and t == 0),
                                   stop=(i == TB - 1), skip_group_check=True)
                mm.then_inc(vk_ok, 1)

            def router_step(b, s):
                if s >= 1:
                    pe.wait_ge(t2c_ok, 1 + b * TB + s)
                    for t in range(CT):
                        mm = pe.matmul(ps[:, 7, C + (s - 1) * E:C + s * E], x2T[:, (s - 1) % 2, t], rt_w[:, t],
                                       start=(t == 0), stop=(t == CT - 1))
                    mm.then_inc(lg_ok, 1)
                if s < TB:
                    if s == 0:
                        pe.wait_ge(lgc_ok, 1 + b)
                    pe.wait_ge(x2_ok, b * TB + (s + 1))
                    for t in range(CT):
                        mm = pe.transpose(ps[:, 7, t * P:(t + 1) * P], x2_cur[:, s, t * P:(t + 1) * P], ident)
                    mm.then_inc(t2_ok, 1)

            def image(b, first):
                for s in range(TB + 2):
                    if s < TB:
                        turn(b, s)
                    if s == 1:
                        pe.wait_ge(ta2_ok, 1 + b * TB)
                    if 1 <= s <= TB:
                        keys_values(b, s - 1)
                    if s >= 2:
                        values_by_keys(b, s - 2)
                    if s >= 1 and not first:
                        router_step(b - 1, s - 1)
                pe.wait_ge(bd_ok, 1 + b + 1)
                for t in range(CT):
                    mm = pe.matmul(ps[:, 2 + t, 0:C], bd[:, t], w_p[:, t], start=True, stop=True)
                mm.then_inc(m_ok, 1)
                pe.wait_ge(mc_ok, b + 1)
                for cb, bank in enumerate((5, 0, 1)):
                    for t in range(CT):
                        pe.matmul(ps[:, bank, 0:C], w_qT[:, t, cb * P:(cb + 1) * P], m_sb[:, t], start=(t == 0), stop=(t == CT - 1))
                for t in range(CT):
                    mm = pe.matmul(ps[0:1, 2, 0:C], bq_col[:, t:t + 1], m_sb[:, t], start=(t == 0), stop=(t == CT - 1))
                mm.then_inc(we_ok, 1)
                pe.wait_ge(wec_ok, b + 1)
                pe.wait_ge(bro_ok, b + 1)
                for i in range(TB):
                    if i >= 2:
                        pe.wait_ge(ta2_ok, 1 + b * TB + (i - 1))
                    for t in range(CT):
                        pe.matmul(ps[:, 3 + i % 2, 0:C], xnT[:, t, i * P:(i + 1) * P], w_eff[:, t], start=(t == 0), stop=False)
                    pe.matmul(ps[:, 3 + i % 2, 0:C], ones[0:1], brow[0:1], start=False, stop=True).then_inc(at_ok, 1)

            image(0, True)
            with nc.tensor.Fori(1, B) as b:
                image(b, False)
            for s in range(TB + 1):
                router_step(B - 1, s)
            pe.wait_ge(hot_ok, 1)
            pe.matmul(ps[:, 0, 0:NT * E], tri, hot.rearrange("p i e -> p (i e)"), start=True, stop=True)
            pe.matmul(ps[:, 1, 0:NT * E], ones, hot.rearrange("p i e -> p (i e)"), start=True, stop=True).then_inc(cum_ok, 1)

            pe.wait_ge(idx_ok, 1)
            with nc.tensor.Fori(0, E // 2) as g:
                for s in range(2):
                    e = g * 2 + s
                    pe.wait_ge(ld_xe, e * 16 + 16)
                    for t in range(CT):
                        for i in range(CPT):
                            mm = pe.transpose(ps[:, t, i * P:(i + 1) * P], xe[:, i, t * P:(t + 1) * P], ident)
                        mm.then_inc(xt_ok, 1)
                    pe.wait_ge(ld_w[s], g * 32 + 32)
                    pe.wait_ge(xtc_ok, e * CT + CT)
                    for m in range(MT):
                        if m >= 3:
                            pe.wait_ge(hg_ok, e * MT + (m - 2))
                        for t in range(CT):
                            mm = pe.matmul(ps[:, 3 + m % 3, :], w1[s][:, t, m * P:(m + 1) * P], xeT[:, t],
                                           start=(t == 0), stop=(t == CT - 1))
                        mm.then_inc(h_ok, 1)
                    for i in range(CPT):
                        if i == 0:
                            pe.wait_ge(hg_ok, e * MT + MT)
                        if i >= 2:
                            pe.wait_ge(ob_ok, 1 + e * CPT + (i - 1))
                        else:
                            pe.wait_ge(ob_ok, 1 + e * CPT)
                        for m in range(MT):
                            mm = pe.matmul(ps[:, 6 + i % 2, 0:C], h_sb[:, m, i * P:(i + 1) * P], w2[s][:, m],
                                           start=(m == 0), stop=(m == MT - 1))
                        mm.then_inc(o_ok, 1)

        @block.vector
        def _(dve):
            chain = Count(dve, dve_c)
            dve.sem_inc(split_ok, 4)
            dve.sem_inc(sc_ok, 2)
            dve.sem_inc(ta_ok, 4)
            dve.sem_inc(kvc_ok, 2)
            for s in (yg_ok, ta2_ok, bd_ok, ob_ok):
                dve.sem_inc(s, 1)
            dve.wait_ge(ld_c, LD_C)
            nc.vector.tensor_scalar(a_neg, a_neg, A_LOG_MAX, None, ALU.min).then_inc(a_cut, 1)
            for j in range(J):
                for tap in range(9):
                    nc.vector.tensor_scalar(conv_diag[:, j, tap], ident, conv_w[:, j, tap:tap + 1], None, ALU.mult)
            nc.vector.tensor_tensor(d_sum.rearrange("p q one -> p (q one)"), d_two[:, 0], d_two[:, 1], ALU.add).then_inc(setup, 1)
            dve.wait_ge(a_exp, 1)
            nc.vector.tensor_scalar(a_neg, a_neg, -1.0, None, ALU.mult).then_inc(setup, 1)

            with nc.vector.Fori(0, NP) as p:
                chain.enter(p, 2 * 8)
                for r in range(2):
                    dve.wait_ge(ld_x[r], p * 16 + 16)
                    for t in range(CT):
                        for h in range(2):
                            ins = nc.vector.bn_stats(bst[:, r, t, h], xt[:, r, t, h * 512:(h + 1) * 512])
                    chain.link(ins)
                    settled(dve)
                    for t in range(CT):
                        ins = nc.vector.bn_aggr(mv[:, r, t], bst[:, r, t].rearrange("p h s -> p (h s)"))
                    chain.link(ins)
                    chain.link(nc.vector.tensor_tensor(chan[:, r, :, 1], mv[:, r, :, 0], mv[:, r, :, 0], ALU.mult))
                    chain.link(nc.vector.tensor_tensor(chan[:, r, :, 1], chan[:, r, :, 1], mv[:, r, :, 1], ALU.add))
                    nc.vector.tensor_copy(chan[:, r, :, 0], mv[:, r, :, 0]).then_inc(chan_ok, 1)
                    dve.wait_ge(grp_ok, p * 2 + (r + 1))
                    g = gst[0:GRP, r]
                    chain.link(nc.vector.tensor_copy(g[:, 0:2], ps[0:GRP, 6, 0:2]))
                    chain.link(nc.vector.tensor_tensor(g[:, 2:3], g[:, 0:1], g[:, 0:1], ALU.mult))
                    nc.vector.tensor_tensor(g[:, 3:4], g[:, 1:2], g[:, 2:3], ALU.subtract).then_inc(gvar_ok, 1)
                    dve.wait_ge(gstd_ok, p * 2 + (r + 1))
                    chain.link(nc.vector.reciprocal(gaff[0:GRP, r, 0:1], gaff[0:GRP, r, 0:1]))
                    nc.vector.scalar_tensor_tensor(out=gaff[0:GRP, r, 1:2], in0=g[:, 0:1], scalar=-1.0,
                                                   in1=gaff[0:GRP, r, 0:1], op0=ALU.mult, op1=ALU.mult).then_inc(gaff_ok, 1)
                    dve.wait_ge(caff_ok, p * 2 + (r + 1))
                    chain.link(nc.vector.tensor_copy(caff[:, r], ps[:, 7, 0:2 * CT].rearrange("p (t s) -> p t s", s=2)))
                    for t in range(CT):
                        ins = nc.vector.tensor_scalar(xt[:, r, t], xt[:, r, t], caff[:, r, t, 0:1], caff[:, r, t, 1:2], ALU.mult, ALU.add)
                    ins.then_inc(xn_ok, 1)
            chain.leave(NP)

            with nc.vector.Fori(0, NP) as p:
                for k in range(K):
                    o, dr = k % 2, k // 2
                    for m in range(2):
                        dve.wait_ge(split_ok, p * (4 * K) + (4 * k + m + 3))
                        dve.wait_ge(hi_ok, p * (2 * K) + (2 * k + m + 1))
                        nc.vector.scalar_tensor_tensor(out=split_rest[0:BR, m], in0=split_hi[0:BR, m], scalar=mask1[0:BR],
                                                       in1=SLOT3[m][0:BR], op0=ALU.mult, op1=ALU.add).then_inc(split_ok, 1)
                    for m in range(2):
                        dve.wait_ge(mid_ok, p * (2 * K) + (2 * k + m + 1))
                        nc.vector.scalar_tensor_tensor(out=bc[0:BR, p * 2 + o, dr, m, :], in0=split_mid[0:BR, m],
                                                       scalar=mask2[0:BR], in1=split_rest[0:BR, m],
                                                       op0=ALU.mult, op1=ALU.add).then_inc(split_ok, 1)

            def delta(q, dr, step):
                jq = q * 2 + dr
                if step == 0:
                    dve.wait_ge(u_ok, jq + 1)
                    nc.vector.tensor_scalar(t_w, dux[:, dr], 1.0, None, ALU.add).then_inc(w_ok, 1)
                elif step == 1:
                    dve.wait_ge(w_ok, jq + 1)
                    nc.vector.scalar_tensor_tensor(out=t_abs, in0=t_w, scalar=-1.0, in1=dux[:, dr],
                                                   op0=ALU.add, op1=ALU.subtract).then_inc(lost_ok, 1)
                elif step == 2:
                    dve.wait_ge(ln_ok, jq + 1)
                    nc.vector.scalar_tensor_tensor(out=dlt[:, dr], in0=dlt[:, dr], scalar=0.0, in1=t_w,
                                                   op0=ALU.max, op1=ALU.add).then_inc(pd_ok, 1)
                elif step == 3:
                    dve.wait_ge(pd_ok, jq + 1)
                    nc.vector.tensor_tensor(dlt[:, dr], dlt[:, dr], t_abs, ALU.subtract).then_inc(d_ok, 1)

            def scans(q, last):
                for u in range(UN):
                    dr, n = divmod(u, N)
                    U = q * UN + u
                    if n == 0:
                        dve.wait_ge(du_ok, q * 2 + (dr + 1))
                    dve.wait_ge(b_ok, U + 1)
                    nc.vector.tensor_tensor(B_PS[u % 2], B_PS[u % 2], dux[:, dr], ALU.mult).then_inc(p1_ok, 1)
                    if u == 1:
                        nc.vector.tensor_scalar(d_diag, ident, d_sum[:, q % OJ, :], None, ALU.mult).then_inc(dd_ok, 1)
                    dve.wait_ge(p1_ok, U + 1)
                    dve.wait_ge(dec_ok, U + 1)
                    dve.wait_ge(ya_ok, U + 1)
                    h, f, x = hst[:, u % RING], decay[:, u % RING], B_PS[u % 2]
                    if dr:
                        h, f, x = h[:, ::-1], f[:, ::-1], x[:, ::-1]
                    nc.vector.tensor_tensor_scan(h, f, x, 0.0, ALU.mult, ALU.add).then_inc(sc_ok, 1)
                    if n in DELTA_AT and not (last and dr):
                        delta(q + dr, 1 - dr, DELTA_AT.index(n))

            for step in range(len(DELTA_AT)):
                delta(0, 0, step)
            with nc.vector.Fori(0, NQ - 1) as q:
                scans(q, False)
            scans(NQ - 1, True)

            dve.wait_ge(yev_ok, NQ)
            dve.wait_ge(ld_t, 16)
            def add_orders(c):
                p, h = c // 2, c % 2
                dve.wait_ge(yg_ok, 1 + c * J)
                for j in range(J):
                    nc.vector.tensor_tensor(yt[:, j].rearrange("p (h w) -> p h w", w=HW),
                                            xy[:, p * OJ + j, :].rearrange("p (h w) -> p h w", w=HW)[:, bass.ts(h, HW // 2), :],
                                            xy[:, p * OJ + (J + j), :].rearrange("p (w h) -> p h w", h=HW)[:, bass.ts(h, HW // 2), :],
                                            ALU.add).then_inc(yt_ok, 1)

            def centre(c):
                dve.wait_ge(mean_ok, c + 1)
                for j in range(J):
                    nc.vector.tensor_tensor(yt[:, j], yt[:, j], ps[:, 0, :], ALU.subtract).then_inc(yc_ok, 1)

            def scale_down(c):
                dve.wait_ge(std_ok, c + 1)
                chain.link(nc.vector.reciprocal(rst4, rst4))
                for j in range(J):
                    nc.vector.tensor_tensor(yt[:, j], yt[:, j], rst4, ALU.mult).then_inc(yn_ok, 1)

            def gate_y(c):
                dve.wait_ge(ld_z, c * 16 + 16)
                dve.wait_ge(op_ok, 1 + c * 8)
                for j in range(J):
                    dve.wait_ge(af_ok, c * J + (j + 1))
                    nc.vector.tensor_tensor(yg[:, j], yt[:, j], z4[:, j], ALU.mult).then_inc(yg_ok, 1)

            def add_tokens(c, r, tiles):
                first = (c // 2) * (2 * TB) + (c % 2) * 4 + r * TB
                for i in tiles:
                    dve.wait_ge(op_ok, 1 + c * 8 + (4 * r + i + 1))
                    row = tok[:, first + i, :]
                    nc.vector.tensor_tensor(row, row, ps[:, 2 + i, 0:C], ALU.add).then_inc(ta_ok, 1)
                dve.wait_ge(ta_ok, c * 8 + (4 + 4 * r + max(tiles) + 1))
                settled(dve)
                for i in tiles:
                    ins = nc.vector.bn_stats(tbst[:, i], tok[:, first + i, :])
                chain.link(ins)
                settled(dve)
                for i in tiles:
                    ins = nc.vector.bn_aggr(tmv[:, i], tbst[:, i])
                chain.link(ins)
                lo, hi = min(tiles), max(tiles) + 1
                chain.link(nc.vector.tensor_copy(tstat[:, bass.ds(first + lo, hi - lo), :], tmv[:, lo:hi]))

            def gated_steps(c, last):
                if not last:
                    add_orders(c + 1)
                add_tokens(c, 0, range(4))
                if not last:
                    centre(c + 1)
                add_tokens(c, 1, range(2))
                if not last:
                    scale_down(c + 1)
                add_tokens(c, 1, range(2, 4))
                if not last:
                    gate_y(c + 1)

            add_orders(0)
            centre(0)
            scale_down(0)
            gate_y(0)
            with nc.vector.Fori(0, 2 * NP - 1) as c:
                chain.enter(c, 10)
                gated_steps(c, False)
            chain.leave(2 * NP - 1)
            gated_steps(2 * NP - 1, True)
            dve.sem_inc(tvar_ok, 1)

            dve.wait_ge(tstd_ok, 1)
            chain.link(nc.vector.reciprocal(trstd, trstd))
            dve.wait_ge(ld5, 16 * 9)

            def attend(b, g):
                for i in range(4 * g, 4 * g + 4):
                    dve.wait_ge(at_ok, 1 + b * TB + (i + 1))
                    row = tok[:, b * TB + i, :]
                    nc.vector.tensor_tensor(row, row, ps[:, 3 + i % 2, 0:C], ALU.add).then_inc(ta2_ok, 1)

            def stats(b, g):
                dve.wait_ge(ta2_ok, 1 + b * TB + (4 * g + 4))
                settled(dve)
                for i in range(4 * g, 4 * g + 4):
                    ins = nc.vector.bn_stats(bst5[:, i], tok[:, b * TB + i, :])
                chain.link(ins)
                settled(dve)
                for i in range(4 * g, 4 * g + 4):
                    ins = nc.vector.bn_aggr(mv5[:, i], bst5[:, i])
                ins.then_inc(tvar_ok, 1)

            def normalise(b, g):
                dve.wait_ge(tstd_ok, b * 2 + (g + 2))
                chain.link(nc.vector.reciprocal(rstd5[:, 4 * g:4 * g + 4], rstd5[:, 4 * g:4 * g + 4]))
                dve.wait_ge(t2_ok, 1 + b * TB)
                dve.wait_ge(x2s_ok, 2 + b * TB)
                for i in range(4 * g, 4 * g + 4):
                    nc.vector.tensor_scalar(x2_cur[:, i], tok[:, b * TB + i, :], mv5[:, i, 0:1], rstd5[:, i],
                                            ALU.subtract, ALU.mult).then_inc(x2_ok, 1)

            with nc.vector.Fori(0, B) as b:
                chain.enter(b, 4)
                for i in range(TB + 1):
                    if i < TB:
                        dve.wait_ge(tp_ok, b * TB + (i + 1))
                        nc.vector.tensor_scalar(xn5[:, i % 2], tok[:, b * TB + i, :], tstat[:, b * TB + i, 0:1],
                                                trstd[:, b * TB + i, :], ALU.subtract, ALU.mult).then_inc(xn5_ok, 1)
                    if i >= 1:
                        k = i - 1
                        dve.wait_ge(kv_ok, b * TB + (k + 1))
                        dve.wait_ge(vk_ok, b * TB + (k + 1))
                        s = 2 + 2 * (k % 2)
                        nc.vector.tensor_tensor(kv[:, k % 2], ps[:, s:s + 2, 0:C], bkv, ALU.add).then_inc(kvc_ok, 1)
                dve.wait_ge(vk_ok, b * TB + (2 + TB))
                nc.vector.tensor_tensor(bd.rearrange("p t c -> p (t c)"), ps[:, 6, 0:C], head_mask, ALU.mult).then_inc(bd_ok, 1)
                dve.wait_ge(we_ok, b + 1)
                nc.vector.tensor_tensor(brow[0:1], ps[0:1, 2, 0:C], bproj[0:1], ALU.add).then_inc(bro_ok, 1)
                attend(b, 0)
                stats(b, 0)
                attend(b, 1)
                normalise(b, 0)
                stats(b, 1)
                normalise(b, 1)
            chain.leave(B)

            dve.wait_ge(lgc_ok, 1 + B)
            chain.link(nc.vector.tensor_reduce(mx, logit, AX.X, ALU.max))
            v = chain.step(nc.vector.tensor_tensor(logit, logit, mx.unsqueeze(2).to_broadcast([P, NT, E]), ALU.subtract))
            dve.wait_ge(dve_c, v)
            nc.vector.scalar_tensor_tensor(out=hot, in0=logit, scalar=0.0, in1=rank8, op0=ALU.is_ge, op1=ALU.mult).then_inc(shift_ok, 1)
            dve.wait_ge(shift_ok, 1)
            chain.link(nc.vector.tensor_reduce(best, hot, AX.X, ALU.max))
            nc.vector.tensor_tensor(hot, rank8, best.unsqueeze(2).to_broadcast([P, NT, E]), ALU.is_equal).then_inc(hot_ok, 1)
            dve.wait_ge(rexp_ok, 1)
            chain.link(nc.vector.tensor_reduce(esum, logit, AX.X, ALU.add))
            chain.link(nc.vector.reciprocal(gate, esum))
            dve.wait_ge(cum_ok, 1)
            chain.link(nc.vector.tensor_copy(tot.rearrange("p i e -> p (i e)"), ps[:, 1, 0:NT * E]))
            for e in range(E):
                ins = nc.vector.tensor_tensor_scan(run[:, :, e], ones[:, 0:NT], tot[:, :, e], 0.0, ALU.mult, ALU.add)
            chain.link(ins)
            chain.link(nc.vector.tensor_tensor(run, run, tot, ALU.subtract))
            chain.link(nc.vector.tensor_tensor(cpos, run, ps[:, 0, 0:NT * E].rearrange("p (i e) -> p i e", e=E), ALU.add))
            chain.link(nc.vector.tensor_tensor(cpos, cpos, hot, ALU.mult))
            chain.link(nc.vector.tensor_reduce(pos, cpos, AX.X, ALU.add))
            chain.link(nc.vector.tensor_scalar(keep, pos, float(CAP) - 0.5, None, ALU.is_lt))
            chain.link(nc.vector.scalar_tensor_tensor(out=pos, in0=best, scalar=-float(CAP), in1=pos, op0=ALU.mult, op1=ALU.add))
            chain.link(nc.vector.tensor_scalar(pos, pos, float(E * CAP), None, ALU.add))
            chain.link(nc.vector.tensor_tensor(slot_g, pos, keep, ALU.mult))
            chain.link(nc.vector.tensor_tensor(gate, gate, keep, ALU.mult))
            chain.link(nc.vector.tensor_scalar(keep, keep, -DROPPED, DROPPED, ALU.mult, ALU.add))
            nc.vector.tensor_tensor(slot_s, pos, keep, ALU.add).then_inc(idx_ok, 1)

            dve.wait_ge(ld_b2, 16)
            with nc.vector.Fori(0, E) as e:
                for i in range(CPT):
                    dve.wait_ge(o_ok, e * CPT + (i + 3))
                    if i >= 2:
                        dve.wait_ge(og_ok, 1 + e * CPT + (i - 1))
                    else:
                        dve.wait_ge(og_ok, 1 + e * CPT)
                    nc.vector.tensor_tensor(y_pre[:, i % 2], ps[:, 6 + i % 2, 0:C], b2_bc[:, e, :], ALU.add).then_inc(ob_ok, 1)

            for i in range(NT):
                if i % 4 == 0:
                    dve.wait_ge(gath[i // 4], 64)
                nc.vector.scalar_tensor_tensor(out=tok[:, i], in0=got[:, i], scalar=gate[:, i:i + 1], in1=tok[:, i],
                                               op0=ALU.mult, op1=ALU.add).then_inc(fin_ok, 1)


def _layouts(i):
    import numpy as np
    f = np.float32
    twice = lambda v: np.concatenate([v, v], 0)
    thirds = lambda v: twice(np.moveaxis(v.reshape((J, H2) + v.shape[1:]), 1, 0))
    order = [[o + 2 * d for d in range(2)] for o in range(2)]
    x = i["x"].reshape(B, S, C)
    d = {}
    d["xT"] = x.transpose(0, 2, 1).reshape(B, CT, P, S).transpose(0, 2, 1, 3)
    d["x_tok"] = x.reshape(NT, P, C).transpose(1, 0, 2)
    w = i["L0_conv_in_proj_w"].T.reshape(CT, P, 2, J, H2)
    d["w_in"] = np.stack([np.concatenate([w[:, :, 0], w[:, :, 1]], -1), np.concatenate([w[:, :, 1], w[:, :, 0]], -1)], 2).transpose(1, 0, 2, 3, 4)
    d["conv_w"] = thirds(i["L0_conv_conv_w"].reshape(DI, 9))
    for name, key in (("conv_b", "L0_conv_conv_b"), ("norm_g", "L0_conv_out_norm_g"), ("norm_b", "L0_conv_out_norm_b")):
        d[name] = thirds(i[key])
    xp = i["L0_conv_x_proj_w"]
    big = np.zeros((2, H2, K, J, XR), f)
    for im in range(2):
        for part in range(PART):
            for m in range(2):
                rows = xp[:, R + m * N:R + (m + 1) * N].reshape(K, N, J, H2).transpose(3, 0, 2, 1)
                at = m * BR + im * PART * N + part * N
                big[im, :, :, :, at:at + N] = rows
        at = 2 * BR + im * R
        big[im, :, :, :, at:at + R] = xp[:, 0:R].reshape(K, R, J, H2).transpose(3, 0, 2, 1)
    d["xproj_w"] = big.reshape(P, K, J, XR)
    dw = i["L0_conv_dt_projs_w"].reshape(K, J, H2, R)[order]
    big = np.zeros((2, R, 2, J, 2, 2, H2), f)
    for im in range(2):
        big[im, :, :, :, :, im, :] = dw.transpose(4, 0, 2, 1, 3)
    d["dt_w"] = big.reshape(DR, OJ, 2, P)
    d["dt_bias"] = twice(i["L0_conv_dt_projs_b"].reshape(K, J, H2)[order].transpose(3, 0, 2, 1).reshape(H2, OJ, 2, 1))
    d["a_logs"] = twice(i["L0_conv_A_logs"].reshape(K, J, H2, N)[order].transpose(3, 0, 2, 1, 4).reshape(H2, OJ, 2, N))
    d["ds"] = twice(i["L0_conv_Ds"].reshape(K, J, H2)[order].transpose(3, 1, 0, 2).reshape(H2, 2, OJ))
    d["w_out"] = thirds(i["L0_conv_out_proj_w"].T)
    wq = i["L1_attn_w_qkv"]
    rows = lambda v: v.reshape((CT, P) + v.shape[1:]).swapaxes(0, 1)
    d["w_kv"], d["w_qT"], d["w_p"] = rows(wq[:, C:]), rows(wq[:, :C].T), rows(i["L1_attn_w_proj"])
    bqkv = i["L1_attn_b_qkv"]
    d["bq"] = bqkv[:C].reshape(CT, P).T
    d["b_kv"] = np.broadcast_to(bqkv[C:].reshape(1, 2, C), (P, 2, C))
    d["b_proj"] = i["L1_attn_b_proj"].reshape(1, C)
    d["router_w"] = rows(i["L1_ffn_router_w"])
    d["w1"], d["w2"], d["b2"] = i["L1_ffn_w1"], i["L1_ffn_w2"], i["L1_ffn_b2"]
    d["b1"] = i["L1_ffn_b1"].reshape(E, MT, P).transpose(2, 0, 1)
    d["ident"], d["ones"] = np.eye(P, dtype=f), np.ones((P, P), f)
    row = np.arange(BR)
    part = (row // N) % PART
    d["mask1"], d["mask2"] = -(part >= 1).astype(f)[:, None], -(part == 2).astype(f)[:, None]
    d["mask1"], d["mask2"] = (np.concatenate([m, np.zeros((P - BR, 1), f)]) for m in (d["mask1"], d["mask2"]))
    d["sel"] = ((row[:, None, None] % N == np.arange(N)[None, :, None])
                & (row[:, None, None] // (PART * N) == np.arange(P)[None, None, :] // H2)).astype(f)
    d["sel"] = np.concatenate([d["sel"], np.zeros((P - BR, N, P), f)])
    ch = np.arange(C)
    g = (ch[:, None] // (C // GRP) == np.arange(GRP)[None]).astype(f)
    d["gn_sel"] = rows(g / f(C // GRP))
    d["gn_back"] = g.T.reshape(GRP, CT, P)
    pp = np.arange(P)
    d["mean_w"] = (pp[:, None] // H2 == pp[None] // H2).astype(f) / f(DI)
    d["head_mask"] = np.tile((pp[:, None] // HD == pp[None] // HD).astype(f) / np.sqrt(f(HD)), (1, CT))
    d["rank"] = np.broadcast_to((E - np.arange(E)).astype(f), (P, NT, E))
    d["tri"] = np.triu(np.ones((P, P), f))
    return d


def kernel(**inputs):
    import numpy as np
    import concourse.bacc as _bacc
    from concourse import mybir as _mybir
    from concourse.bass_utils import run_bass_kernel_spmd as _run

    nc = _bacc.Bacc("TRN2", target_bir_lowering=False, num_devices=1)
    arrays, aps = {}, {}
    for name, v in _layouts({k: np.asarray(v) for k, v in inputs.items()}).items():
        dt = BF16 if name == "sel" else F32
        v = np.ascontiguousarray(v).astype(_mybir.dt.np(BF16)) if name == "sel" else np.ascontiguousarray(v)
        arrays[f"in_{name}"] = v
        aps[name] = nc.dram_tensor(f"in_{name}", v.shape, dt, kind="ExternalInput").ap()
    out = nc.dram_tensor("out_0", (T, C), F32, kind="ExternalOutput").ap()
    hybrid_block_kernel(nc, aps, out)
    r = _run(nc, [arrays], core_ids=[0])
    return r.results[0]["out_0"].reshape(B, HW, HW, C)
```

```python
from contextlib import ExitStack

import concourse.bass as bass
from concourse import mybir

ALU = mybir.AluOpType
ACT = mybir.ActivationFunctionType
AX = mybir.AxisListType
F32 = mybir.dt.float32
BF16 = mybir.dt.bfloat16
U32 = mybir.dt.uint32

B, HW, C, DI, N, R, K = 4, 32, 384, 192, 16, 24, 4
S = HW * HW
T = B * S
P = 128
CT = C // P
H2 = P // 2
J = DI // H2
NP = B // 2
NQ = NP * 2 * J
OJ = 2 * J
PART = 3
DR = 2 * R
SR = 2 * N
BR = PART * SR
UN = 2 * N
HALF = S // 2
DELTA_AT = (8, 9, 11, 12)
POOL_AT = 12
DT_AT = 4
ACT_AT = (5, 6, 7, 10)
RING = 4
LAG = 3
PADW = HW + 2
TAPS, PE_TAPS = 9, 5
NT = T // P
TB = S // P
NH = 12
HD = C // NH
E, M = 8, 1536
MT = M // P
CAP = T // E
CPT = CAP // P
GRP = 32
A_LOG_MAX = 84.0
DROPPED = 100000.0


class Count:

    def __init__(self, eng, sem):
        self.eng, self.sem, self.base, self.n, self.loop, self.per = eng, sem, 0, 0, None, 0

    def enter(self, i, per):
        self.base, self.n, self.loop, self.per = self.base + self.n, 0, i, per

    def leave(self, trips):
        assert self.n == self.per, (self.n, self.per)
        self.base, self.n, self.loop = self.base + self.per * trips, 0, None

    def step(self, ins):
        ins.then_inc(self.sem, 1)
        self.n += 1
        v = self.base + self.n
        return v if self.loop is None else self.loop * self.per + v

    def link(self, ins):
        self.eng.wait_ge(self.sem, self.step(ins))


class Region:

    def __init__(self, arena, start, end):
        self.arena, self.at, self.end = arena, start, end

    def take(self, *dims, dtype=F32, rows=P):
        n = 1
        for d in dims:
            n *= d
        cols = n // 2 if dtype == BF16 else n
        assert self.at + cols <= self.end, (self.at, cols, self.end)
        v = self.arena[0:rows, self.at:self.at + cols]
        self.at += cols
        if dtype != F32:
            v = v.bitcast(dtype)
        if len(dims) > 1:
            names = [f"d{i}" for i in range(len(dims))]
            v = v.rearrange(f"p ({' '.join(names)}) -> p {' '.join(names)}", **dict(zip(names[1:], dims[1:])))
        return v


def hybrid_block_kernel(nc, a, out):
    with ExitStack() as ctx:
        def sem(name):
            return ctx.enter_context(nc.semaphore(name))

        z_dram = nc.dram_tensor("z_scratch", (NP, P, J, S), F32, kind="Internal").ap()
        slot_in = nc.dram_tensor("slot_in", (E * CAP, C), F32, kind="Internal").ap()
        slot_out = nc.dram_tensor("slot_out", (E * CAP, C), F32, kind="Internal").ap()

        COLS = 53200
        arena = ctx.enter_context(nc.sbuf_tensor("arena", [P, COLS], F32))
        ALWAYS = 3700
        XY = ALWAYS + NQ * S
        BCD = XY + 16 * S
        always = Region(arena, 0, ALWAYS)
        ident, ones = always.take(P), always.take(P)
        eps_col = always.take(1)
        a_neg = always.take(OJ, 2, N)
        dt_bias = always.take(OJ, 2, 1)
        d_sum = always.take(OJ, 1)
        d_two = always.take(2, OJ)
        conv_b, norm_g, norm_b = always.take(J), always.take(J), always.take(J)
        b1_col, bq_col = always.take(E, MT), always.take(CT)
        sel_lhs = always.take(N, P, dtype=BF16)
        dt_w = always.take(OJ, 2, P)
        xy = Region(arena, ALWAYS, XY).take(NQ, S)

        rb = Region(arena, XY, BCD)
        bc = rb.take(2 * NP, 2, 2, S, dtype=BF16)
        dts = rb.take(2 * NP, 2, S)

        ra = Region(arena, XY, BCD)
        xt = ra.take(2, CT, S)
        w_in, conv_w = ra.take(CT, 2, J, P), ra.take(J, TAPS)
        gn_sel, gn_back = ra.take(CT, GRP), ra.take(CT, P)
        bst, mv, chan = ra.take(2, CT, 2, 6), ra.take(2, CT, 2), ra.take(2, CT, 2)
        gst, gaff, caff = ra.take(2, 4), ra.take(2, 2), ra.take(2, CT, 2)
        rw = Region(arena, BCD, COLS - CPT * C)
        z_sb, xpad, conv_diag = rw.take(J, S), rw.take(J, PADW, PADW), rw.take(J, PE_TAPS, P)
        tap_sum = rw.take(2, S)
        xproj_w = rw.take(K, J, P)
        parts = rw.take(2, PART, S, dtype=BF16)
        rest = rw.take(2, S)
        zeros = Region(arena, COLS - CPT * C, COLS).take(CPT * C)

        rs = Region(arena, BCD, COLS - CPT * C)
        t_abs, t_w = rs.take(S), rs.take(S)
        dlt, dux, decay = rs.take(2, S), rs.take(2, S), rs.take(RING, S)
        hst, c_sb = rs.take(RING, S), rs.take(RING, S)
        wdt_cur = rs.take(2, P)

        tok = Region(arena, XY, BCD).take(NT, C)
        R4 = XY + NT * C
        r4 = Region(arena, R4, COLS - CPT * C)
        w_out, mean_w = r4.take(J, C), r4.take(P)
        z4, yt, ysq, yg, rst4 = r4.take(J, HALF), r4.take(J, HALF), r4.take(J, HALF), r4.take(J, HALF), r4.take(HALF)

        x2 = Region(arena, ALWAYS, XY).take(NT, C)
        r5 = Region(arena, R4 + CT * M, COLS)
        xn5, xnT = r5.take(2, C + 1), r5.take(CT, S)
        w_kv, w_qT, w_p = r5.take(CT, 2 * C), r5.take(CT, C), r5.take(CT, C)
        bkv, head_mask, rt_w = r5.take(2, C), r5.take(C), r5.take(CT, E)
        x2T = r5.take(2, CT, P)
        gram, w_row = r5.take(CT, C + 1), r5.take(C)
        x2_cur = r5.take(TB, C)
        bd, w_eff = r5.take(CT, P), r5.take(CT, C)
        m_sb, xk = gram[:, :, 0:C], w_eff
        brow, bproj = r5.take(C), r5.take(C)
        bst5, mv5, rstd5 = r5.take(TB, 6), r5.take(TB, 2), r5.take(TB, 1)
        logit, hot, cpos, tot, run, rank8 = (r5.take(NT, E) for _ in range(6))
        tri = r5.take(P)
        pos, keep = r5.take(NT), r5.take(NT)
        rg = always
        mx, esum, best = (rg.take(NT) for _ in range(3))
        gate, slot_s, slot_g = rg.take(NT), rg.take(NT, dtype=U32), rg.take(NT, dtype=U32)
        tstat, trstd, tbst, tmv = rg.take(NT, 2), rg.take(NT, 1), rg.take(4, 6), rg.take(4, 2)

        w1 = [Region(arena, R4, R4 + CT * M).take(CT, M), None]
        r6y = Region(arena, ALWAYS, XY)
        w1[1] = r6y.take(CT, M)
        w2 = [None, r6y.take(MT, C)]
        b2_bc = r6y.take(E, C)
        r6 = Region(arena, R4 + CT * M, COLS)
        w2[0] = r6.take(MT, C)
        xe, xeT, h_sb = r6.take(CPT, C), r6.take(CT, CAP), r6.take(MT, CAP)
        y_pre, yo = r6.take(2, C), r6.take(CPT, C)
        got = Region(arena, ALWAYS, XY).take(NT, C)

        ps = ctx.enter_context(nc.psum_tensor("ps", [P, 8, 512], F32))

        def pair_of_banks(b):
            return ps[:, b:b + 2, :].rearrange("p b c -> p (b c)")

        SLOT3 = [pair_of_banks(b) for b in (0, 2, 4)]
        B_PS = [pair_of_banks(0), pair_of_banks(2)]
        C_PS, Y_PS = pair_of_banks(4), pair_of_banks(6)
        TAIL_T2 = (0, 1)

        ld_c, ld_x, z_st = sem("ld_consts"), [sem("ld_x0"), sem("ld_x1")], [sem("z_stored0"), sem("z_stored1")]
        pool_set, dve_c, act_c = sem("pool_set"), sem("dve_chain"), sem("act_chain")
        a_cut, a_exp, setup = sem("a_clamped"), sem("a_exp"), sem("dve_setup")
        chan_ok, grp_ok, gaff_ok, caff_ok, xn_ok = (sem(n) for n in ("channel_stats", "group_sums", "group_affine", "channel_affine", "xn_ready"))
        ip_ok, ev_free, xh_ok, xT_ok = sem("slot_filled"), sem("slot_free"), sem("xh_padded"), sem("x_by_columns")
        xp_ok, hi_ok, mid_ok, split_ok, dts_ok = (sem(n) for n in ("xproj_filled", "split_hi", "split_mid", "split_steps", "dt_rows_copied"))
        conv_ok = sem("taps_added")
        bc_st = [sem("bc_placed0"), sem("bc_placed1")]
        wdt_ok, dt_ok, dtev_ok, lost_ok, ln_ok = (sem(n) for n in ("dt_weights", "dt_filled", "dt_evacuated", "lost_part", "ln_ready"))
        d_ok, du_ok, pd_ok = sem("delta_ready"), sem("delta_x_ready"), sem("delta_uncorrected")
        u_ok, w_ok = sem("u_ready"), sem("w_ready")
        b_ok, c_ok, c_free, dec_ok = (sem(n) for n in ("b_spread", "c_spread", "c_copied", "decay_ready"))
        p1_ok, sc_ok, p2_ok, ya_ok, yev_ok = (sem(n) for n in ("input_ready", "scanned", "readout_ready", "y_added", "y_evacuated"))
        ld4, ld_t, ld_z, yt_ok, mean_ok, yc_ok, sq_ok, var_ok, yn_ok, af_ok, yg_ok, op_ok, ta_ok = (sem(n) for n in (
            "ld_w4", "ld_tokens", "ld_z", "yt_ready", "mean_filled", "centred", "squared", "var_filled", "normed",
            "affine_done", "gated", "outproj_filled", "tokens_added"))
        ld5, xn5_ok, tp_ok, tpc_ok, gr_ok, gc_ok, xk_ok, xkc_ok, vk_ok, bd_ok, m_ok, mc_ok, we_ok, wec_ok, bro_ok = (sem(n) for n in (
            "ld_w5", "tokens_normed", "turned", "turned_copied", "gram_added", "gram_copied", "xk_filled", "xk_copied", "vk_added", "vk_masked",
            "m_filled", "m_copied", "weff_filled", "weff_copied", "bias_row"))
        at_ok, ta2_ok, x2_ok, t2_ok, t2c_ok, lg_ok, lgc_ok = (sem(n) for n in (
            "attn_filled", "attn_added", "x2_ready", "x2_turned", "x2_turned_copied", "logits_filled", "logits_copied"))
        x2s_ok = sem("x2_stored")
        passed = sem("passed")
        gvar_ok, gstd_ok, std_ok = sem("group_var"), sem("group_std"), sem("std_ready")
        tvar_ok, tstd_ok = sem("token_var"), sem("token_std")
        shift_ok, rexp_ok, hot_ok, cum_ok, idx_ok = (sem(n) for n in ("logits_shifted", "router_exp", "one_hot", "cumsum_filled", "slots_ready"))
        zero_st, scat, ld_w, ld_xe, ld_b2 = sem("zeros_stored"), sem("scattered"), [sem("ld_set0"), sem("ld_set1")], sem("ld_slots"), sem("ld_b2")
        xt_ok, xtc_ok, h_ok, hg_ok, o_ok, ob_ok, og_ok, yo_st = (sem(n) for n in (
            "slots_turned", "slots_turned_copied", "h_filled", "h_gelu", "o_filled", "o_biased", "o_gelu", "slots_stored"))
        gath, fin_ok, out_st = [sem(f"gathered{g}") for g in range(NT // 4)], sem("final_ready"), sem("out_stored")

        CONSTS = [
            (ident, "ident"), (ones, "ones"), (a_neg, "a_logs"), (dt_bias, "dt_bias"), (d_two, "ds"),
            (conv_b, "conv_b"), (norm_g, "norm_g"), (norm_b, "norm_b"),
            (b1_col, "b1"), (bq_col, "bq"), (sel_lhs, "sel"), (dt_w[0:DR], "dt_w"), (w_in, "w_in"),
            (conv_w, "conv_w"), (gn_sel, "gn_sel"), (gn_back[0:GRP], "gn_back"), (xproj_w, "xproj_w"),
        ]
        LD_C = 16 * len(CONSTS)
        PLACED = 16 * 2 * PART
        block = ctx.enter_context(nc.Block())

        def settled(eng):
            eng.sem_inc(passed, 1)

        @block.sync
        def _(sp):
            for s in (*z_st, *bc_st, yo_st):
                sp.sem_inc(s, 1)
            for r in range(2):
                sp.dma_start(xt[:, r], a["xT"][r]).then_inc(ld_x[r], 16)
            for dst, name in CONSTS:
                sp.dma_start(dst, a[name]).then_inc(ld_c, 16)
            sp.wait_ge(pool_set, 3)
            for e in range(E):
                sp.dma_start(slot_in[e * CAP:(e + 1) * CAP].rearrange("(p i) c -> p (i c)", i=CPT), zeros).then_inc(zero_st, 16)

            def store_z(p):
                for r in range(2):
                    sp.wait_ge(ev_free, 3 + p * 9 + (3 * r + 3))
                    lo = H2 * (1 - r)
                    sp.dma_start(z_dram[p, H2 * r:H2 * r + H2], z_sb[lo:lo + H2]).then_inc(z_st[r], 16)

            with nc.sync.Fori(0, NP - 1) as p:
                store_z(p)
                sp.wait_ge(ip_ok, 1 + p * 9 + 6)
                for r in range(2):
                    sp.dma_start(xt[:, r], a["xT"][p * 2 + (2 + r)]).then_inc(ld_x[r], 16)
            store_z(NP - 1)
            with nc.sync.Fori(0, NP) as p:
                for k in range(K):
                    o, dr = k % 2, k // 2
                    sp.wait_ge(split_ok, p * (2 * K) + (4 + 2 * k + 2))
                    for part in range(PART):
                        for m in range(2):
                            sp.dma_start(bc[part * SR:part * SR + SR, p * 2 + o, dr, m, :],
                                         parts[H2 + m * SR:H2 + m * SR + SR, k % 2, part]).then_inc(bc_st[k % 2], 16)
            sp.wait_ge(yev_ok, NQ)
            sp.wait_ge(du_ok, 2 * NQ)
            for r in range(2):
                sp.wait_ge(z_st[r], 1 + 16 * NP)
            sp.dma_start(w_out, a["w_out"]).then_inc(ld4, 16)
            sp.dma_start(mean_w, a["mean_w"]).then_inc(ld4, 16)
            sp.dma_start(z4, z_dram[0, :, :, 0:HALF]).then_inc(ld_z, 16)
            sp.dma_start(tok, a["x_tok"]).then_inc(ld_t, 16)
            sp.wait_ge(zero_st, 16 * E)
            for dst, name in ((w_kv, "w_kv"), (w_qT, "w_qT"), (w_p, "w_p"), (bkv, "b_kv"), (head_mask, "head_mask"),
                              (rt_w, "router_w"), (bproj[0:1], "b_proj"), (rank8, "rank"), (tri, "tri")):
                sp.dma_start(dst, a[name]).then_inc(ld5, 16)
            with nc.sync.Fori(1, 2 * NP) as c:
                sp.wait_ge(yg_ok, 1 + c * J)
                sp.dma_start(z4, z_dram[c // 2, :, :, bass.ts(c % 2, HALF)]).then_inc(ld_z, 16)
            sp.wait_ge(ta_ok, 4 + NT)
            w1_v = a["w1"].rearrange("e (t p) m -> e p t m", p=P)
            w2_v = a["w2"].rearrange("e (t p) c -> e p t c", p=P)
            sp.dma_start(w1[0], w1_v[0]).then_inc(ld_w[0], 16)
            sp.wait_ge(idx_ok, 1)
            sp.dma_start(w2[0], w2_v[0]).then_inc(ld_w[0], 16)
            sp.wait_ge(scat, 16 * NT)
            slot_in_v = slot_in.rearrange("(e i p) c -> e p i c", i=CPT, p=P)
            slot_out_v = slot_out.rearrange("(e i p) c -> e p i c", i=CPT, p=P)
            sp.dma_start(xe, slot_in_v[0]).then_inc(ld_xe, 16)
            sp.dma_start(b2_bc, a["b2"].rearrange("e c -> (e c)").partition_broadcast(P)).then_inc(ld_b2, 16)
            sp.dma_start(w1[1], w1_v[1]).then_inc(ld_w[1], 16)
            sp.dma_start(w2[1], w2_v[1]).then_inc(ld_w[1], 16)

            def slots_in(e):
                sp.wait_ge(xt_ok, e * CT)
                sp.dma_start(xe, slot_in_v[e]).then_inc(ld_xe, 16)

            def slots_out(e):
                sp.wait_ge(og_ok, 1 + e * CPT + CPT)
                sp.dma_start(slot_out_v[e], yo).then_inc(yo_st, 16)

            with nc.sync.Fori(0, E // 2 - 1) as g:
                for s in range(2):
                    slots_in(g * 2 + (s + 1))
                    slots_out(g * 2 + s)
                    sp.dma_start(w1[s], w1_v[g * 2 + (s + 2)]).then_inc(ld_w[s], 16)
                    sp.dma_start(w2[s], w2_v[g * 2 + (s + 2)]).then_inc(ld_w[s], 16)
            slots_in(E - 1)
            slots_out(E - 2)
            slots_out(E - 1)
            out_v = out.rearrange("(i p) c -> p i c", p=P)
            for g in range(NT // 4):
                sp.wait_ge(fin_ok, 4 * g + 4)
                sp.dma_start(out_v[:, 4 * g:4 * g + 4], tok[:, 4 * g:4 * g + 4]).then_inc(out_st, 16)
            sp.wait_ge(out_st, 16 * (NT // 4))

        @block.gpsimd
        def _(pool):
            pool.memset(xpad, 0.0).then_inc(pool_set, 1)
            pool.memset(eps_col, 1e-5).then_inc(pool_set, 1)
            pool.memset(zeros, 0.0).then_inc(pool_set, 1)
            pool.sem_inc(p2_ok, RING)
            pool.sem_inc(x2s_ok, 2)

            with nc.gpsimd.Fori(0, NP) as p:
                for j in range(J):
                    pool.wait_ge(ev_free, 3 + p * 9 + (6 + j + 1))
                    nc.gpsimd.tensor_copy(xy[:, p * OJ + (J + j), :].rearrange("p (w h) -> p w h", h=HW),
                                          xy[:, p * OJ + j, :].rearrange("p (h w) -> p w h", w=HW)).then_inc(xT_ok, 1)

            def delta_x(q, dr):
                pool.wait_ge(d_ok, q * 2 + (dr + 1))
                nc.gpsimd.tensor_tensor(dux[:, dr], dlt[:, dr], xy[:, q, :], ALU.mult).then_inc(du_ok, 1)

            def read_outs(q, last):
                for u in range(UN):
                    dr, n = divmod(u, N)
                    U = q * UN + u
                    pool.wait_ge(sc_ok, U + 3)
                    pool.wait_ge(c_free, U + 2)
                    nc.gpsimd.tensor_tensor(hst[:, u % RING], hst[:, u % RING], c_sb[:, u % RING], ALU.mult).then_inc(p2_ok, 1)
                    if n == POOL_AT and not (last and dr):
                        delta_x(q + dr, 1 - dr)

            pool.wait_ge(xT_ok, NP * J)
            delta_x(0, 0)
            with nc.gpsimd.Fori(0, NQ - 1) as q:
                read_outs(q, False)
            read_outs(NQ - 1, True)

            with nc.gpsimd.Fori(0, B) as b:
                for i in range(TB):
                    pool.wait_ge(x2_ok, b * TB + (i + 1))
                    nc.gpsimd.tensor_copy(x2[:, b * TB + i, :], x2_cur[:, i]).then_inc(x2s_ok, 1)

            pool.wait_ge(idx_ok, 1)
            pool.wait_ge(zero_st, 16 * E)
            pool.wait_ge(x2s_ok, 2 + NT)
            for i in range(NT):
                pool.indirect_dma_start(out=slot_in, out_offset=bass.IndirectOffsetOnAxis(ap=slot_s[:, i:i + 1], axis=0),
                                        in_=x2[:, i, :], in_offset=None, bounds_check=E * CAP - 1,
                                        oob_is_err=False).then_inc(scat, 16)
            pool.wait_ge(yo_st, 1 + 16 * E)
            pool.wait_ge(o_ok, E * CPT + 2)
            pool.wait_ge(ob_ok, 1 + E * CPT)
            for i in range(NT):
                pool.indirect_dma_start(out=got[:, i, :], out_offset=None, in_=slot_out,
                                        in_offset=bass.IndirectOffsetOnAxis(ap=slot_g[:, i:i + 1], axis=0),
                                        bounds_check=E * CAP - 1, oob_is_err=False).then_inc(gath[i // 4], 16)

        @block.scalar
        def _(act):
            chain = Count(act, act_c)
            act.sem_inc(ev_free, 3)
            act.sem_inc(dts_ok, 2)
            act.sem_inc(c_free, 1)
            act.sem_inc(tpc_ok, 2)
            for s in (t2c_ok, lgc_ok, og_ok):
                act.sem_inc(s, 1)
            act.wait_ge(ld_c, LD_C)
            act.wait_ge(a_cut, 1)
            nc.scalar.activation(a_neg, a_neg, ACT.Exp).then_inc(a_exp, 1)
            act.wait_ge(pool_set, 3)

            with nc.scalar.Fori(0, NP) as p:
                for r in range(2):
                    act.wait_ge(gvar_ok, p * 2 + (r + 1))
                    nc.scalar.activation(gaff[0:GRP, r, 0:1], gst[0:GRP, r, 3:4], ACT.Sqrt, bias=eps_col[0:GRP]).then_inc(gstd_ok, 1)
                    act.wait_ge(z_st[r], 1 + p * 16)
                    for j in range(J):
                        n = 3 * r + j
                        lo, zlo = H2 * r, H2 * (1 - r)
                        act.wait_ge(ip_ok, 1 + p * 9 + (n + 1))
                        nc.scalar.activation(xpad[lo:lo + H2, j, 1:1 + HW, 1:1 + HW],
                                             SLOT3[n % 3][lo:lo + H2].rearrange("p (h w) -> p h w", w=HW),
                                             ACT.Copy).then_inc(xh_ok, 1)
                        nc.scalar.activation(z_sb[zlo:zlo + H2, j], SLOT3[n % 3][zlo:zlo + H2], ACT.Silu).then_inc(ev_free, 1)
                for j in range(J):
                    act.wait_ge(conv_ok, p * J + (2 + j + 1))
                    settled(act)
                    nc.scalar.activation(xy[:, p * OJ + j, :], SLOT3[j], ACT.Silu, bias=conv_b[:, j:j + 1]).then_inc(ev_free, 1)

            def delta_weights(q, dr):
                nc.scalar.activation(wdt_cur[0:DR, dr], dt_w[0:DR, q % OJ, dr, :], ACT.Copy).then_inc(wdt_ok, 1)

            delta_weights(0, 0)
            with nc.scalar.Fori(0, NP) as p:
                for k in range(K):
                    o, dr = k % 2, k // 2
                    act.wait_ge(xp_ok, p * K + (k + 1))
                    act.wait_ge(bc_st[k % 2], p * (K * PLACED // 2) + (1 + k // 2 * PLACED))
                    nc.scalar.activation(parts[H2:P, k % 2, 0], SLOT3[k % 2][H2:P], ACT.Copy).then_inc(hi_ok, 1)
                    nc.scalar.activation(dts[0:DR, p * 2 + o, dr, :], SLOT3[k % 2][0:DR], ACT.Copy).then_inc(dts_ok, 1)
                    act.wait_ge(split_ok, p * (2 * K) + (4 + 2 * k + 1))
                    nc.scalar.activation(parts[H2:P, k % 2, 1], rest[H2:P, k % 2], ACT.Copy).then_inc(mid_ok, 1)

            u_made = [None]

            def delta_parts(q, dr, step):
                jq = q * 2 + dr
                bias = dt_bias[:, q % OJ, dr, :]
                if step == 0:
                    act.wait_ge(dt_ok, jq + 1)
                    if not (isinstance(jq, int) and jq == 0):
                        act.wait_ge(d_ok, jq)
                    settled(act)
                    nc.scalar.activation(dlt[:, dr], C_PS, ACT.Identity, bias=bias).then_inc(dtev_ok, 1)
                elif step == 1:
                    act.wait_ge(dtev_ok, jq + 1)
                    u_made[0] = chain.step(nc.scalar.activation(t_abs, dlt[:, dr], ACT.Abs))
                elif step == 2:
                    act.wait_ge(act_c, u_made[0])
                    nc.scalar.activation(dux[:, dr], t_abs, ACT.Exp, scale=-1.0).then_inc(u_ok, 1)
                else:
                    act.wait_ge(lost_ok, jq + 1)
                    nc.scalar.activation(t_w, t_w, ACT.Ln).then_inc(ln_ok, 1)

            def units(q, first, last):
                for u in range(UN):
                    dr, n = divmod(u, N)
                    U = q * UN + u
                    if n == 0:
                        act.wait_ge(d_ok, q * 2 + (dr + 1))
                    if not (first and u < RING):
                        act.wait_ge(sc_ok, U + (3 - RING))
                        settled(act)
                    nc.scalar.activation(decay[:, u % RING], dlt[:, dr], ACT.Exp,
                                         scale=a_neg[:, q % OJ, dr, n:n + 1]).then_inc(dec_ok, 1)
                    if n == ACT_AT[0] and not (last and dr):
                        delta_parts(q + dr, 1 - dr, 0)
                    act.wait_ge(c_ok, U + 1)
                    act.wait_ge(p2_ok, U + 1)
                    nc.scalar.activation(c_sb[:, u % RING], C_PS, ACT.Copy).then_inc(c_free, 1)
                    if not (last and dr):
                        nq, nd = q + dr, 1 - dr
                        if n == 1:
                            delta_weights(nq, nd)
                        if n in ACT_AT[1:]:
                            delta_parts(nq, nd, ACT_AT.index(n))

            for r in range(2):
                act.wait_ge(z_st[r], 1 + 16 * NP)
            for step in range(len(ACT_AT)):
                delta_parts(0, 0, step)
            act.wait_ge(split_ok, 4 + 2 * K * NP)
            for b in bc_st:
                act.wait_ge(b, 1 + K * NP // 2 * PLACED)
            act.wait_ge(setup, 2)
            units(0, True, False)
            PER = 2
            with nc.scalar.Fori(1, NQ - 1) as q:
                chain.enter(q - 1, PER)
                units(q, False, False)
            chain.leave(NQ - 2)
            units(NQ - 1, False, True)

            with nc.scalar.Fori(0, 2 * NP) as c:
                for j in range(J):
                    act.wait_ge(yc_ok, c * J + (j + 1))
                    act.wait_ge(var_ok, 1 + c)
                    nc.scalar.activation(ysq[:, j], yt[:, j], ACT.Square).then_inc(sq_ok, 1)
                act.wait_ge(var_ok, 1 + c + 1)
                nc.scalar.activation(rst4, ps[:, 1, :], ACT.Sqrt, bias=eps_col).then_inc(std_ok, 1)
                for j in range(J):
                    act.wait_ge(yn_ok, c * J + (j + 1))
                    nc.scalar.activation(yt[:, j], yt[:, j], ACT.Identity, bias=norm_b[:, j:j + 1],
                                         scale=norm_g[:, j:j + 1]).then_inc(af_ok, 1)

            act.wait_ge(tvar_ok, 1)
            nc.scalar.activation(trstd.rearrange("p i s -> p (i s)"), tstat[:, :, 1], ACT.Sqrt, bias=eps_col).then_inc(tstd_ok, 1)

            def turned(b, i):
                act.wait_ge(tp_ok, b * TB + (2 + i + 1))
                act.wait_ge(at_ok, 1 + b * TB)
                nc.scalar.activation(xnT[:, :, i * P:(i + 1) * P],
                                     ps[:, i % 2, 0:C].rearrange("p (t c) -> p t c", t=CT), ACT.Copy).then_inc(tpc_ok, 1)

            def x2_turned(b, i, bank):
                act.wait_ge(t2_ok, b * TB + (i + 2))
                act.wait_ge(lg_ok, b * TB + (i + 1))
                nc.scalar.activation(x2T[:, i % 2], ps[:, bank, 0:C].rearrange("p (t c) -> p t c", t=CT),
                                     ACT.Copy).then_inc(t2c_ok, 1)

            def logits_out(b):
                act.wait_ge(lg_ok, b * TB + (2 + TB))
                settled(act)
                nc.scalar.activation(logit[:, bass.ts(b, TB), :], ps[:, 7, C:C + TB * E].rearrange("p (i e) -> p i e", e=E),
                                     ACT.Copy).then_inc(lgc_ok, 1)

            def image(b, first):
                for s in range(TB + 1):
                    if s < TB:
                        turned(b, s)
                    if s >= 1 and not first:
                        x2_turned(b - 1, s - 1, 7)
                if not first:
                    logits_out(b - 1)
                act.wait_ge(gr_ok, b * TB + (2 + TB))
                nc.scalar.activation(gram, ps[:, 2:5, 0:C + 1], ACT.Copy).then_inc(gc_ok, 1)
                for t in range(CT):
                    act.wait_ge(m_ok, b * CT + (t + 1))
                    ins = nc.scalar.activation(m_sb[:, t], ps[:, 2 + t, 0:C], ACT.Copy)
                ins.then_inc(mc_ok, 1)
                for cb, bank in enumerate((5, 0, 1)):
                    act.wait_ge(we_ok, b * (CT + 1) + (cb + 2))
                    ins = nc.scalar.activation(w_eff[:, cb], ps[:, bank, 0:C], ACT.Copy)
                ins.then_inc(wec_ok, 1)
                for g in range(2):
                    act.wait_ge(tvar_ok, b * 2 + (g + 2))
                    nc.scalar.activation(rstd5[:, 4 * g:4 * g + 4, 0], mv5[:, 4 * g:4 * g + 4, 1], ACT.Sqrt,
                                         bias=eps_col).then_inc(tstd_ok, 1)

            image(0, True)
            with nc.scalar.Fori(1, B) as b:
                image(b, False)
            for i in range(TB):
                x2_turned(B - 1, i, TAIL_T2[i % 2])
            logits_out(B - 1)
            act.wait_ge(shift_ok, 1)
            nc.scalar.activation(logit, logit, ACT.Exp).then_inc(rexp_ok, 1)

            act.wait_ge(idx_ok, 1)
            with nc.scalar.Fori(0, E) as e:
                for t in range(CT):
                    act.wait_ge(xt_ok, e * CT + (t + 1))
                    nc.scalar.activation(xeT[:, t], ps[:, t, :], ACT.Copy).then_inc(xtc_ok, 1)
                for m in range(MT):
                    act.wait_ge(h_ok, e * MT + (m + 1))
                    if m == 0:
                        act.wait_ge(o_ok, e * CPT + 2)
                    settled(act)
                    nc.scalar.activation(h_sb[:, m], ps[:, 3 + m % 3, :], ACT.Gelu_apprx_tanh,
                                         bias=b1_col[:, e, m:m + 1]).then_inc(hg_ok, 1)
                act.wait_ge(yo_st, 1 + e * 16)
                for i in range(CPT):
                    act.wait_ge(ob_ok, 1 + e * CPT + (i + 1))
                    nc.scalar.activation(yo[:, i], y_pre[:, i % 2], ACT.Gelu_apprx_tanh).then_inc(og_ok, 1)

        @block.tensor
        def _(pe):
            pe.sem_inc(ya_ok, RING)
            for s in (tp_ok, gr_ok, lg_ok, o_ok):
                pe.sem_inc(s, 2)
            pe.sem_inc(t2_ok, 1)
            for s in (ip_ok, var_ok, at_ok, op_ok):
                pe.sem_inc(s, 1)
            pe.wait_ge(ld_c, LD_C)
            pe.wait_ge(setup, 1)

            with nc.tensor.Fori(0, NP) as p:
                for r in range(2):
                    pe.wait_ge(chan_ok, p * 2 + (r + 1))
                    for t in range(CT):
                        mm = pe.matmul(ps[0:GRP, 6, 0:2], gn_sel[:, t], chan[:, r, t], start=(t == 0), stop=(t == CT - 1))
                    mm.then_inc(grp_ok, 1)
                    pe.wait_ge(gaff_ok, p * 2 + (r + 1))
                    for t in range(CT):
                        mm = pe.matmul(ps[:, 7, 2 * t:2 * t + 2], gn_back[0:GRP, t], gaff[0:GRP, r], start=True, stop=True)
                    mm.then_inc(caff_ok, 1)
                    pe.wait_ge(xn_ok, p * 2 + (r + 1))
                    for j in range(J):
                        n = 3 * r + j
                        pe.wait_ge(ev_free, p * 9 + (n + 1))
                        for h in range(2):
                            for t in range(CT):
                                mm = pe.matmul(SLOT3[n % 3][:, h * 512:(h + 1) * 512], w_in[:, t, r, j],
                                               xt[:, r, t, h * 512:(h + 1) * 512], start=(t == 0), stop=(t == CT - 1))
                        mm.then_inc(ip_ok, 1)
                for j in range(J):
                    pe.wait_ge(ev_free, p * 9 + (7 + j))
                    pe.wait_ge(xh_ok, p * 6 + (3 + j + 1))
                    for h in range(2):
                        for tap in range(PE_TAPS):
                            dy, dx = divmod(tap, 3)
                            y0 = dy + h * (HW // 2)
                            mm = pe.matmul(SLOT3[j][:, h * 512:(h + 1) * 512].rearrange("p (h w) -> p h w", w=HW),
                                           conv_diag[:, j, tap], xpad[:, j, y0:y0 + HW // 2, dx:dx + HW],
                                           start=(tap == 0), stop=(tap == PE_TAPS - 1))
                    mm.then_inc(ip_ok, 1)

            pe.wait_ge(ev_free, 3 + 9 * NP)
            pe.wait_ge(xT_ok, J * NP)
            with nc.tensor.Fori(0, NP) as p:
                for k in range(K):
                    o = k % 2
                    pe.wait_ge(split_ok, p * (2 * K) + (2 * k + 1))
                    pe.wait_ge(dts_ok, p * K + (k + 1))
                    for h in range(2):
                        for j in range(J):
                            mm = pe.matmul(SLOT3[k % 2][:, h * 512:(h + 1) * 512], xproj_w[:, k, j],
                                           xy[:, p * OJ + (o * J + j), h * 512:(h + 1) * 512],
                                           start=(j == 0), stop=(j == J - 1))
                    mm.then_inc(xp_ok, 1)

            def spread(q, u, m, dst):
                dr, n = divmod(u, N)
                for h in range(2):
                    mm = pe.matmul(dst[:, h * 512:(h + 1) * 512], sel_lhs[0:BR, n],
                                   bc[0:BR, q // J, dr, m, h * 512:(h + 1) * 512], start=True, stop=True)
                return mm

            def delta_product(q, dr):
                pe.wait_ge(wdt_ok, q * 2 + (dr + 1))
                for h in range(2):
                    mm = pe.matmul(C_PS[:, h * 512:(h + 1) * 512], wdt_cur[0:DR, dr],
                                   dts[0:DR, q // J, dr, h * 512:(h + 1) * 512], start=True, stop=True)
                mm.then_inc(dt_ok, 1)

            def add_y(q, u):
                if u == 0 and not (isinstance(q, int) and q == 0):
                    pe.wait_ge(yev_ok, q)
                pe.wait_ge(p2_ok, q * UN + (u + 1 + RING))
                for h in range(2):
                    mm = pe.matmul(Y_PS[:, h * 512:(h + 1) * 512], ident, hst[:, u % RING, h * 512:(h + 1) * 512],
                                   start=(u == 0), stop=(u == UN - 1))
                mm.then_inc(ya_ok, 1)

            def add_trailing_y(q, u, first):
                if u >= LAG:
                    add_y(q, u - LAG)
                elif not first:
                    add_y(q - 1, UN - LAG + u)

            def tile_steps(q, first, last):
                for u in range(UN):
                    dr, n = divmod(u, N)
                    U = q * UN + u
                    pe.wait_ge(sc_ok, U + 1)
                    spread(q, u, 0, B_PS[u % 2]).then_inc(b_ok, 1)
                    after_dt = n == DT_AT + 1 and not (last and dr)
                    if after_dt:
                        add_trailing_y(q, u, first)
                        pe.wait_ge(dtev_ok, q * 2 + (dr + 2))
                    pe.wait_ge(c_free, U + 1)
                    spread(q, u, 1, C_PS).then_inc(c_ok, 1)
                    if not after_dt:
                        add_trailing_y(q, u, first)
                    if n == DT_AT and not (last and dr):
                        pe.wait_ge(c_free, U + 2)
                        delta_product(q + dr, 1 - dr)

            pe.wait_ge(dts_ok, 2 + 1)
            delta_product(0, 0)
            pe.wait_ge(split_ok, 4 + 2 * K * NP)
            pe.wait_ge(dts_ok, 2 + K * NP)
            for b in bc_st:
                pe.wait_ge(b, 1 + K * NP // 2 * PLACED)
            pe.wait_ge(dtev_ok, 1)
            tile_steps(0, True, False)
            with nc.tensor.Fori(1, NQ - 1) as q:
                tile_steps(q, False, False)
            tile_steps(NQ - 1, False, True)
            for u in range(UN - LAG, UN):
                add_y(NQ - 1, u)

            pe.wait_ge(ld4, 32)
            def mean_sums(c):
                pe.wait_ge(yt_ok, c * J + J)
                for j in range(J):
                    mm = pe.matmul(ps[:, 0, :], mean_w, yt[:, j], start=(j == 0), stop=(j == J - 1))
                mm.then_inc(mean_ok, 1)

            def square_sums(c):
                pe.wait_ge(sq_ok, c * J + J)
                for j in range(J):
                    mm = pe.matmul(ps[:, 1, :], mean_w, ysq[:, j], start=(j == 0), stop=(j == J - 1))
                mm.then_inc(var_ok, 1)

            def out_proj(c, r, tiles):
                lo = H2 * r
                pe.wait_ge(yg_ok, 1 + c * J + J)
                for i in tiles:
                    pe.wait_ge(ta_ok, c * 8 + (4 * r + i + 1))
                    for j in range(J):
                        mm = pe.matmul(ps[:, 2 + i, 0:C], yg[lo:lo + H2, j, i * P:(i + 1) * P], w_out[lo:lo + H2, j],
                                       start=(j == 0), stop=(j == J - 1))
                    mm.then_inc(op_ok, 1)

            def gated_steps(c, last):
                out_proj(c, 0, range(2))
                if not last:
                    mean_sums(c + 1)
                out_proj(c, 0, range(2, 4))
                out_proj(c, 1, range(1))
                if not last:
                    square_sums(c + 1)
                out_proj(c, 1, range(1, 4))

            mean_sums(0)
            square_sums(0)
            with nc.tensor.Fori(0, 2 * NP - 1) as c:
                gated_steps(c, False)
            gated_steps(2 * NP - 1, True)

            pe.wait_ge(ld5, 16 * 9)
            pe.wait_ge(ta_ok, 4 + NT)

            def turn(b, i):
                pe.wait_ge(xn5_ok, b * TB + (i + 1))
                pe.wait_ge(tpc_ok, b * TB + (i + 1))
                for t in range(CT):
                    mm = pe.transpose(ps[:, i % 2, t * P:(t + 1) * P], xn5[:, i % 2, t * P:(t + 1) * P], ident)
                mm.then_inc(tp_ok, 1)

            def add_gram(b, i):
                if i == 0:
                    pe.wait_ge(ta2_ok, 1 + b * TB)
                for t in range(CT):
                    mm = pe.matmul(ps[:, 2 + t, 0:C + 1], xn5[:, i % 2, t * P:(t + 1) * P], xn5[:, i % 2],
                                   start=(i == 0), stop=(i == TB - 1))
                mm.then_inc(gr_ok, 1)

            def turn_x2(b, i, bank):
                if i == 0:
                    pe.wait_ge(lgc_ok, 1 + b)
                pe.wait_ge(x2_ok, b * TB + (i + 1))
                for t in range(CT):
                    mm = pe.transpose(ps[:, bank, t * P:(t + 1) * P], x2_cur[:, i, t * P:(t + 1) * P], ident)
                mm.then_inc(t2_ok, 1)

            def logits(b, i):
                pe.wait_ge(t2c_ok, 1 + b * TB + (i + 1))
                for t in range(CT):
                    mm = pe.matmul(ps[:, 7, C + i * E:C + (i + 1) * E], x2T[:, i % 2, t], rt_w[:, t],
                                   start=(t == 0), stop=(t == CT - 1))
                mm.then_inc(lg_ok, 1)

            def router_step(b, s):
                if s >= 1:
                    logits(b, s - 1)
                if s < TB:
                    turn_x2(b, s, 7)

            def image(b, first):
                for s in range(TB + 2):
                    if s < TB:
                        turn(b, s)
                        add_gram(b, s)
                    if s >= 1 and not first:
                        router_step(b - 1, s - 1)
                pe.wait_ge(gc_ok, b + 1)
                pe.wait_ge(tpc_ok, b * TB + (2 + TB))
                for t in range(CT):
                    mm = pe.matmul(ps[0:1, 2, 0:C], gram[:, t, C:C + 1], w_kv[:, t, 0:C], start=(t == 0), stop=(t == CT - 1))
                mm.then_inc(xk_ok, 1)
                for cb, bank in enumerate((5, 0, 1)):
                    for t in range(CT):
                        mm = pe.matmul(ps[:, bank, 0:C], gram[:, t, cb * P:(cb + 1) * P], w_kv[:, t, 0:C], start=(t == 0), stop=(t == CT - 1))
                    mm.then_inc(xk_ok, 1)
                pe.wait_ge(xkc_ok, b + 1)
                pe.wait_ge(bd_ok, 1 + b)
                for t in range(CT):
                    for c in range(CT):
                        pe.matmul(ps[:, 6, t * P:(t + 1) * P], w_kv[:, c, C + t * P:C + (t + 1) * P], xk[:, c, t * P:(t + 1) * P],
                                  start=(t == 0 and c == 0), stop=False, skip_group_check=True)
                    mm = pe.matmul(ps[:, 6, t * P:(t + 1) * P], bkv[0:1, 1, t * P:(t + 1) * P], w_row[0:1, t * P:(t + 1) * P],
                                   start=False, stop=True, skip_group_check=True)
                mm.then_inc(vk_ok, 1)
                pe.wait_ge(bd_ok, 1 + b + 1)
                for t in range(CT):
                    pe.matmul(ps[:, 2 + t, 0:C], bd[:, t], w_p[:, t], start=True, stop=True).then_inc(m_ok, 1)
                pe.wait_ge(mc_ok, b + 1)
                for t in range(CT):
                    mm = pe.matmul(ps[0:1, 2, 0:C], bq_col[:, t:t + 1], m_sb[:, t], start=(t == 0), stop=(t == CT - 1))
                mm.then_inc(we_ok, 1)
                for cb, bank in enumerate((5, 0, 1)):
                    for t in range(CT):
                        mm = pe.matmul(ps[:, bank, 0:C], w_qT[:, t, cb * P:(cb + 1) * P], m_sb[:, t], start=(t == 0), stop=(t == CT - 1))
                    mm.then_inc(we_ok, 1)
                pe.wait_ge(wec_ok, b + 1)
                pe.wait_ge(bro_ok, b + 1)
                for i in range(TB):
                    if i >= 2:
                        pe.wait_ge(ta2_ok, 1 + b * TB + (i - 1))
                    for t in range(CT):
                        pe.matmul(ps[:, 3 + i % 2, 0:C], xnT[:, t, i * P:(i + 1) * P], w_eff[:, t], start=(t == 0), stop=False)
                    pe.matmul(ps[:, 3 + i % 2, 0:C], ones[0:1], brow[0:1], start=False, stop=True).then_inc(at_ok, 1)

            image(0, True)
            with nc.tensor.Fori(1, B) as b:
                image(b, False)
            for i in range(2):
                turn_x2(B - 1, i, TAIL_T2[i])
            for i in range(TB):
                logits(B - 1, i)
                if i + 2 < TB:
                    turn_x2(B - 1, i + 2, TAIL_T2[i % 2])
            pe.wait_ge(hot_ok, 1)
            pe.matmul(ps[:, 0, 0:NT * E], tri, hot.rearrange("p i e -> p (i e)"), start=True, stop=True)
            pe.matmul(ps[:, 1, 0:NT * E], ones, hot.rearrange("p i e -> p (i e)"), start=True, stop=True).then_inc(cum_ok, 1)

            pe.wait_ge(idx_ok, 1)
            with nc.tensor.Fori(0, E // 2) as g:
                for s in range(2):
                    e = g * 2 + s
                    pe.wait_ge(ld_xe, e * 16 + 16)
                    for t in range(CT):
                        for i in range(CPT):
                            mm = pe.transpose(ps[:, t, i * P:(i + 1) * P], xe[:, i, t * P:(t + 1) * P], ident)
                        mm.then_inc(xt_ok, 1)
                    pe.wait_ge(ld_w[s], g * 32 + 32)
                    pe.wait_ge(xtc_ok, e * CT + CT)
                    for m in range(MT):
                        if m >= 3:
                            pe.wait_ge(hg_ok, e * MT + (m - 2))
                        for t in range(CT):
                            mm = pe.matmul(ps[:, 3 + m % 3, :], w1[s][:, t, m * P:(m + 1) * P], xeT[:, t],
                                           start=(t == 0), stop=(t == CT - 1))
                        mm.then_inc(h_ok, 1)
                    for i in range(CPT):
                        if i == 0:
                            pe.wait_ge(hg_ok, e * MT + MT)
                        if i >= 2:
                            pe.wait_ge(ob_ok, 1 + e * CPT + (i - 1))
                        else:
                            pe.wait_ge(ob_ok, 1 + e * CPT)
                        for m in range(MT):
                            mm = pe.matmul(ps[:, 6 + i % 2, 0:C], h_sb[:, m, i * P:(i + 1) * P], w2[s][:, m],
                                           start=(m == 0), stop=(m == MT - 1))
                        mm.then_inc(o_ok, 1)

        @block.vector
        def _(dve):
            chain = Count(dve, dve_c)
            dve.sem_inc(split_ok, 4)
            dve.sem_inc(conv_ok, 2)
            dve.sem_inc(sc_ok, 2)
            dve.sem_inc(ta_ok, 4)
            for s in (yg_ok, ta2_ok, bd_ok, ob_ok):
                dve.sem_inc(s, 1)
            dve.wait_ge(ld_c, LD_C)
            nc.vector.tensor_scalar(a_neg, a_neg, A_LOG_MAX, None, ALU.min).then_inc(a_cut, 1)
            for j in range(J):
                for tap in range(PE_TAPS):
                    nc.vector.tensor_scalar(conv_diag[:, j, tap], ident, conv_w[:, j, tap:tap + 1], None, ALU.mult)
            nc.vector.tensor_tensor(d_sum.rearrange("p q one -> p (q one)"), d_two[:, 0], d_two[:, 1], ALU.add).then_inc(setup, 1)
            dve.wait_ge(a_exp, 1)
            nc.vector.tensor_scalar(a_neg, a_neg, -1.0, None, ALU.mult).then_inc(setup, 1)

            with nc.vector.Fori(0, NP) as p:
                chain.enter(p, 2 * 8 + J * (TAPS - PE_TAPS))
                for r in range(2):
                    dve.wait_ge(ld_x[r], p * 16 + 16)
                    for t in range(CT):
                        for h in range(2):
                            ins = nc.vector.bn_stats(bst[:, r, t, h], xt[:, r, t, h * 512:(h + 1) * 512])
                    chain.link(ins)
                    settled(dve)
                    for t in range(CT):
                        ins = nc.vector.bn_aggr(mv[:, r, t], bst[:, r, t].rearrange("p h s -> p (h s)"))
                    chain.link(ins)
                    chain.link(nc.vector.tensor_tensor(chan[:, r, :, 1], mv[:, r, :, 0], mv[:, r, :, 0], ALU.mult))
                    chain.link(nc.vector.tensor_tensor(chan[:, r, :, 1], chan[:, r, :, 1], mv[:, r, :, 1], ALU.add))
                    nc.vector.tensor_copy(chan[:, r, :, 0], mv[:, r, :, 0]).then_inc(chan_ok, 1)
                    dve.wait_ge(grp_ok, p * 2 + (r + 1))
                    g = gst[0:GRP, r]
                    chain.link(nc.vector.tensor_copy(g[:, 0:2], ps[0:GRP, 6, 0:2]))
                    chain.link(nc.vector.tensor_tensor(g[:, 2:3], g[:, 0:1], g[:, 0:1], ALU.mult))
                    nc.vector.tensor_tensor(g[:, 3:4], g[:, 1:2], g[:, 2:3], ALU.subtract).then_inc(gvar_ok, 1)
                    dve.wait_ge(gstd_ok, p * 2 + (r + 1))
                    chain.link(nc.vector.reciprocal(gaff[0:GRP, r, 0:1], gaff[0:GRP, r, 0:1]))
                    nc.vector.scalar_tensor_tensor(out=gaff[0:GRP, r, 1:2], in0=g[:, 0:1], scalar=-1.0,
                                                   in1=gaff[0:GRP, r, 0:1], op0=ALU.mult, op1=ALU.mult).then_inc(gaff_ok, 1)
                    dve.wait_ge(caff_ok, p * 2 + (r + 1))
                    chain.link(nc.vector.tensor_copy(caff[:, r], ps[:, 7, 0:2 * CT].rearrange("p (t s) -> p t s", s=2)))
                    for t in range(CT):
                        ins = nc.vector.tensor_scalar(xt[:, r, t], xt[:, r, t], caff[:, r, t, 0:1], caff[:, r, t, 1:2], ALU.mult, ALU.add)
                    ins.then_inc(xn_ok, 1)
                for j in range(J):
                    dve.wait_ge(xh_ok, p * 6 + (3 + j + 1))
                    dve.wait_ge(conv_ok, p * J + (j + 1))
                    acc = tap_sum[:, j % 2].rearrange("p (h w) -> p h w", w=HW)
                    for tap in range(PE_TAPS, TAPS):
                        dy, dx = divmod(tap, 3)
                        x, w = xpad[:, j, dy:dy + HW, dx:dx + HW], conv_w[:, j, tap:tap + 1]
                        if tap == PE_TAPS:
                            chain.link(nc.vector.tensor_scalar(acc, x, w, None, ALU.mult))
                        else:
                            chain.link(nc.vector.scalar_tensor_tensor(out=acc, in0=x, scalar=w, in1=acc,
                                                                      op0=ALU.mult, op1=ALU.add))
                    dve.wait_ge(ip_ok, 1 + p * 9 + (7 + j))
                    nc.vector.tensor_tensor(SLOT3[j], SLOT3[j], tap_sum[:, j % 2], ALU.add).then_inc(conv_ok, 1)
            chain.leave(NP)

            with nc.vector.Fori(0, NP) as p:
                for k in range(K):
                    dve.wait_ge(split_ok, p * (2 * K) + (2 * k + 2))
                    dve.wait_ge(hi_ok, p * K + (k + 1))
                    nc.vector.tensor_tensor(rest[H2:P, k % 2], SLOT3[k % 2][H2:P], parts[H2:P, k % 2, 0],
                                            ALU.subtract).then_inc(split_ok, 1)
                    dve.wait_ge(mid_ok, p * K + (k + 1))
                    nc.vector.tensor_tensor(parts[H2:P, k % 2, 2], rest[H2:P, k % 2], parts[H2:P, k % 2, 1],
                                            ALU.subtract).then_inc(split_ok, 1)

            def delta(q, dr, step):
                jq = q * 2 + dr
                if step == 0:
                    dve.wait_ge(u_ok, jq + 1)
                    nc.vector.tensor_scalar(t_w, dux[:, dr], 1.0, None, ALU.add).then_inc(w_ok, 1)
                elif step == 1:
                    dve.wait_ge(w_ok, jq + 1)
                    nc.vector.scalar_tensor_tensor(out=t_abs, in0=t_w, scalar=-1.0, in1=dux[:, dr],
                                                   op0=ALU.add, op1=ALU.subtract).then_inc(lost_ok, 1)
                elif step == 2:
                    dve.wait_ge(ln_ok, jq + 1)
                    nc.vector.scalar_tensor_tensor(out=dlt[:, dr], in0=dlt[:, dr], scalar=0.0, in1=t_w,
                                                   op0=ALU.max, op1=ALU.add).then_inc(pd_ok, 1)
                elif step == 3:
                    dve.wait_ge(pd_ok, jq + 1)
                    nc.vector.tensor_tensor(dlt[:, dr], dlt[:, dr], t_abs, ALU.subtract).then_inc(d_ok, 1)

            def evacuate_y(q):
                dve.wait_ge(ya_ok, q * UN + (UN + RING))
                dve.wait_ge(du_ok, q * 2 + 2)
                nc.vector.scalar_tensor_tensor(out=xy[:, q, :], in0=xy[:, q, :], scalar=d_sum[:, q % OJ, :], in1=Y_PS,
                                               op0=ALU.mult, op1=ALU.add).then_inc(yev_ok, 1)

            def scans(q, first, last):
                for u in range(UN):
                    dr, n = divmod(u, N)
                    U = q * UN + u
                    if n == 0:
                        dve.wait_ge(du_ok, q * 2 + (dr + 1))
                    if u == LAG and not first:
                        evacuate_y(q - 1)
                    dve.wait_ge(b_ok, U + 1)
                    nc.vector.tensor_tensor(B_PS[u % 2], B_PS[u % 2], dux[:, dr], ALU.mult).then_inc(p1_ok, 1)
                    dve.wait_ge(p1_ok, U + 1)
                    dve.wait_ge(dec_ok, U + 1)
                    dve.wait_ge(ya_ok, U + 1)
                    h, f, x = hst[:, u % RING], decay[:, u % RING], B_PS[u % 2]
                    if dr:
                        h, f, x = h[:, ::-1], f[:, ::-1], x[:, ::-1]
                    nc.vector.tensor_tensor_scan(h, f, x, 0.0, ALU.mult, ALU.add).then_inc(sc_ok, 1)
                    if n in DELTA_AT and not (last and dr):
                        delta(q + dr, 1 - dr, DELTA_AT.index(n))

            for step in range(len(DELTA_AT)):
                delta(0, 0, step)
            scans(0, True, False)
            with nc.vector.Fori(1, NQ - 1) as q:
                scans(q, False, False)
            scans(NQ - 1, False, True)
            evacuate_y(NQ - 1)

            dve.wait_ge(yev_ok, NQ)
            def add_orders(c):
                p, h = c // 2, c % 2
                dve.wait_ge(yg_ok, 1 + c * J)
                for j in range(J):
                    nc.vector.tensor_tensor(yt[:, j].rearrange("p (h w) -> p h w", w=HW),
                                            xy[:, p * OJ + j, :].rearrange("p (h w) -> p h w", w=HW)[:, bass.ts(h, HW // 2), :],
                                            xy[:, p * OJ + (J + j), :].rearrange("p (w h) -> p h w", h=HW)[:, bass.ts(h, HW // 2), :],
                                            ALU.add).then_inc(yt_ok, 1)

            def centre(c):
                dve.wait_ge(mean_ok, c + 1)
                for j in range(J):
                    nc.vector.tensor_tensor(yt[:, j], yt[:, j], ps[:, 0, :], ALU.subtract).then_inc(yc_ok, 1)

            def scale_down(c):
                dve.wait_ge(std_ok, c + 1)
                chain.link(nc.vector.reciprocal(rst4, rst4))
                for j in range(J):
                    nc.vector.tensor_tensor(yt[:, j], yt[:, j], rst4, ALU.mult).then_inc(yn_ok, 1)

            def gate_y(c):
                dve.wait_ge(ld_z, c * 16 + 16)
                dve.wait_ge(op_ok, 1 + c * 8)
                for j in range(J):
                    dve.wait_ge(af_ok, c * J + (j + 1))
                    nc.vector.tensor_tensor(yg[:, j], yt[:, j], z4[:, j], ALU.mult).then_inc(yg_ok, 1)

            def add_tokens(c, r, tiles):
                first = (c // 2) * (2 * TB) + (c % 2) * 4 + r * TB
                for i in tiles:
                    dve.wait_ge(op_ok, 1 + c * 8 + (4 * r + i + 1))
                    row = tok[:, first + i, :]
                    nc.vector.tensor_tensor(row, row, ps[:, 2 + i, 0:C], ALU.add).then_inc(ta_ok, 1)
                dve.wait_ge(ta_ok, c * 8 + (4 + 4 * r + max(tiles) + 1))
                settled(dve)
                for i in tiles:
                    ins = nc.vector.bn_stats(tbst[:, i], tok[:, first + i, :])
                chain.link(ins)
                settled(dve)
                for i in tiles:
                    ins = nc.vector.bn_aggr(tmv[:, i], tbst[:, i])
                chain.link(ins)
                lo, hi = min(tiles), max(tiles) + 1
                chain.link(nc.vector.tensor_copy(tstat[:, bass.ds(first + lo, hi - lo), :], tmv[:, lo:hi]))

            def gated_steps(c, last):
                if not last:
                    add_orders(c + 1)
                add_tokens(c, 0, range(2))
                if not last:
                    centre(c + 1)
                add_tokens(c, 0, range(2, 4))
                add_tokens(c, 1, range(1))
                if not last:
                    scale_down(c + 1)
                    gate_y(c + 1)
                add_tokens(c, 1, range(1, 4))

            add_orders(0)
            centre(0)
            scale_down(0)
            gate_y(0)
            dve.wait_ge(ld_t, 16)
            with nc.vector.Fori(0, 2 * NP - 1) as c:
                chain.enter(c, 13)
                gated_steps(c, False)
            chain.leave(2 * NP - 1)
            gated_steps(2 * NP - 1, True)
            dve.sem_inc(tvar_ok, 1)

            dve.wait_ge(tstd_ok, 1)
            chain.link(nc.vector.reciprocal(trstd, trstd))
            dve.wait_ge(ld5, 16 * 9)

            def attend(b, g):
                for i in range(4 * g, 4 * g + 4):
                    dve.wait_ge(at_ok, 1 + b * TB + (i + 1))
                    row = tok[:, b * TB + i, :]
                    nc.vector.tensor_tensor(row, row, ps[:, 3 + i % 2, 0:C], ALU.add).then_inc(ta2_ok, 1)

            def stats(b, g):
                dve.wait_ge(ta2_ok, 1 + b * TB + (4 * g + 4))
                settled(dve)
                for i in range(4 * g, 4 * g + 4):
                    ins = nc.vector.bn_stats(bst5[:, i], tok[:, b * TB + i, :])
                chain.link(ins)
                settled(dve)
                for i in range(4 * g, 4 * g + 4):
                    ins = nc.vector.bn_aggr(mv5[:, i], bst5[:, i])
                ins.then_inc(tvar_ok, 1)

            def normalise(b, g):
                dve.wait_ge(tstd_ok, b * 2 + (g + 2))
                chain.link(nc.vector.reciprocal(rstd5[:, 4 * g:4 * g + 4], rstd5[:, 4 * g:4 * g + 4]))
                dve.wait_ge(t2_ok, 1 + b * TB)
                dve.wait_ge(x2s_ok, 2 + b * TB)
                for i in range(4 * g, 4 * g + 4):
                    nc.vector.tensor_scalar(x2_cur[:, i], tok[:, b * TB + i, :], mv5[:, i, 0:1], rstd5[:, i],
                                            ALU.subtract, ALU.mult).then_inc(x2_ok, 1)

            chain.link(nc.vector.memset(xn5[:, :, C:C + 1], 1.0))

            def token_norm(b, i):
                dve.wait_ge(gr_ok, b * TB + (i + 1))
                nc.vector.tensor_scalar(xn5[:, i % 2, 0:C], tok[:, b * TB + i, :], tstat[:, b * TB + i, 0:1],
                                        trstd[:, b * TB + i, :], ALU.subtract, ALU.mult).then_inc(xn5_ok, 1)

            def image(b, last):
                for i in range(2, TB):
                    token_norm(b, i)
                dve.wait_ge(xk_ok, b * (CT + 1) + 1)
                nc.vector.scalar_tensor_tensor(out=w_row[0:1], in0=bkv[0:1, 0], scalar=float(S), in1=ps[0:1, 2, 0:C],
                                               op0=ALU.mult, op1=ALU.add)
                for t, bank in enumerate((5, 0, 1)):
                    dve.wait_ge(xk_ok, b * (CT + 1) + (t + 2))
                    ins = nc.vector.scalar_tensor_tensor(out=xk[:, t], in0=bkv[:, 0], scalar=gram[:, t, C:C + 1],
                                                         in1=ps[:, bank, 0:C], op0=ALU.mult, op1=ALU.add)
                ins.then_inc(xkc_ok, 1)
                dve.wait_ge(vk_ok, b + 1)
                nc.vector.tensor_tensor(bd.rearrange("p t c -> p (t c)"), ps[:, 6, 0:C], head_mask, ALU.mult).then_inc(bd_ok, 1)
                dve.wait_ge(we_ok, b * (CT + 1) + 1)
                nc.vector.tensor_tensor(brow[0:1], ps[0:1, 2, 0:C], bproj[0:1], ALU.add).then_inc(bro_ok, 1)
                attend(b, 0)
                stats(b, 0)
                if not last:
                    for i in range(2):
                        token_norm(b + 1, i)
                attend(b, 1)
                normalise(b, 0)
                stats(b, 1)
                normalise(b, 1)

            for i in range(2):
                token_norm(0, i)
            with nc.vector.Fori(0, B - 1) as b:
                chain.enter(b, 4)
                image(b, False)
            chain.leave(B - 1)
            image(B - 1, True)

            dve.wait_ge(lgc_ok, 1 + B)
            chain.link(nc.vector.tensor_reduce(mx, logit, AX.X, ALU.max))
            v = chain.step(nc.vector.tensor_tensor(logit, logit, mx.unsqueeze(2).to_broadcast([P, NT, E]), ALU.subtract))
            dve.wait_ge(dve_c, v)
            nc.vector.scalar_tensor_tensor(out=hot, in0=logit, scalar=0.0, in1=rank8, op0=ALU.is_ge, op1=ALU.mult).then_inc(shift_ok, 1)
            dve.wait_ge(shift_ok, 1)
            chain.link(nc.vector.tensor_reduce(best, hot, AX.X, ALU.max))
            nc.vector.tensor_tensor(hot, rank8, best.unsqueeze(2).to_broadcast([P, NT, E]), ALU.is_equal).then_inc(hot_ok, 1)
            dve.wait_ge(rexp_ok, 1)
            chain.link(nc.vector.tensor_reduce(esum, logit, AX.X, ALU.add))
            chain.link(nc.vector.reciprocal(gate, esum))
            dve.wait_ge(cum_ok, 1)
            chain.link(nc.vector.tensor_copy(tot.rearrange("p i e -> p (i e)"), ps[:, 1, 0:NT * E]))
            for e in range(E):
                ins = nc.vector.tensor_tensor_scan(run[:, :, e], ones[:, 0:NT], tot[:, :, e], 0.0, ALU.mult, ALU.add)
            chain.link(ins)
            chain.link(nc.vector.tensor_tensor(run, run, tot, ALU.subtract))
            chain.link(nc.vector.tensor_tensor(cpos, run, ps[:, 0, 0:NT * E].rearrange("p (i e) -> p i e", e=E), ALU.add))
            chain.link(nc.vector.tensor_tensor(cpos, cpos, hot, ALU.mult))
            chain.link(nc.vector.tensor_reduce(pos, cpos, AX.X, ALU.add))
            chain.link(nc.vector.tensor_scalar(keep, pos, float(CAP) - 0.5, None, ALU.is_lt))
            chain.link(nc.vector.scalar_tensor_tensor(out=pos, in0=best, scalar=-float(CAP), in1=pos, op0=ALU.mult, op1=ALU.add))
            chain.link(nc.vector.tensor_scalar(pos, pos, float(E * CAP), None, ALU.add))
            chain.link(nc.vector.tensor_tensor(slot_g, pos, keep, ALU.mult))
            chain.link(nc.vector.tensor_tensor(gate, gate, keep, ALU.mult))
            chain.link(nc.vector.tensor_scalar(keep, keep, -DROPPED, DROPPED, ALU.mult, ALU.add))
            nc.vector.tensor_tensor(slot_s, pos, keep, ALU.add).then_inc(idx_ok, 1)

            dve.wait_ge(ld_b2, 16)
            with nc.vector.Fori(0, E) as e:
                for i in range(CPT):
                    dve.wait_ge(o_ok, e * CPT + (i + 3))
                    if i >= 2:
                        dve.wait_ge(og_ok, 1 + e * CPT + (i - 1))
                    else:
                        dve.wait_ge(og_ok, 1 + e * CPT)
                    nc.vector.tensor_tensor(y_pre[:, i % 2], ps[:, 6 + i % 2, 0:C], b2_bc[:, e, :], ALU.add).then_inc(ob_ok, 1)

            for i in range(NT):
                if i % 4 == 0:
                    dve.wait_ge(gath[i // 4], 64)
                nc.vector.scalar_tensor_tensor(out=tok[:, i], in0=got[:, i], scalar=gate[:, i:i + 1], in1=tok[:, i],
                                               op0=ALU.mult, op1=ALU.add).then_inc(fin_ok, 1)


def _layouts(i):
    import numpy as np
    f = np.float32
    twice = lambda v: np.concatenate([v, v], 0)
    thirds = lambda v: twice(np.moveaxis(v.reshape((J, H2) + v.shape[1:]), 1, 0))
    order = [[o + 2 * d for d in range(2)] for o in range(2)]
    x = i["x"].reshape(B, S, C)
    d = {}
    d["xT"] = x.transpose(0, 2, 1).reshape(B, CT, P, S).transpose(0, 2, 1, 3)
    d["x_tok"] = x.reshape(NT, P, C).transpose(1, 0, 2)
    w = i["L0_conv_in_proj_w"].T.reshape(CT, P, 2, J, H2)
    d["w_in"] = np.stack([np.concatenate([w[:, :, 0], w[:, :, 1]], -1), np.concatenate([w[:, :, 1], w[:, :, 0]], -1)], 2).transpose(1, 0, 2, 3, 4)
    d["conv_w"] = thirds(i["L0_conv_conv_w"].reshape(DI, TAPS))
    for name, key in (("conv_b", "L0_conv_conv_b"), ("norm_g", "L0_conv_out_norm_g"), ("norm_b", "L0_conv_out_norm_b")):
        d[name] = thirds(i[key])
    xp = i["L0_conv_x_proj_w"]
    big = np.zeros((2, H2, K, J, P), f)
    for im in range(2):
        for m in range(2):
            at = H2 + m * SR + im * N
            big[im, :, :, :, at:at + N] = xp[:, R + m * N:R + (m + 1) * N].reshape(K, N, J, H2).transpose(3, 0, 2, 1)
        big[im, :, :, :, im * R:im * R + R] = xp[:, 0:R].reshape(K, R, J, H2).transpose(3, 0, 2, 1)
    d["xproj_w"] = big.reshape(P, K, J, P)
    dw = i["L0_conv_dt_projs_w"].reshape(K, J, H2, R)[order]
    big = np.zeros((2, R, 2, J, 2, 2, H2), f)
    for im in range(2):
        big[im, :, :, :, :, im, :] = dw.transpose(4, 0, 2, 1, 3)
    d["dt_w"] = big.reshape(DR, OJ, 2, P)
    d["dt_bias"] = twice(i["L0_conv_dt_projs_b"].reshape(K, J, H2)[order].transpose(3, 0, 2, 1).reshape(H2, OJ, 2, 1))
    d["a_logs"] = twice(i["L0_conv_A_logs"].reshape(K, J, H2, N)[order].transpose(3, 0, 2, 1, 4).reshape(H2, OJ, 2, N))
    d["ds"] = twice(i["L0_conv_Ds"].reshape(K, J, H2)[order].transpose(3, 1, 0, 2).reshape(H2, 2, OJ))
    d["w_out"] = thirds(i["L0_conv_out_proj_w"].T)
    wq = i["L1_attn_w_qkv"]
    rows = lambda v: v.reshape((CT, P) + v.shape[1:]).swapaxes(0, 1)
    d["w_kv"], d["w_qT"], d["w_p"] = rows(wq[:, C:]), rows(wq[:, :C].T), rows(i["L1_attn_w_proj"])
    bqkv = i["L1_attn_b_qkv"]
    d["bq"] = bqkv[:C].reshape(CT, P).T
    d["b_kv"] = np.broadcast_to(bqkv[C:].reshape(1, 2, C), (P, 2, C))
    d["b_proj"] = i["L1_attn_b_proj"].reshape(1, C)
    d["router_w"] = rows(i["L1_ffn_router_w"])
    d["w1"], d["w2"], d["b2"] = i["L1_ffn_w1"], i["L1_ffn_w2"], i["L1_ffn_b2"]
    d["b1"] = i["L1_ffn_b1"].reshape(E, MT, P).transpose(2, 0, 1)
    d["ident"], d["ones"] = np.eye(P, dtype=f), np.ones((P, P), f)
    row = np.arange(BR)
    d["sel"] = ((row[:, None, None] % N == np.arange(N)[None, :, None])
                & (row[:, None, None] // N % 2 == np.arange(P)[None, None, :] // H2)).astype(f)
    d["sel"] = np.concatenate([d["sel"], np.zeros((P - BR, N, P), f)])
    ch = np.arange(C)
    g = (ch[:, None] // (C // GRP) == np.arange(GRP)[None]).astype(f)
    d["gn_sel"] = rows(g / f(C // GRP))
    d["gn_back"] = g.T.reshape(GRP, CT, P)
    pp = np.arange(P)
    d["mean_w"] = (pp[:, None] // H2 == pp[None] // H2).astype(f) / f(DI)
    d["head_mask"] = np.tile((pp[:, None] // HD == pp[None] // HD).astype(f) / np.sqrt(f(HD)), (1, CT))
    d["rank"] = np.broadcast_to((E - np.arange(E)).astype(f), (P, NT, E))
    d["tri"] = np.triu(np.ones((P, P), f))
    return d


def kernel(**inputs):
    import numpy as np
    import concourse.bacc as _bacc
    from concourse import mybir as _mybir
    from concourse.bass_utils import run_bass_kernel_spmd as _run

    nc = _bacc.Bacc("TRN2", target_bir_lowering=False, num_devices=1)
    arrays, aps = {}, {}
    for name, v in _layouts({k: np.asarray(v) for k, v in inputs.items()}).items():
        dt = BF16 if name == "sel" else F32
        v = np.ascontiguousarray(v).astype(_mybir.dt.np(BF16)) if name == "sel" else np.ascontiguousarray(v)
        arrays[f"in_{name}"] = v
        aps[name] = nc.dram_tensor(f"in_{name}", v.shape, dt, kind="ExternalInput").ap()
    out = nc.dram_tensor("out_0", (T, C), F32, kind="ExternalOutput").ap()
    hybrid_block_kernel(nc, aps, out)
    r = _run(nc, [arrays], core_ids=[0])
    return r.results[0]["out_0"].reshape(B, HW, HW, C)
```
